# Optimizing a Trainium2 kernel written in Bass

```python
import numpy as np
import jax
import jax.numpy as jnp

def _softmax(x, axis=-1):
    return jax.nn.softmax(x, axis=axis)

def _gelu(x):
    return jax.nn.gelu(x, approximate=True)

def _silu(x):
    return jax.nn.silu(x)

def _sigmoid(x):
    return jax.nn.sigmoid(x)

def _layernorm(x, axis=-1, eps=1e-05):
    m = jnp.mean(x, axis=axis, keepdims=True)
    v = jnp.var(x, axis=axis, keepdims=True)
    return (x - m) / jnp.sqrt(v + eps)

def _scatter_add(tgt, idx, src, axis=0):
    return tgt.at[idx].add(src)

def _segment_sum(src, seg, n):
    return jax.ops.segment_sum(src, seg, n)
kernel_name = 'mk_audio_tower_d1_tok_audfeat512_r4_0e0c5d'

def setup_inputs(seed: int=0):
    np.random.seed(seed)
    _w = jnp.asarray

    def _rec_inputs():
        import jax
        import jax.numpy as jnp
        _rk = jax.random.key(seed)
        x = -0.000292821 + 1.00034 * jax.random.normal(jax.random.fold_in(_rk, 1), (128, 1024, 8), jnp.float32)
        return x
    x = _rec_inputs()

    def _L0_tok_setup():
        import jax, jax.numpy as jnp
        import numpy as np
        PATCH, STRIDE, NUM_PATCHES, LN_EPS = (16, 8, 511, 1e-05)

        def _extract_patches(x):
            B, S, C = x.shape
            idx = jnp.arange(NUM_PATCHES)[:, None] * STRIDE + jnp.arange(PATCH)[None, :]
            p = x[:, idx, :]
            p = jnp.transpose(p, (0, 1, 3, 2))
            return p.reshape(B, NUM_PATCHES, C * PATCH)

        def _patch_types(patches):
            std = jnp.std(patches, axis=2, ddof=1)
            rng = jnp.max(patches, axis=2) - jnp.min(patches, axis=2)
            types = jnp.where(std < 0.1, 0, jnp.where(std < 0.3, 1, 2))
            types = jnp.where(rng >= 0.5, 3, types)
            return types.astype(jnp.int32)
        key = jax.random.key(seed)
        ks = jax.random.split(key, 4)
        B, S, C, D = (128, 1024, 8, 128)
        x = jax.random.normal(ks[0], (B, S, C), dtype=jnp.float32)
        W = jax.random.normal(ks[1], (PATCH * C, D), dtype=jnp.float32) * (1.0 / np.sqrt(PATCH * C))
        b = jnp.zeros((D,), dtype=jnp.float32)
        ln_g = jnp.ones((D,), dtype=jnp.float32)
        ln_b = jnp.zeros((D,), dtype=jnp.float32)
        pos_emb = jax.random.normal(ks[2], (1, NUM_PATCHES, D), dtype=jnp.float32)
        type_emb = jax.random.normal(ks[3], (4, D), dtype=jnp.float32)
        return {'x': x, 'W': W, 'b': b, 'ln_g': ln_g, 'ln_b': ln_b, 'pos_emb': pos_emb, 'type_emb': type_emb}
    _L0_tok_all = _L0_tok_setup()
    _L0_tok_in = {k: v for k, v in _L0_tok_all.items() if k in ('W', 'b', 'ln_g', 'ln_b', 'pos_emb', 'type_emb')}
    del _L0_tok_all

    def _L0_attn_setup():
        import jax, jax.numpy as jnp
        import numpy as np
        B, L, F, H = (16, 1024, 128, 128)
        key = jax.random.key(seed)
        ks = jax.random.split(key, 8)
        return {'x': jax.random.normal(ks[0], (B, L, F), dtype=jnp.float32), 'B_real': jax.random.normal(ks[1], (F, H), dtype=jnp.float32), 'B_img': jax.random.normal(ks[2], (F, H), dtype=jnp.float32), 'nu': jax.random.normal(ks[3], (H,), dtype=jnp.float32), 'theta': jax.random.uniform(ks[4], (H,), dtype=jnp.float32), 'delta': jax.random.uniform(ks[5], (H,), dtype=jnp.float32), 'h0_real': jax.random.normal(ks[6], (H,), dtype=jnp.float32), 'h0_img': jax.random.normal(ks[7], (H,), dtype=jnp.float32)}
    _L0_attn_all = _L0_attn_setup()
    _L0_attn_in = {k: v for k, v in _L0_attn_all.items() if k in ('B_real', 'B_img', 'nu', 'theta', 'delta', 'h0_real', 'h0_img')}
    del _L0_attn_all

    def _L0_ffn_setup():
        import jax, jax.numpy as jnp
        import numpy as np
        E = 64
        K = 2
        D = 128
        H = 64
        NSH = 2
        ROUTE_SCALE = 2.5
        CAP = 256
        STD = 0.02
        key = jax.random.key(seed)
        ks = jax.random.split(key, 8)
        x = jax.random.normal(ks[0], (4, 512, D), dtype=jnp.float32)
        gate_w = jax.random.normal(ks[1], (E, D), dtype=jnp.float32) * STD
        w1 = jax.random.normal(ks[2], (E, D, H), dtype=jnp.float32) * STD
        w3 = jax.random.normal(ks[3], (E, D, H), dtype=jnp.float32) * STD
        w2 = jax.random.normal(ks[4], (E, H, D), dtype=jnp.float32) * STD
        sw1 = jax.random.normal(ks[5], (D, H * NSH), dtype=jnp.float32) * STD
        sw3 = jax.random.normal(ks[6], (D, H * NSH), dtype=jnp.float32) * STD
        sw2 = jax.random.normal(ks[7], (H * NSH, D), dtype=jnp.float32) * STD
        return {'x': x, 'gate_w': gate_w, 'w1': w1, 'w3': w3, 'w2': w2, 'sw1': sw1, 'sw3': sw3, 'sw2': sw2}
    _L0_ffn_all = _L0_ffn_setup()
    _L0_ffn_in = {k: v for k, v in _L0_ffn_all.items() if k in ('gate_w', 'w1', 'w3', 'w2', 'sw1', 'sw3', 'sw2')}
    del _L0_ffn_all
    return {'x': x, 'L0_tok_W': _L0_tok_in['W'], 'L0_tok_b': _L0_tok_in['b'], 'L0_tok_ln_g': _L0_tok_in['ln_g'], 'L0_tok_ln_b': _L0_tok_in['ln_b'], 'L0_tok_pos_emb': _L0_tok_in['pos_emb'], 'L0_tok_type_emb': _L0_tok_in['type_emb'], 'L0_attn_B_real': _L0_attn_in['B_real'], 'L0_attn_B_img': _L0_attn_in['B_img'], 'L0_attn_nu': _L0_attn_in['nu'], 'L0_attn_theta': _L0_attn_in['theta'], 'L0_attn_delta': _L0_attn_in['delta'], 'L0_attn_h0_real': _L0_attn_in['h0_real'], 'L0_attn_h0_img': _L0_attn_in['h0_img'], 'L0_ffn_gate_w': _L0_ffn_in['gate_w'], 'L0_ffn_w1': _L0_ffn_in['w1'], 'L0_ffn_w3': _L0_ffn_in['w3'], 'L0_ffn_w2': _L0_ffn_in['w2'], 'L0_ffn_sw1': _L0_ffn_in['sw1'], 'L0_ffn_sw3': _L0_ffn_in['sw3'], 'L0_ffn_sw2': _L0_ffn_in['sw2']}

def reference(x, L0_tok_W, L0_tok_b, L0_tok_ln_g, L0_tok_ln_b, L0_tok_pos_emb, L0_tok_type_emb, L0_attn_B_real, L0_attn_B_img, L0_attn_nu, L0_attn_theta, L0_attn_delta, L0_attn_h0_real, L0_attn_h0_img, L0_ffn_gate_w, L0_ffn_w1, L0_ffn_w3, L0_ffn_w2, L0_ffn_sw1, L0_ffn_sw3, L0_ffn_sw2):
    import jax
    import jax.numpy as jnp

    def _L0_tok_ref(x, W, b, ln_g, ln_b, pos_emb, type_emb):
        import jax, jax.numpy as jnp
        import numpy as np
        PATCH, STRIDE, NUM_PATCHES, LN_EPS = (16, 8, 511, 1e-05)

        def _extract_patches(x):
            B, S, C = x.shape
            idx = jnp.arange(NUM_PATCHES)[:, None] * STRIDE + jnp.arange(PATCH)[None, :]
            p = x[:, idx, :]
            p = jnp.transpose(p, (0, 1, 3, 2))
            return p.reshape(B, NUM_PATCHES, C * PATCH)

        def _patch_types(patches):
            std = jnp.std(patches, axis=2, ddof=1)
            rng = jnp.max(patches, axis=2) - jnp.min(patches, axis=2)
            types = jnp.where(std < 0.1, 0, jnp.where(std < 0.3, 1, 2))
            types = jnp.where(rng >= 0.5, 3, types)
            return types.astype(jnp.int32)
        patches = _extract_patches(x)
        h = jnp.einsum('bnf,fd->bnd', patches, W) + b
        mu = jnp.mean(h, axis=-1, keepdims=True)
        var = jnp.mean((h - mu) ** 2, axis=-1, keepdims=True)
        h = (h - mu) * jax.lax.rsqrt(var + LN_EPS) * ln_g + ln_b
        h = jax.nn.gelu(h, approximate=False)
        h = h + pos_emb
        types = _patch_types(patches)
        h = h + type_emb[types]
        return h

    def _L0_attn_ref(x, B_real, B_img, nu, theta, delta, h0_real, h0_img):
        import jax, jax.numpy as jnp
        import numpy as np
        B, L, F, H = (16, 1024, 128, 128)
        lam = jnp.exp(-jnp.exp(nu) + 1j * theta)
        Bx = (jnp.matmul(x, B_real) + 1j * jnp.matmul(x, B_img)) * delta
        bsz, seqlen, hid = Bx.shape
        lam_b = jnp.broadcast_to(lam, Bx.shape)

        def combine(e1, e2):
            a1, b1 = e1
            a2, b2 = e2
            return (a1 * a2, a2 * b1 + b2)
        _, h = jax.lax.associative_scan(combine, (lam_b, Bx), axis=1)
        lam_pow = jnp.cumprod(jnp.broadcast_to(lam, (seqlen, hid)), axis=0)
        h0 = h0_real + 1j * h0_img
        h0_contrib = lam_pow[None, :, :] * h0[None, None, :]
        return (h + h0_contrib).real

    def _L0_ffn_ref(x, gate_w, w1, w3, w2, sw1, sw3, sw2):
        import jax, jax.numpy as jnp
        import numpy as np
        E = 64
        K = 2
        D = 128
        H = 64
        NSH = 2
        ROUTE_SCALE = 2.5
        CAP = 256
        STD = 0.02
        bs, slen, d = x.shape
        xf = x.reshape(-1, d)
        logits = xf @ gate_w.T
        scores = jax.nn.sigmoid(logits.astype(jnp.float32))
        top_scores, top_idx = jax.lax.top_k(scores, K)
        top_scores = top_scores / (top_scores.sum(-1, keepdims=True) + 1e-20)
        top_scores = top_scores * ROUTE_SCALE
        flat_e = top_idx.reshape(-1)
        x_pairs = jnp.repeat(xf, K, axis=0)
        oh = jax.nn.one_hot(flat_e, E, dtype=jnp.int32)
        pos = jnp.take_along_axis(jnp.cumsum(oh, axis=0), flat_e[:, None], axis=1)[:, 0] - 1
        buf = jnp.zeros((E, CAP, d), dtype=xf.dtype).at[flat_e, pos].set(x_pairs, mode='drop')
        h = jax.nn.silu(jnp.einsum('ecd,edh->ech', buf, w1)) * jnp.einsum('ecd,edh->ech', buf, w3)
        y = jnp.einsum('ech,ehd->ecd', h, w2)
        valid = (pos < CAP)[:, None]
        y_pairs = jnp.where(valid, y[flat_e, jnp.minimum(pos, CAP - 1)], 0.0)
        routed = (y_pairs.reshape(-1, K, d) * top_scores[..., None].astype(xf.dtype)).sum(axis=1)
        shared = jax.nn.silu(xf @ sw1) * (xf @ sw3) @ sw2
        return (shared + routed).reshape(bs, slen, d)
    h = _L0_tok_ref(x, L0_tok_W, L0_tok_b, L0_tok_ln_g, L0_tok_ln_b, L0_tok_pos_emb, L0_tok_type_emb)
    h = h + _L0_attn_ref(_layernorm(h, axis=-1), L0_attn_B_real, L0_attn_B_img, L0_attn_nu, L0_attn_theta, L0_attn_delta, L0_attn_h0_real, L0_attn_h0_img)
    h = h + _L0_ffn_ref(_layernorm(h, axis=-1), L0_ffn_gate_w, L0_ffn_w1, L0_ffn_w3, L0_ffn_w2, L0_ffn_sw1, L0_ffn_sw3, L0_ffn_sw2)
    return h

_drawn_inputs = setup_inputs


def setup_inputs(seed=0):
    import zlib

    import numpy as np

    out = dict(_drawn_inputs(seed))
    spreads = {'L0_tok_b': (0.0, 0.1), 'L0_tok_ln_g': (1.0, 0.2), 'L0_tok_ln_b': (0.0, 0.1)}
    factors = {'L0_attn_h0_real': 8.0,
     'L0_attn_h0_img': 22.576,
     'L0_ffn_gate_w': 8.0,
     'L0_ffn_w1': 8.0,
     'L0_ffn_w3': 8.0,
     'L0_ffn_w2': 8.0,
     'L0_ffn_sw1': 8.0,
     'L0_ffn_sw3': 8.0,
     'L0_ffn_sw2': 8.0}
    for name, (base, spread) in spreads.items():
        noise = np.random.default_rng([zlib.crc32(name.encode()), seed]).standard_normal(out[name].shape)
        drawn = base * np.exp(spread * noise) if base else spread * noise
        out[name] = jnp.asarray(drawn.astype(out[name].dtype))
    for name, factor in factors.items():
        out[name] = (out[name] * factor).astype(out[name].dtype)
    return out
```

```python
from contextlib import ExitStack

import concourse.bass as bass
from concourse import mybir

F32 = mybir.dt.float32
F16 = mybir.dt.float16
BF16 = mybir.dt.bfloat16
U32 = mybir.dt.uint32
ALU = mybir.AluOpType
ACT = mybir.ActivationFunctionType
AX = mybir.AxisListType.X

B, D = 128, 128
STEPS = 511
NP = 512
C, PATCH, STRIDE = 8, 16, 8
SEG = STRIDE * C
FIRST = 128
GR, CH = 4, 16
NG = NP // GR
NC_A = FIRST // CH
NC = NP // CH
E, HID, CAP = 64, 64, 256
ROUTE_SCALE = 2.5
EPS = 1e-5
ROW = D + 4
ROWS = B * NP + CAP
FG = FIRST // GR + 1
HALF_PI = 1.5707963267948966


def wait(eng, sem, value):
    if isinstance(value, int) and value <= 0:
        return
    eng.wait_ge(sem, value)


def tower(nc, x, W, b, ln_g, ln_b, posA, pos, type_emb, Br, Bi, nu, theta, delta, h0r, h0i,
          gate_w, w13, w2, sw1, sw3, sw2, out):
    u_dram = nc.dram_tensor("u_dram", [128, FG, GR * 2 * 128], F32, kind="Internal").ap()
    h1_dram = nc.dram_tensor("h1_dram", [128, FG, GR * 128], F32, kind="Internal").ap()
    rT_dram = nc.dram_tensor("rT_dram", [NP - FIRST, 128], F32, kind="Internal").ap()
    x3_dram = nc.dram_tensor("x3_dram", [ROWS, ROW], F32, kind="Internal").ap()
    scratch = dict(u=u_dram, h1=h1_dram, rT=rT_dram, x3=x3_dram)
    with ExitStack() as ctx:
        def sb(name, shape, dt=F32):
            return ctx.enter_context(nc.sbuf_tensor(name, shape, dt))

        keep = dict(
            sems=ctx,
            ident=sb("ident", [128, 128]), ones=sb("ones", [128, 128]),
            turn=sb("turn", [128, CH, 2, 128]),
            Bj=sb("Bj", [128, CH, 2, 128]),
            colC=sb("colC", [128, CH + 1]), colS=sb("colS", [128, CH + 1]),
            decay=sb("decay", [128, 1]),
            base=sb("base", [128, 128]),
            carry=sb("carry", [128, 2, 128]),
            top=sb("top", [128, 2, NP]),
            eps=sb("eps", [128, GR]), minus=sb("minus", [128, GR]),
            halfneg=sb("halfneg", [128, NP]),
            g2=sb("g2", [128, 2 * GR, 2, 128]),
        )
        setup(nc, keep, W, Br, Bi, nu, theta, delta, h0r, h0i)
        front(nc, keep, scratch, x, W, b, ln_g, ln_b, posA, type_emb)
        with ExitStack() as inner:
            A = inner.enter_context(nc.sbuf_tensor("A", [128, CH, 2, 128], F32))
            P = inner.enter_context(nc.sbuf_tensor("P", [128, NP - FIRST, 2], F32))
            keep["A"], keep["P"] = A, P
            between(nc, keep, scratch, pos)
            scan(nc, keep, scratch, pos, gate_w, sw1, sw3, sw2, out)
        routed(nc, keep, scratch, w13, w2, out)


def setup(nc, keep, W, Br, Bi, nu, theta, delta, h0r, h0i):
    ident, ones, turn, Bj = keep["ident"], keep["ones"], keep["turn"], keep["Bj"]
    colC, colS, decay, carry = keep["colC"], keep["colS"], keep["decay"], keep["carry"]
    with ExitStack() as ctx:
        def sb(name, shape, dt=F32):
            return ctx.enter_context(nc.sbuf_tensor(name, shape, dt))

        def sem(name):
            return keep["sems"].enter_context(nc.semaphore("c_" + name))

        cols = sb("cols", [128, 8])
        tmp = sb("s_tmp", [128, 4, CH])
        Bw = sb("Bw", [128, 2, 128])
        dB = sb("dB", [128, 2, 128])
        diag_delta = sb("diag_delta", [128, 128])
        zeros = sb("zeros", [128, 128])
        t4 = sb("t4", [128, 4, GR, 128])
        ps = ctx.enter_context(nc.psum_tensor("s_ps", [128, 2, GR, 128], F32))
        psd = ctx.enter_context(nc.psum_tensor("s_psd", [128, 512], F32))
        s_in, s_id, s_act, s_dve, s_diag, s_bc, s_bcu, s_pd = (
            sem(n) for n in ("s_in", "s_id", "s_act", "s_dve", "s_diag", "s_bc", "s_bcu", "s_pd"))
        block = ctx.enter_context(nc.Block())

        @block.sync
        def _(sp):
            for i, v in enumerate((nu, theta, delta, h0r, h0i)):
                sp.dma_start(cols[:, i:i + 1], v.rearrange("(p a) -> p a", a=1)).then_inc(s_in, 16)
            sp.dma_start(Bw[:, 0, :], Br).then_inc(s_in, 16)
            sp.dma_start(Bw[:, 1, :], Bi).then_inc(s_in, 16)
            sp.wait_ge(s_in, 112)

        @block.gpsimd
        def _(pool):
            nc.gpsimd.memset(ident[:], 0.0).then_inc(s_id, 1)
            nc.gpsimd.memset(ones[:], 1.0).then_inc(s_id, 1)
            nc.gpsimd.memset(zeros[:], 0.0).then_inc(s_id, 1)
            nc.gpsimd.memset(keep["halfneg"][:], -0.5).then_inc(s_id, 1)
            nc.gpsimd.memset(keep["eps"][:], EPS)
            nc.gpsimd.memset(keep["minus"][:], -1.0)
            nc.gpsimd.memset(cols[:, 5:6], HALF_PI).then_inc(s_id, 1)
            pool.wait_ge(s_id, 5)
            nc.gpsimd.affine_select(out=ident[:], in_=ident[:], compare_op=ALU.not_equal, fill=1.0, base=0,
                                    pattern=[[-1, 128]], channel_multiplier=1).then_inc(s_id, 1)

        @block.scalar
        def _(act):
            act.wait_ge(s_in, 112)
            act.wait_ge(s_id, 5)
            nc.scalar.activation(cols[:, 6:7], cols[:, 0:1], ACT.Exp).then_inc(s_act, 1)
            act.wait_ge(s_act, 1)
            nc.scalar.activation(decay[:], cols[:, 6:7], ACT.Exp, scale=-1.0).then_inc(s_act, 1)
            nc.scalar.activation(colC[:, 1:2], cols[:, 1:2], ACT.Sin, bias=cols[:, 5:6]).then_inc(s_act, 1)
            nc.scalar.activation(colS[:, 1:2], cols[:, 1:2], ACT.Sin).then_inc(s_act, 1)

        @block.vector
        def _(dve):
            done = [0]

            def then(ins):
                done[0] += 1
                ins.then_inc(s_dve, 1)
                dve.wait_ge(s_dve, done[0])

            nc.vector.memset(colC[:, 0:1], 1.0).then_inc(s_dve, 1)
            nc.vector.memset(colS[:, 0:1], 0.0).then_inc(s_dve, 1)
            done[0] = 2
            dve.wait_ge(s_dve, 2)
            dve.wait_ge(s_act, 4)
            k = 1
            while k < CH:
                a, o = slice(1, k + 1), slice(k + 1, 2 * k + 1)
                then(nc.vector.tensor_scalar(tmp[:, 0, 0:k], colS[:, a], colS[:, k:k + 1], None, ALU.mult))
                then(nc.vector.tensor_scalar(tmp[:, 1, 0:k], colC[:, a], colS[:, k:k + 1], None, ALU.mult))
                then(nc.vector.scalar_tensor_tensor(out=colC[:, o], in0=colC[:, a], scalar=colC[:, k:k + 1],
                                                    in1=tmp[:, 0, 0:k], op0=ALU.mult, op1=ALU.subtract))
                then(nc.vector.scalar_tensor_tensor(out=colS[:, o], in0=colS[:, a], scalar=colC[:, k:k + 1],
                                                    in1=tmp[:, 1, 0:k], op0=ALU.mult, op1=ALU.add))
                k *= 2
            then(nc.vector.tensor_scalar(tmp[:, 0, 0:1], cols[:, 4:5], colS[:, 1:2], None, ALU.mult))
            then(nc.vector.tensor_scalar(tmp[:, 1, 0:1], cols[:, 3:4], colS[:, 1:2], None, ALU.mult))
            then(nc.vector.scalar_tensor_tensor(out=tmp[:, 2, 0:1], in0=cols[:, 3:4], scalar=colC[:, 1:2],
                                                in1=tmp[:, 0, 0:1], op0=ALU.mult, op1=ALU.subtract))
            then(nc.vector.scalar_tensor_tensor(out=tmp[:, 3, 0:1], in0=cols[:, 4:5], scalar=colC[:, 1:2],
                                                in1=tmp[:, 1, 0:1], op0=ALU.mult, op1=ALU.add))
            dve.wait_ge(s_id, 6)
            for c in range(2):
                then(nc.vector.tensor_scalar(carry[:, c, :], zeros[:], tmp[:, 2 + c, 0:1], None, ALU.add))
            then(nc.vector.tensor_scalar(diag_delta[:], ident[:], cols[:, 2:3], None, ALU.mult))
            for j in range(CH):
                nc.vector.tensor_scalar(turn[:, j, 0, :], ident[:], colC[:, j:j + 1], None,
                                        ALU.mult).then_inc(s_diag, 1)
                nc.vector.tensor_scalar(turn[:, j, 1, :], ident[:], colS[:, j:j + 1], -1.0,
                                        ALU.mult, ALU.mult).then_inc(s_diag, 1)
            dve.wait_ge(s_pd, 1)
            for c in range(2):
                then(nc.vector.tensor_tensor(dB[:, c, :], Bw[:, c, :], psd[:, 0:128], ALU.mult))
            for q in range(CH // GR):
                dve.wait_ge(s_bc, q + 1)
                bre = dB[:, 0, :].unsqueeze(1).to_broadcast([128, GR, 128])
                bim = dB[:, 1, :].unsqueeze(1).to_broadcast([128, GR, 128])
                for i, (p, w) in enumerate(((0, bre), (1, bim), (0, bim), (1, bre))):
                    ins = nc.vector.tensor_tensor(t4[:, i, :, :], ps[:, p, :, :], w, ALU.mult)
                    ins.then_inc(s_dve, 1)
                    done[0] += 1
                dve.wait_ge(s_dve, done[0])
                js = slice(q * GR, (q + 1) * GR)
                then(nc.vector.tensor_tensor(Bj[:, js, 0, :], t4[:, 0, :, :], t4[:, 1, :, :], ALU.subtract))
                ins = nc.vector.tensor_tensor(Bj[:, js, 1, :], t4[:, 2, :, :], t4[:, 3, :, :], ALU.add)
                then(ins)
                nc.vector.memset(tmp[:, 0, 0:1], 0.0).then_inc(s_bcu, 1)

        @block.tensor
        def _(pe):
            pe.wait_ge(s_id, 6)
            pe.wait_ge(s_diag, 1)
            nc.tensor.matmul(psd[:, 0:128], ones[:], diag_delta[:], start=True, stop=True).then_inc(s_pd, 1)
            pe.wait_ge(s_diag, 2 * CH)
            for q in range(CH // GR):
                wait(pe, s_bcu, q)
                for p in range(2):
                    ins = nc.tensor.matmul(ps[:, p, :, :], ones[:], turn[:, q * GR:(q + 1) * GR, p, :],
                                           start=True, stop=True)
                ins.then_inc(s_bc, 1)


def front(nc, keep, scratch, x, W, b, ln_g, ln_b, posA, type_emb):
    ident, Bj, halfneg, base = keep["ident"], keep["Bj"], keep["halfneg"], keep["base"]
    L_H, L_STAT, L_V, L_U, L_OUT = 0, 1, 2, 3, 4
    used = []
    LAST = FG + L_OUT
    with ExitStack() as ctx:
        def sb(name, shape, dt=F32):
            return ctx.enter_context(nc.sbuf_tensor(name, shape, dt))

        def ps(name, shape):
            return ctx.enter_context(nc.psum_tensor(name, shape, F32))

        def sem(name):
            used.append(nc.alloc_semaphore(name="f_" + name))
            return used[-1]

        XW = (GR + 1) * SEG
        xg = sb("xg", [128, 4, XW])
        rows = sb("rows", [17, 4, GR * 128])
        Wp = sb("Wp", [128, 128])
        brow = sb("brow", [1, 128])
        lng = sb("lng", [128, 128])
        lnb = sb("lnb", [128, 128])
        pT = sb("pT", [128, 2, GR, 128])
        hst = sb("hst", [128, 2, GR, 6])
        hmv = sb("hmv", [128, 2, GR, 2])
        hr = sb("hr", [128, 2, 2, GR])
        ht = sb("ht", [128, 2, 2, GR])
        z0 = sb("z0", [128, 2, GR, 128])
        z1 = sb("z1", [128, 2, GR, 128])
        z2 = sb("z2", [128, 2, GR, 128])
        er = sb("er", [128, 2, GR, 128])
        h1 = sb("h1", [128, 4, GR, 128])
        pst = sb("pst", [128, 2, GR, 6])
        pmv = sb("pmv", [128, 2, GR, 2])
        seg = sb("seg", [128, 2, 2, GR + 1])
        pmm = sb("pmm", [128, 2, 2, GR])
        tm = sb("tm", [128, 2, 5, GR])
        mask = sb("mask", [128, 2, 17])
        mT = sb("mT", [17, 2, 128])
        gst = sb("gst", [128, GR, 6])
        gmv = sb("gmv", [128, 2, GR, 2])
        gr = sb("gr", [128, 2, 2, GR])
        gt = sb("gt", [128, 2, 2, GR])
        xn = sb("xn", [128, 2, GR, 128])
        xnT = sb("xnT", [128, 2, GR, 128])
        us = sb("us", [128, 2, GR, 2, 128])
        kc = sb("kc", [128, 2, GR])
        HALF, BESSEL = range(2)
        KC = (0.5, 128.0 / 127.0)
        p_pT, p_H, p_T, p_m, p_xT = (ps(n, [128, 512]) for n in ("p_pT", "p_H", "p_T", "p_m", "p_xT"))
        p_u = ps("p_u", [128, GR, 2, 128])

        consts, pool_c = sem("consts"), sem("pool_c")
        x_in = [sem(f"x_in{i}") for i in range(4)]
        row_in = [sem(f"row_in{i}") for i in range(4)]
        h1_out = [sem(f"h1_out{i}") for i in range(4)]
        u_out = [sem(f"u_out{i}") for i in range(2)]
        (pT_ps, pT_sb, h_ps, hbn, hag, hr1, hr2, hr3, hr4, z_0, z_1, z_2, e_ok, segs, pbn, pag, pmm_ok, std_ok, range_ok, tmk, m_ok,
         m_ps, m_sb, T_ps, h1_ok, gbn, gag, gr1, gr2, gr3, gr4, xn_ok, xT_ps, xT_sb, u_ps, u_sb, base_ok) = (
            sem(n) for n in
            "pT_ps pT_sb h_ps hbn hag hr1 hr2 hr3 hr4 z_0 z_1 z_2 e_ok segs pbn pag pmm_ok std_ok range_ok tmk m_ok "
            "m_ps m_sb T_ps h1_ok gbn gag gr1 gr2 gr3 gr4 xn_ok xT_ps xT_sb u_ps u_sb base_ok".split())
        block = ctx.enter_context(nc.Block())

        def slots(eng, slot):
            for s in range(8):
                slot(s, s % 4)
            with eng.Fori(2, FIRST // CH) as c:
                for q in range(4):
                    slot(4 * c + q, q)
            for s in range(FIRST // GR, LAST):
                slot(s, s % 4)

        def live(s, lag):
            return not isinstance(s, int) or 0 <= s - lag < FG

        @block.sync
        def _(sp):
            sp.dma_start(Wp[:], W).then_inc(consts, 16)
            sp.dma_start(brow[:], b.rearrange("(a n) -> a n", a=1)).then_inc(consts, 16)
            sp.dma_start(lng[:], ln_g.partition_broadcast(128)).then_inc(consts, 16)
            sp.dma_start(lnb[:], ln_b.partition_broadcast(128)).then_inc(consts, 16)
            sp.wait_ge(pool_c, 2)
            for r in range(4):
                for i in range(GR):
                    sp.dma_start(rows[4 * i:4 * i + 4, r, i * 128:(i + 1) * 128], type_emb).then_inc(consts, 16)

            def slot(s, q):
                if live(s, L_V):
                    g = s - L_V
                    wait(sp, h1_ok, g + 1)
                    sp.dma_start(scratch["h1"][:, bass.ds(g, 1), :].rearrange("p a n -> p (a n)"),
                                 h1[:, (q - L_V) % 4, :, :].rearrange("p a n -> p (a n)")).then_inc(h1_out[(q - L_V) % 4], 16)
                if live(s, L_OUT):
                    g = s - L_OUT
                    wait(sp, u_sb, 2 * (g + 1))
                    sp.dma_start(scratch["u"][:, bass.ds(g, 1), :].rearrange("p a n -> p (a n)"),
                                 us[:, (q - L_OUT) % 2, :, :, :].rearrange("p a c n -> p (a c n)")).then_inc(u_out[(q - L_OUT) % 2], 16)
            slots(sp, slot)
            for i in range(4):
                sp.wait_ge(h1_out[i], 16 * ((FG - i + 3) // 4))
            for i in range(2):
                sp.wait_ge(u_out[i], 16 * ((FG - i + 1) // 2))

        @block.gpsimd
        def _(pool):
            nc.gpsimd.memset(rows[:], 0.0).then_inc(pool_c, 1)
            nc.gpsimd.memset(mask[:], 1.0).then_inc(pool_c, 1)
            for i, value in enumerate(KC):
                nc.gpsimd.memset(kc[:, i, :], value).then_inc(pool_c, 1)
            pool.wait_ge(pool_c, 2 + len(KC))
            pool.wait_ge(consts, 64 + 256)

            def inverse_std(mv, t, r, q2, stat, n, s1, s2, s3, s4):
                wait(pool, stat, 4 * n)
                nc.gpsimd.tensor_tensor(t[:, q2, 0, :], mv[:, q2, :, 1], keep["eps"][:], ALU.add).then_inc(s1, 1)
                nc.gpsimd.tensor_tensor(t[:, q2, 1, :], mv[:, q2, :, 0], keep["minus"][:], ALU.mult).then_inc(s2, 1)
                wait(pool, s1, n)
                nc.gpsimd.tensor_tensor(r[:, q2, 0, :], t[:, q2, 0, :], halfneg[:, 0:GR], ALU.pow).then_inc(s3, 1)
                wait(pool, s2, n)
                wait(pool, s3, n)
                nc.gpsimd.tensor_tensor(r[:, q2, 1, :], t[:, q2, 1, :], r[:, q2, 0, :], ALU.mult).then_inc(s4, 1)

            def slot(s, q):
                if live(s, L_V):
                    g, q2 = s - L_V, q % 2
                    wait(pool, xn_ok, 4 * (g - 1))
                    inverse_std(gmv, gt, gr, q2, gag, g + 1, gr1, gr2, gr3, gr4)
                if live(s, L_STAT):
                    g, q2 = s - L_STAT, (q - L_STAT) % 2
                    inverse_std(hmv, ht, hr, q2, hag, g + 1, hr1, hr2, hr3, hr4)
                    wait(pool, z_0, 4 * (g + 1))
                    wait(pool, z_2, g - 1)
                    nc.gpsimd.tensor_tensor(z1[:, q2, :, :], z0[:, q2, :, :],
                                            lng[:].unsqueeze(1).to_broadcast([128, GR, 128]), ALU.mult).then_inc(z_1, 1)
                    wait(pool, z_1, g + 1)
                    wait(pool, e_ok, g - 1)
                    nc.gpsimd.tensor_tensor(z2[:, q2, :, :], z1[:, q2, :, :],
                                            lnb[:].unsqueeze(1).to_broadcast([128, GR, 128]), ALU.add).then_inc(z_2, 1)
                if live(s, L_H):
                    q2 = q % 2
                    wait(pool, pag, 4 * (s + 1))
                    nc.gpsimd.tensor_tensor(tm[:, q2, 2, :], pmv[:, q2, :, 1], kc[:, BESSEL, :], ALU.mult).then_inc(std_ok, 1)
                    wait(pool, std_ok, 2 * s + 1)
                    wait(pool, tmk, 5 * (s - 1))
                    nc.gpsimd.tensor_tensor(tm[:, q2, 3, :], tm[:, q2, 2, :], kc[:, HALF, :], ALU.pow).then_inc(std_ok, 1)
            slots(pool, slot)

        @block.scalar
        def _(act):
            def load(s, q):
                if isinstance(s, int) and s >= FG:
                    return
                wait(act, segs, 2 * (s - 3))
                wait(act, pbn, 4 * (s - 3))
                wait(act, pT_ps, s - 3)
                act.dma_start(xg[:, q, :], x[:, bass.ds(s * (GR * SEG), XW)]).then_inc(x_in[q], 16)
                wait(act, T_ps, s - 3)
                act.dma_start(rows[16:17, q, :], posA[:, bass.ds(s * (GR * 128), GR * 128)]).then_inc(row_in[q], 16)

            act.wait_ge(pool_c, 2)
            load(0, 0)

            def slot(s, q):
                load(s + 1, (q + 1) % 4)
                if live(s, L_STAT):
                    g, q2 = s - L_STAT, (q - L_STAT) % 2
                    wait(act, hr4, g + 1)
                    wait(act, z_1, g - 1)
                    for i in range(GR):
                        nc.scalar.activation(z0[:, q2, i, :], p_H[:, i * 128:(i + 1) * 128], ACT.Identity,
                                             bias=hr[:, q2, 1, i:i + 1], scale=hr[:, q2, 0, i:i + 1]).then_inc(z_0, 1)
                if live(s, L_H):
                    wait(act, pT_ps, s + 1)
                    wait(act, h_ps, s - 1)
                    nc.scalar.activation(pT[:, q % 2, :, :], p_pT[:].rearrange("p (a n) -> p a n", a=GR),
                                         ACT.Copy).then_inc(pT_sb, 1)
                if live(s, L_STAT):
                    g, q2 = s - L_STAT, (q - L_STAT) % 2
                    wait(act, z_2, g + 1)
                    wait(act, h1_ok, g - 1)
                    nc.scalar.activation(er[:, q2, :, :], z2[:, q2, :, :], ACT.Gelu).then_inc(e_ok, 1)
                    wait(act, m_ps, g + 1)
                    wait(act, T_ps, g - 1)
                    nc.scalar.activation(mT[:, q2, :], p_m[0:17, 0:128], ACT.Copy).then_inc(m_sb, 1)
                if live(s, L_V):
                    g, q2 = s - L_V, q % 2
                    wait(act, gr4, g + 1)
                    wait(act, xT_ps, g - 1)
                    for i in range(GR):
                        nc.scalar.activation(xn[:, q2, i, :], h1[:, (q - L_V) % 4, i, :], ACT.Identity,
                                             bias=gr[:, q2, 1, i:i + 1], scale=gr[:, q2, 0, i:i + 1]).then_inc(xn_ok, 1)
                if live(s, L_OUT):
                    g, q2 = s - L_OUT, q % 2
                    wait(act, u_ps, g + 1)
                    if not isinstance(s, int) or g >= 2:
                        act.wait_ge(u_out[q2], 8 * (g - q2))
                    nc.scalar.activation(us[:, q2, 0:2, :, :], p_u[:, 0:2, :, :], ACT.Copy).then_inc(u_sb, 1)
            slots(act, slot)

        @block.vector
        def _(dve):
            dve.wait_ge(consts, 64 + 256)

            def slot(s, q):
                if live(s, L_STAT):
                    g, q2 = s - L_STAT, (q - L_STAT) % 2
                    t, mk = tm[:, q2, :, :], mask[:, q2, 0:16].rearrange("p (a k) -> p a k", k=4)
                    dve.wait_ge(range_ok, g + 1)
                    nc.vector.tensor_scalar(t[:, 1, :], t[:, 0, :], 0.5, None, ALU.is_lt).then_inc(tmk, 1)
                    dve.wait_ge(std_ok, 2 * (g + 1))
                    wait(dve, m_ps, g - 1)
                    dve.wait_ge(tmk, 5 * g + 1)
                    nc.vector.scalar_tensor_tensor(out=mk[:, :, 0], in0=t[:, 3, :], scalar=0.1, in1=t[:, 1, :],
                                                   op0=ALU.is_lt, op1=ALU.mult).then_inc(tmk, 1)
                    nc.vector.scalar_tensor_tensor(out=t[:, 4, :], in0=t[:, 3, :], scalar=0.3, in1=t[:, 1, :],
                                                   op0=ALU.is_lt, op1=ALU.mult).then_inc(tmk, 1)
                    nc.vector.tensor_scalar(mk[:, :, 3], t[:, 1, :], -1.0, 1.0, ALU.mult, ALU.add)
                    dve.wait_ge(tmk, 5 * g + 3)
                    nc.vector.tensor_tensor(mk[:, :, 1], t[:, 4, :], mk[:, :, 0], ALU.subtract).then_inc(tmk, 1)
                    nc.vector.tensor_tensor(mk[:, :, 2], t[:, 1, :], t[:, 4, :], ALU.subtract).then_inc(tmk, 1)
                if live(s, L_H):
                    q2 = q % 2
                    dve.wait_ge(x_in[q], 4 * (s - q) + 16)
                    if not isinstance(s, int) or s >= 2:
                        wait(dve, std_ok, 2 * (s - 1))
                    win = xg[:, q, :].rearrange("p (a n) -> p a n", n=SEG)
                    for i in range(GR):
                        nc.vector.bn_stats(pst[:, q2, i, :], xg[:, q, i * SEG:(i + 2) * SEG]).then_inc(pbn, 1)
                    wait(dve, pbn, 4 * (s + 1))
                    nc.vector.tensor_reduce(seg[:, q2, 0, :], win, AX, ALU.max).then_inc(segs, 1)
                    nc.vector.tensor_reduce(seg[:, q2, 1, :], win, AX, ALU.min).then_inc(segs, 1)
                    for i in range(GR):
                        nc.vector.bn_aggr(pmv[:, q2, i, :], pst[:, q2, i, :]).then_inc(pag, 1)
                    wait(dve, segs, 2 * (s + 1))
                    for i, op in enumerate((ALU.max, ALU.min)):
                        nc.vector.tensor_tensor(pmm[:, q2, i, :], seg[:, q2, i, 0:GR], seg[:, q2, i, 1:GR + 1], op).then_inc(pmm_ok, 1)
                    wait(dve, pmm_ok, 2 * (s + 1))
                    nc.vector.tensor_tensor(tm[:, q2, 0, :], pmm[:, q2, 0, :], pmm[:, q2, 1, :], ALU.subtract).then_inc(range_ok, 1)
                if live(s, L_V):
                    g, q2 = s - L_V, q % 2
                    wait(dve, e_ok, g + 1)
                    wait(dve, h1_ok, g)
                    wait(dve, T_ps, g + 1)
                    hs = h1[:, (q - L_V) % 4, :, :]
                    if not isinstance(s, int) or g >= 4:
                        dve.wait_ge(h1_out[(q - L_V) % 4], 4 * (g - (q - L_V) % 4))
                    wait(dve, xn_ok, 4 * (g - 3))
                    nc.vector.tensor_tensor(hs, er[:, q2, :, :], p_T[:].rearrange("p (a n) -> p a n", a=GR),
                                            ALU.add).then_inc(h1_ok, 1)
                    wait(dve, h1_ok, g + 1)
                    wait(dve, gr4, g - 1)
                    for i in range(GR):
                        nc.vector.bn_stats(gst[:, i, :], hs[:, i, :]).then_inc(gbn, 1)
                    wait(dve, gbn, 4 * (g + 1))
                if live(s, L_U):
                    g, q2 = s - L_U, (q - L_U) % 2
                    wait(dve, xT_ps, g + 1)
                    wait(dve, u_ps, g - 1)
                    nc.vector.tensor_copy(xnT[:, q2, :, :], p_xT[:].rearrange("p (a n) -> p a n", a=GR)).then_inc(xT_sb, 1)
                if live(s, L_V):
                    for i in range(GR):
                        nc.vector.bn_aggr(gmv[:, q % 2, i, :], gst[:, i, :]).then_inc(gag, 1)
                if live(s, L_H):
                    q2 = q % 2
                    wait(dve, h_ps, s + 1)
                    wait(dve, hr4, s - 1)
                    for i in range(GR):
                        nc.vector.bn_stats(hst[:, q2, i, :], p_H[:, i * 128:(i + 1) * 128]).then_inc(hbn, 1)
                    wait(dve, hbn, 4 * (s + 1))
                if live(s, L_OUT):
                    g, q2 = s - L_OUT, q % 2
                    wait(dve, u_ps, g + 1)
                    if not isinstance(s, int) or g >= 2:
                        dve.wait_ge(u_out[q2], 8 * (g - q2))
                    nc.vector.tensor_copy(us[:, q2, 2:4, :, :], p_u[:, 2:4, :, :]).then_inc(u_sb, 1)
                if live(s, L_H):
                    for i in range(GR):
                        nc.vector.bn_aggr(hmv[:, q % 2, i, :], hst[:, q % 2, i, :]).then_inc(hag, 1)
            slots(dve, slot)
            dve.wait_ge(h1_ok, FG)
            nc.vector.tensor_copy(base[:], h1[:, (FG - 1) % 4, 0, :]).then_inc(base_ok, 1)

        @block.tensor
        def _(pe):
            pe.wait_ge(consts, 64 + 256)

            def slot(s, q):
                if live(s, L_H):
                    pe.wait_ge(x_in[q], 4 * (s - q) + 16)
                    wait(pe, pT_sb, s)
                    for i in range(GR):
                        ins = nc.tensor.transpose(p_pT[:, i * 128:(i + 1) * 128], xg[:, q, i * SEG:(i + 2) * SEG], ident[:])
                    ins.then_inc(pT_ps, 1)
                if live(s, L_STAT):
                    g, q2 = s - L_STAT, (q - L_STAT) % 2
                    pe.wait_ge(tmk, 5 * (g + 1))
                    wait(pe, m_sb, g)
                    nc.tensor.transpose(p_m[0:17, 0:128], mask[:, q2, :], ident[:]).then_inc(m_ps, 1)
                    wait(pe, m_sb, g + 1)
                    wait(pe, h1_ok, g)
                    r = (q - L_STAT) % 4
                    pe.wait_ge(row_in[r], 4 * (g - r) + 16)
                    nc.tensor.matmul(p_T[:], mT[:, q2, :], rows[:, r, :], start=True, stop=True).then_inc(T_ps, 1)
                if live(s, L_H):
                    wait(pe, z_0, 4 * s)
                    wait(pe, hbn, 4 * s)
                    pe.wait_ge(pT_sb, s + 1)
                    for i in range(GR):
                        o = p_H[:, i * 128:(i + 1) * 128]
                        nc.tensor.matmul(o, keep["ones"][0:1, :], brow[:], start=True, stop=False)
                        ins = nc.tensor.matmul(o, pT[:, q % 2, i, :], Wp[:], start=False, stop=True)
                    ins.then_inc(h_ps, 1)
                if live(s, L_V):
                    g, q2 = s - L_V, q % 2
                    pe.wait_ge(xn_ok, 4 * (g + 1))
                    wait(pe, xT_sb, g)
                    for i in range(GR):
                        ins = nc.tensor.transpose(p_xT[:, i * 128:(i + 1) * 128], xn[:, q2, i, :], ident[:])
                    ins.then_inc(xT_ps, 1)
                if live(s, L_U):
                    g, q2 = s - L_U, (q - L_U) % 2
                    wait(pe, xT_sb, g + 1)
                    wait(pe, u_sb, 2 * g)
                    for i in range(GR):
                        j = GR * ((q - L_U) % 4) + i
                        for c in range(2):
                            ins = nc.tensor.matmul(p_u[:, i, c, :], Bj[:, j, c, :], xnT[:, q2, i, :], start=True, stop=True)
                    ins.then_inc(u_ps, 1)
            slots(pe, slot)

    nc.all_engine_barrier()
    nc.clear_and_free_semaphores(used)
    nc.all_engine_barrier()


def between(nc, keep, scratch, pos):
    ident, ones, Bj, base, A, P = (keep[k] for k in ("ident", "ones", "Bj", "base", "A", "P"))
    NB = NP - FIRST
    T = NB // 128
    with ExitStack() as ctx:
        def sb(name, shape, dt=F32):
            return ctx.enter_context(nc.sbuf_tensor(name, shape, dt))

        def ps(name, shape):
            return ctx.enter_context(nc.psum_tensor(name, shape, F32))

        def sem(name):
            return keep["sems"].enter_context(nc.semaphore("b_" + name))

        cen = sb("cen", [128, T + 1, 128])
        raw = sb("raw", [128, T + 1, 128])
        bst = sb("bst", [128, T + 1, 6])
        bmv = sb("bmv", [128, T + 1, 2])
        cT = sb("cT", [128, T + 1, 128])
        twice = sb("twice", [128, 128])
        sq = sb("sq", [128, NB])
        var = sb("var", [128, 2, NB])
        R = sb("R", [128, T, 128])
        RT = sb("RT", [128, T, 128])
        p_c, p_v = ps("p_c", [128, 512]), ps("p_v", [128, 512])
        p_A = ps("p_A", [128, 2, 8, 128])
        p_P = ps("p_P", [128, 2, 512])
        names = "pos_in raw_ok st mv cen_ok c_ps c_sb tw sq_ok v_ps var_1 var_2 R_ok R_ps RT_ok RT_out A_ps A_sb P_ps P_sb".split()
        (pos_in, raw_ok, st, mv, cen_ok, c_ps, c_sb, tw, sq_ok, v_ps, var_1, var_2, R_ok, R_ps, RT_ok, RT_out,
         A_ps, A_sb, P_ps, P_sb) = (sem(n) for n in names)
        block = ctx.enter_context(nc.Block())

        @block.sync
        def _(sp):
            sp.dma_start(raw[:, 0:T, :], pos[FIRST:NP, :].rearrange("(t p) n -> p t n", p=128)).then_inc(pos_in, 16)
            sp.wait_ge(RT_ok, 1)
            sp.dma_start(scratch["rT"].rearrange("(t p) n -> p t n", p=128), RT[:]).then_inc(RT_out, 16)
            sp.wait_ge(RT_out, 16)

        @block.gpsimd
        def _(pool):
            nc.gpsimd.tensor_copy(raw[:, T, :], base[:]).then_inc(raw_ok, 1)
            pool.wait_ge(var_2, 1)
            nc.gpsimd.tensor_tensor(R[:].rearrange("p t n -> p (t n)"), var[:, 1, :], keep["halfneg"][:, 0:NB],
                                    ALU.pow).then_inc(R_ok, 1)

        @block.scalar
        def _(act):
            act.wait_ge(c_ps, 1)
            nc.scalar.activation(cT[:], p_c[:].rearrange("p (t n) -> p t n", n=128), ACT.Copy).then_inc(c_sb, 1)
            for q in range(4):
                act.wait_ge(A_ps, q + 1)
                nc.scalar.activation(A[:, 4 * q:4 * q + 4, :, :].rearrange("p a c n -> p (a c) n"), p_A[:, q % 2, :, :],
                                     ACT.Copy).then_inc(A_sb, 1)
            act.wait_ge(R_ps, 1)
            nc.scalar.activation(RT[:], p_c[:, 0:NB].rearrange("p (t n) -> p t n", n=128), ACT.Copy).then_inc(RT_ok, 1)

        @block.vector
        def _(dve):
            dve.wait_ge(pos_in, 16)
            dve.wait_ge(raw_ok, 1)
            for t in range(T + 1):
                nc.vector.bn_stats(bst[:, t, :], raw[:, t, :]).then_inc(st, 1)
            dve.wait_ge(st, T + 1)
            for t in range(T + 1):
                nc.vector.bn_aggr(bmv[:, t, :], bst[:, t, :]).then_inc(mv, 1)
            dve.wait_ge(mv, T + 1)
            for t in range(T + 1):
                nc.vector.tensor_scalar(cen[:, t, :], raw[:, t, :], bmv[:, t, 0:1], None, ALU.subtract).then_inc(cen_ok, 1)
            dve.wait_ge(c_sb, 1)
            nc.vector.tensor_scalar(twice[:], cT[:, T, :], 2.0, None, ALU.mult).then_inc(tw, 1)
            pT = cT[:, 0:T, :].rearrange("p t n -> p (t n)")
            nc.vector.tensor_tensor(sq[:], pT, pT, ALU.mult).then_inc(sq_ok, 1)
            dve.wait_ge(v_ps, 1)
            nc.vector.tensor_scalar(var[:, 0, :], p_v[:, 0:NB], 1.0 / D, bmv[:, T, 1:2], ALU.mult, ALU.add).then_inc(var_1, 1)
            dve.wait_ge(var_1, 1)
            nc.vector.tensor_scalar(var[:, 1, :], var[:, 0, :], 0.0, EPS, ALU.max, ALU.add).then_inc(var_2, 1)
            dve.wait_ge(P_ps, 1)
            view = P[:].rearrange("p (k j) c -> p j c k", j=CH)
            for h in range(2):
                nc.vector.tensor_copy(view[:, 8 * h:8 * h + 8, :, :],
                                      p_P[:, h, 0:8 * 2 * (NB // CH)].rearrange("p (j c k) -> p j c k", j=8, c=2)).then_inc(P_sb, 1)

        @block.tensor
        def _(pe):
            pe.wait_ge(cen_ok, T + 1)
            for t in range(T + 1):
                ins = nc.tensor.transpose(p_c[:, t * 128:(t + 1) * 128], cen[:, t, :], ident[:])
            ins.then_inc(c_ps, 1)
            pe.wait_ge(c_sb, 1)
            pe.wait_ge(tw, 1)
            pT = cT[:, 0:T, :].rearrange("p t n -> p (t n)")
            nc.tensor.matmul(p_v[:, 0:NB], twice[:], pT, start=True, stop=False)
            pe.wait_ge(sq_ok, 1)
            nc.tensor.matmul(p_v[:, 0:NB], ones[:], sq[:], start=False, stop=True).then_inc(v_ps, 1)
            for q in range(4):
                wait(pe, A_sb, q - 1)
                for i in range(4):
                    for c in range(2):
                        ins = nc.tensor.matmul(p_A[:, q % 2, 2 * i + c, :], Bj[:, 4 * q + i, c, :], cT[:, T, :],
                                               start=True, stop=True)
                ins.then_inc(A_ps, 1)
            K = NB // CH
            for j in range(CH):
                for c in range(2):
                    o = ((j % 8) * 2 + c) * K
                    ins = nc.tensor.matmul(p_P[:, j // 8, o:o + K], Bj[:, j, c, :],
                                           pT.rearrange("p (k j) -> p j k", j=CH)[:, j, :], start=True, stop=True)
            ins.then_inc(P_ps, 1)
            pe.wait_ge(R_ok, 1)
            for t in range(T):
                ins = nc.tensor.transpose(p_c[:, t * 128:(t + 1) * 128], R[:, t, :], ident[:])
            ins.then_inc(R_ps, 1)


def scan(nc, keep, scratch, pos, gate_w, sw1, sw3, sw2, out):
    ident, turn, decay, base, carry, g2, top, halfneg, A, P, colC, colS = (keep[k] for k in (
        "ident", "turn", "decay", "base", "carry", "g2", "top", "halfneg", "A", "P", "colC", "colS"))
    L_Y, L_H2, L_X3, L_FF, L_HS, L_OUT, L_ST = 1, 2, 3, 4, 5, 6, 8
    with ExitStack() as ctx:
        def sb(name, shape, dt=F32):
            return ctx.enter_context(nc.sbuf_tensor(name, shape, dt))

        def ps(name, shape):
            return ctx.enter_context(nc.psum_tensor(name, shape, F32))

        def sem(name):
            return keep["sems"].enter_context(nc.semaphore("m_" + name))

        gT = sb("gT", [128, E])
        w13 = sb("w13", [128, 2, 128])
        w2s = sb("w2s", [128, 128])
        gnat = sb("gnat", [E, 128])
        ub = sb("ub", [128, 4, GR, 2, 128])
        h1 = sb("h1b", [128, 4, GR, 128])
        posb = sb("posb", [128, 4, GR, 128])
        Rb = sb("Rb", [128, 4, GR, 128])
        ap_ = sb("ap_", [128, 2, GR * 2, 128])
        tre = sb("tre", [128, 2, 128])
        h2 = sb("h2", [128, 4, GR, 128])
        st3 = sb("st3", [128, GR, 6])
        mv3 = sb("mv3", [128, 2, GR, 2])
        t3 = sb("t3", [128, 2, 2, GR])
        r3 = sb("r3", [128, 2, 2, GR])
        x3 = sb("x3", [128, 4, GR, ROW])
        xTs = sb("xTs", [128, 2, GR * 128])
        sa = sb("sa", [128, 2, GR * 128])
        hs = sb("hs", [128, 2, GR * 128])
        mx = sb("mx", [128, 4, GR, 8])
        ix = sb("ix", [128, 4, GR, 8], U32)
        ob = sb("ob", [128, 2, GR * 128])
        zr = sb("zr", [128, 2 * ROW])
        none = sb("none", [128, 2, NP - STEPS])
        p_y = ps("p_y", [128, 2, 512])
        p_xT, p_a, p_z, p_s = (ps(n, [128, 512]) for n in ("p_xT3", "p_a", "p_z", "p_s"))
        p_l = ps("p_l", [128, 2, 512])

        consts, prep, gt_ps, gt_sb, zeros_out = sem("consts"), sem("prep"), sem("gt_ps"), sem("gt_sb"), sem("zeros_out")
        u_in, h1_in, pos_in, R_in, x3_out = ([sem(f"{n}{i}") for i in range(4)] for n in ("u_in", "h1_in", "pos_in", "R_in", "x3_out"))
        o_out = [sem(f"o_out{i}") for i in range(2)]
        names = ("ap_ok ap_act u_pool h1_pool rec turned y_ps h2_ok bn ag r3a r3b r3c r3d x3_ok xT_ps xT_sb lg_ps a_ps z_ps "
                 "silu_ok hs_ok sh_ps out_ok mx_ok ix_ok aug").split()
        (ap_ok, ap_act, u_pool, h1_pool, rec, turned, y_ps, h2_ok, bn, ag, r3a, r3b, r3c, r3d, x3_ok, xT_ps, xT_sb, lg_ps, a_ps,
         z_ps, silu_ok, hs_ok, sh_ps, out_ok, mx_ok, ix_ok, aug) = (sem(n) for n in names)
        block = ctx.enter_context(nc.Block())
        GA = FIRST // GR
        ACT_STEPS = 3

        def slots(eng, slot, lag):
            for s in range(8):
                slot(s, s % 4, 0)
            with eng.Fori(2, NC_A) as c:
                for q in range(4):
                    slot(4 * c + q, q, 0)
            for s in range(GA, GA + 4):
                slot(s, s % 4, 1)
            with eng.Fori(NC_A + 1, NC - 1) as c:
                for q in range(4):
                    slot(4 * c + q, q, 1)
            for s in range(NG - 4, NG + lag):
                slot(s, s % 4, 1)

        def live(s, lag):
            return not isinstance(s, int) or 0 <= s - lag < NG

        @block.sync
        def _(sp):
            sp.dma_start(gnat[:], gate_w).then_inc(consts, 16)
            sp.dma_start(w13[:, 0, :], sw1).then_inc(consts, 16)
            sp.dma_start(w13[:, 1, :], sw3).then_inc(consts, 16)
            sp.dma_start(w2s[:], sw2).then_inc(consts, 16)
            sp.wait_ge(prep, 2)
            sp.dma_start(scratch["x3"][B * NP:ROWS, :].rearrange("(p a) n -> p (a n)", p=128), zr[:]).then_inc(zeros_out, 16)
            sp.dma_start(out[B * NP:ROWS, :].rearrange("(p a) n -> p (a n)", p=128), zr[:, 0:2 * D]).then_inc(zeros_out, 16)

            def slot(s, q, region):
                if region == 0 and live(s, 0):
                    wait(sp, rec, 4 * (s - 3))
                    sp.dma_start(ub[:, q, :, :, :].rearrange("p a c n -> p (a c n)"),
                                 scratch["u"][:, bass.ds(s, 1), :].rearrange("p a n -> p (a n)")).then_inc(u_in[q], 16)
                    wait(sp, h2_ok, s - 3)
                    sp.dma_start(h1[:, q, :, :].rearrange("p a n -> p (a n)"),
                                 scratch["h1"][:, bass.ds(s, 1), :].rearrange("p a n -> p (a n)")).then_inc(h1_in[q], 16)
                elif live(s, 0):
                    wait(sp, rec, 4 * (s - 3))
                    sp.dma_start(Rb[:, q, :, :].rearrange("p a n -> p (a n)"),
                                 scratch["rT"].rearrange("n b -> (n b)")[bass.ds((s - GA) * (GR * 128), GR * 128)]
                                 .partition_broadcast(128)).then_inc(R_in[q], 16)
                    wait(sp, h2_ok, s - 3)
                    sp.dma_start(posb[:, q, :, :].rearrange("p a n -> p (a n)"),
                                 pos.rearrange("n d -> (n d)")[bass.ds(s * (GR * 128), GR * 128)]
                                 .partition_broadcast(128)).then_inc(pos_in[q], 16)
                if live(s, L_ST):
                    g = s - L_ST
                    sp.wait_ge(aug, 3 * (g + 1))
                    sp.dma_start(scratch["x3"][0:B * NP, :].rearrange("(b n) r -> b (n r)", b=128)[:, bass.ds(g * (GR * ROW), GR * ROW)],
                                 x3[:, (q - L_ST) % 4, :, :].rearrange("p a n -> p (a n)")).then_inc(x3_out[(q - L_ST) % 4], 16)
                    sp.wait_ge(out_ok, g + 1)
                    sp.dma_start(out[0:B * NP, :].rearrange("(b n) r -> b (n r)", b=128)[:, bass.ds(g * (GR * D), GR * D)],
                                 ob[:, (q - L_ST) % 2, :]).then_inc(o_out[(q - L_ST) % 2], 16)
            slots(sp, slot, L_ST)
            sp.wait_ge(zeros_out, 32)
            for r in range(4):
                sp.wait_ge(x3_out[r], 4 * NG)
            for r in range(2):
                sp.wait_ge(o_out[r], 8 * NG)

        @block.gpsimd
        def _(pool):
            nc.gpsimd.memset(x3[:], 0.0).then_inc(prep, 1)
            nc.gpsimd.memset(zr[:], 0.0).then_inc(prep, 1)
            nc.gpsimd.memset(none[:], 99.0).then_inc(prep, 1)
            pool.wait_ge(prep, 3)

            def scan_input(s, q):
                n = s - GA
                wait(pool, u_pool, n - 1)
                k = GR - ACT_STEPS
                cols = P[:, bass.ds(n * GR + ACT_STEPS, k), :].rearrange("p a c -> p (a c)").unsqueeze(2).to_broadcast([128, 2 * k, 128])
                nc.gpsimd.tensor_tensor(ap_[:, q % 2, 2 * ACT_STEPS:, :], A[:, GR * q + ACT_STEPS:GR * (q + 1), :, :]
                                        .rearrange("p a c n -> p (a c) n"), cols, ALU.add).then_inc(ap_ok, 1)
                pool.wait_ge(R_in[q], 4 * (n - q) + 16)
                wait(pool, rec, 4 * (s - 3))
                wait(pool, ap_ok, n + 1)
                wait(pool, ap_act, 2 * ACT_STEPS * (n + 1))
                nc.gpsimd.tensor_tensor(ub[:, q, :, :, :], ap_[:, q % 2, :, :].rearrange("p (a c) n -> p a c n", c=2),
                                        Rb[:, q, :, :].unsqueeze(2).to_broadcast([128, GR, 2, 128]),
                                        ALU.mult).then_inc(u_pool, 1)
                pool.wait_ge(pos_in[q], 4 * (n - q) + 16)
                wait(pool, h2_ok, s - 3)
                nc.gpsimd.tensor_tensor(h1[:, q, :, :], posb[:, q, :, :],
                                        base[:].unsqueeze(1).to_broadcast([128, GR, 128]), ALU.add).then_inc(h1_pool, 1)

            def slot(s, q, region):
                if isinstance(s, int) and s == GA:
                    scan_input(s, q)
                if live(s, L_X3):
                    g, q2 = s - L_X3, (q - L_X3) % 2
                    pool.wait_ge(ag, 4 * (g + 1))
                    nc.gpsimd.tensor_tensor(t3[:, q2, 0, :], mv3[:, q2, :, 1], keep["eps"][:], ALU.add).then_inc(r3a, 1)
                    nc.gpsimd.tensor_tensor(t3[:, q2, 1, :], mv3[:, q2, :, 0], keep["minus"][:], ALU.mult).then_inc(r3b, 1)
                    pool.wait_ge(r3a, g + 1)
                    wait(pool, x3_ok, 4 * (g - 1))
                    nc.gpsimd.tensor_tensor(r3[:, q2, 0, :], t3[:, q2, 0, :], halfneg[:, 0:GR], ALU.pow).then_inc(r3c, 1)
                    pool.wait_ge(r3b, g + 1)
                    pool.wait_ge(r3c, g + 1)
                    nc.gpsimd.tensor_tensor(r3[:, q2, 1, :], t3[:, q2, 1, :], r3[:, q2, 0, :], ALU.mult).then_inc(r3d, 1)
                if region == 1 and live(s + 1, 0):
                    scan_input(s + 1, (q + 1) % 4)
            slots(pool, slot, L_X3)

        @block.scalar
        def _(act):
            act.wait_ge(gt_ps, 1)
            nc.scalar.activation(gT[:], p_l[:, 0, 0:E], ACT.Copy).then_inc(gt_sb, 1)
            act.wait_ge(prep, 1)

            def add_positions(s, q):
                n = s - GA
                wait(act, u_pool, n - 1)
                for i in range(ACT_STEPS):
                    for c in range(2):
                        nc.scalar.activation(ap_[:, q % 2, 2 * i + c, :], A[:, GR * q + i, c, :], ACT.Identity,
                                             bias=P[:, bass.ds(n * GR + i, 1), c]).then_inc(ap_act, 1)

            def slot(s, q, region):
                if isinstance(s, int) and s == GA:
                    add_positions(s, q)
                    add_positions(s + 1, q + 1)
                if live(s, L_OUT):
                    g, r = s - L_OUT, (q - L_OUT) % 4
                    act.wait_ge(ix_ok, 4 * (g + 1))
                    nc.scalar.activation(x3[:, r, :, D:D + 2], mx[:, r, :, 0:2], ACT.Copy).then_inc(aug, 1)
                    nc.scalar.activation(x3[:, r, :, D + 2:D + 3], ix[:, r, :, 0:1], ACT.Copy).then_inc(aug, 1)
                    nc.scalar.activation(top[:, :, bass.ds(g * GR, GR)], ix[:, r, :, 0:2].rearrange("p a k -> p k a"),
                                         ACT.Copy).then_inc(aug, 1)
                if live(s, L_X3):
                    g, q2, r = s - L_X3, (q - L_X3) % 2, (q - L_X3) % 4
                    act.wait_ge(r3d, g + 1)
                    if not isinstance(s, int) or g >= 4:
                        act.wait_ge(x3_out[r], 4 * (g - r))
                    for i in range(GR):
                        nc.scalar.activation(x3[:, r, i, 0:D], h2[:, r, i, :], ACT.Identity,
                                             bias=r3[:, q2, 1, i:i + 1], scale=r3[:, q2, 0, i:i + 1]).then_inc(x3_ok, 1)
                if region == 1 and live(s + 2, 0):
                    add_positions(s + 2, (q + 2) % 4)
                if live(s, L_FF):
                    g, q2 = s - L_FF, (q - L_FF) % 2
                    act.wait_ge(a_ps, g + 1)
                    wait(act, hs_ok, g - 1)
                    nc.scalar.activation(sa[:, q2, :], p_a[:], ACT.Silu).then_inc(silu_ok, 1)
                if live(s, L_X3):
                    g, q2 = s - L_X3, (q - L_X3) % 2
                    act.wait_ge(xT_ps, g + 1)
                    wait(act, z_ps, g - 1)
                    nc.scalar.activation(xTs[:, q2, :], p_xT[:], ACT.Copy).then_inc(xT_sb, 1)
            slots(act, slot, L_OUT)
            act.wait_ge(aug, 3 * NG)
            nc.scalar.activation(top[:, :, STEPS:NP], none[:], ACT.Copy)

        @block.vector
        def _(dve):

            def slot(s, q, region):
                if live(s, L_OUT):
                    g, r, o = s - L_OUT, (q - L_OUT) % 4, (q - L_OUT) % 2
                    dve.wait_ge(sh_ps, g + 1)
                    if not isinstance(s, int) or g >= 2:
                        dve.wait_ge(o_out[o], 8 * (g - o))
                    nc.vector.tensor_tensor(ob[:, o, :], h2[:, r, :, :].rearrange("p a n -> p (a n)"), p_s[:], ALU.add).then_inc(out_ok, 1)
                if live(s, L_HS):
                    g, q2 = s - L_HS, (q - L_HS) % 2
                    dve.wait_ge(silu_ok, g + 1)
                    dve.wait_ge(z_ps, g + 1)
                    dve.wait_ge(lg_ps, g + 1)
                    wait(dve, aug, 3 * (g - 3))
                    wait(dve, sh_ps, g - 1)
                    nc.vector.tensor_tensor(hs[:, q2, :], sa[:, q2, :], p_z[:], ALU.mult).then_inc(hs_ok, 1)
                if live(s, L_H2):
                    g, q2, r = s - L_H2, (q - L_H2) % 2, (q - L_H2) % 4
                    dve.wait_ge(y_ps, g + 1)
                    wait(dve, out_ok, g - 3)
                    if region == 0 or isinstance(s, int) and g < GA:
                        dve.wait_ge(h1_in[r], 4 * (g - r) + 16)
                    else:
                        dve.wait_ge(h1_pool, g + 1 - GA)
                    nc.vector.tensor_tensor(h2[:, r, :, :], p_y[:, q2, :].rearrange("p (a n) -> p a n", a=GR),
                                            h1[:, r, :, :], ALU.add).then_inc(h2_ok, 1)
                if live(s, 0) and q == 0 and not (isinstance(s, int) and s == 0):
                    dve.wait_ge(rec, 4 * s)
                    k = s - 4
                    last = g2[:, 2 * GR - 1, :, :]
                    nc.vector.tensor_scalar(tre[:, 0, :], last[:, 1, :], colS[:, CH:CH + 1], None, ALU.mult).then_inc(turned, 1)
                    nc.vector.tensor_scalar(tre[:, 1, :], last[:, 0, :], colS[:, CH:CH + 1], None, ALU.mult).then_inc(turned, 1)
                    dve.wait_ge(turned, k + 1)
                    nc.vector.scalar_tensor_tensor(out=carry[:, 0, :], in0=last[:, 0, :], scalar=colC[:, CH:CH + 1],
                                                   in1=tre[:, 0, :], op0=ALU.mult, op1=ALU.subtract).then_inc(turned, 1)
                    dve.wait_ge(turned, k + 2)
                    nc.vector.scalar_tensor_tensor(out=carry[:, 1, :], in0=last[:, 1, :], scalar=colC[:, CH:CH + 1],
                                                   in1=tre[:, 1, :], op0=ALU.mult, op1=ALU.add).then_inc(turned, 1)
                g5, half, r5 = s - L_HS, (q - L_HS) % 2, (q - L_HS) % 4
                g2_, q2, r2 = s - L_H2, (q - L_H2) % 2, (q - L_H2) % 4
                for i in range(GR):
                    lg = p_l[:, half, i * E:(i + 1) * E]
                    if live(s, L_HS):
                        nc.vector.max(mx[:, r5, i, :], lg).then_inc(mx_ok, 1)
                    if live(s, L_H2):
                        if i == 0:
                            dve.wait_ge(h2_ok, g2_ + 1)
                            wait(dve, r3d, g2_ - 1)
                        else:
                            wait(dve, bn, 4 * g2_ + i)
                    if live(s, L_HS):
                        dve.wait_ge(mx_ok, 4 * g5 + i + 1)
                    if live(s, L_H2):
                        nc.vector.bn_stats(st3[:, i, :], h2[:, r2, i, :]).then_inc(bn, 1)
                        if i:
                            nc.vector.bn_aggr(mv3[:, q2, i - 1, :], st3[:, i - 1, :]).then_inc(ag, 1)
                    if live(s, L_HS):
                        nc.vector.max_index(ix[:, r5, i, :], mx[:, r5, i, :], lg).then_inc(ix_ok, 1)
                    if i == GR - 1 and live(s, L_H2):
                        dve.wait_ge(bn, 4 * g2_ + GR)
                    if live(s, 0):
                        if i == 0:
                            if region == 0:
                                dve.wait_ge(u_in[q], 4 * (s - q) + 16)
                            else:
                                dve.wait_ge(u_pool, s + 1 - GA)
                            wait(dve, y_ps, s - 1)
                        wait(dve, rec, 4 * s + i)
                        if q == 0 and i == 0 and not (isinstance(s, int) and s == 0):
                            dve.wait_ge(turned, s)
                        k = (q % 2) * GR + i
                        prev = carry[:] if q == 0 and i == 0 else g2[:, (k - 1) % (2 * GR), :, :]
                        nc.vector.scalar_tensor_tensor(out=g2[:, k, :, :], in0=prev, scalar=decay[:, 0:1],
                                                       in1=ub[:, q, i, :, :], op0=ALU.mult, op1=ALU.add).then_inc(rec, 1)
                if live(s, L_H2):
                    nc.vector.bn_aggr(mv3[:, q2, GR - 1, :], st3[:, GR - 1, :]).then_inc(ag, 1)
            slots(dve, slot, L_OUT)

        @block.tensor
        def _(pe):
            pe.wait_ge(consts, 64)
            nc.tensor.transpose(p_l[:, 0, 0:E], gnat[:], ident[0:E, 0:E]).then_inc(gt_ps, 1)
            pe.wait_ge(gt_sb, 1)

            def slot(s, q, region):
                if live(s, L_Y):
                    g, q2 = s - L_Y, (q - L_Y) % 2
                    pe.wait_ge(rec, 4 * (g + 1))
                    wait(pe, h2_ok, g - 1)
                    for i in range(GR):
                        j, o = GR * ((q - L_Y) % 4) + i, p_y[:, q2, i * 128:(i + 1) * 128]
                        nc.tensor.matmul(o, g2[:, q2 * GR + i, 0, :], turn[:, j, 0, :], start=True, stop=False)
                        ins = nc.tensor.matmul(o, g2[:, q2 * GR + i, 1, :], turn[:, j, 1, :], start=False, stop=True)
                    ins.then_inc(y_ps, 1)
                if live(s, L_FF):
                    g, q2 = s - L_FF, (q - L_FF) % 2
                    pe.wait_ge(xT_sb, g + 1)
                    wait(pe, silu_ok, g)
                    nc.tensor.matmul(p_a[:], w13[:, 0, :], xTs[:, q2, :], start=True, stop=True).then_inc(a_ps, 1)
                    wait(pe, ix_ok, 4 * (g - 1))
                    for i in range(GR):
                        ins = nc.tensor.matmul(p_l[:, q2, i * E:(i + 1) * E], xTs[:, q2, i * 128:(i + 1) * 128],
                                               gT[:], start=True, stop=True)
                    ins.then_inc(lg_ps, 1)
                    wait(pe, hs_ok, g)
                    nc.tensor.matmul(p_z[:], w13[:, 1, :], xTs[:, q2, :], start=True, stop=True).then_inc(z_ps, 1)
                if live(s, L_HS):
                    g, q2 = s - L_HS, (q - L_HS) % 2
                    pe.wait_ge(hs_ok, g + 1)
                    wait(pe, out_ok, g)
                    for i in range(GR):
                        ins = nc.tensor.matmul(p_s[:, i * 128:(i + 1) * 128], hs[:, q2, i * 128:(i + 1) * 128], w2s[:],
                                               start=True, stop=True)
                    ins.then_inc(sh_ps, 1)
                if live(s, L_X3):
                    g, r = s - L_X3, (q - L_X3) % 4
                    pe.wait_ge(x3_ok, 4 * (g + 1))
                    wait(pe, xT_sb, g)
                    for i in range(GR):
                        ins = nc.tensor.transpose(p_xT[:, i * 128:(i + 1) * 128], x3[:, r, i, 0:D], ident[:])
                    ins.then_inc(xT_ps, 1)
            slots(pe, slot, L_ST)


def routed(nc, keep, scratch, w13, w2, out):
    ident, top = keep["ident"], keep["top"]
    T = CAP // 128
    L_SEL, L_IDX, L_T, L_H, L_Y, L_SC = 0, 1, 3, 4, 5, 6
    U = 8
    with ExitStack() as ctx:
        def sb(name, shape, dt=F32):
            return ctx.enter_context(nc.sbuf_tensor("r_" + name, shape, dt))

        def ps(name, shape):
            return ctx.enter_context(nc.psum_tensor("r_" + name, shape, F32))

        def sem(name):
            return keep["sems"].enter_context(nc.semaphore("r_" + name))

        cnt = sb("cnt", [128, E, NP], F16)
        is0 = sb("is0", [128, 2, NP], BF16)
        is1 = sb("is1", [128, 2, NP], BF16)
        ecol = sb("ecol", [128, E])
        slot_row = sb("slot_row", [128, CAP])
        slot_col = sb("slot_col", [128, T])
        slot_half = sb("slot_half", [128, T])
        empty_row = sb("empty_row", [128, T])
        before = sb("before", [128, 128])
        one_on = sb("one_on", [128, 1])
        rowp1 = sb("rowp1", [128, 1], F16)
        tot = sb("tot", [128, E])
        exc = sb("exc", [128, E])
        inc = sb("inc", [128, E])
        exc16 = sb("exc16", [128, E], F16)
        past = sb("past", [128, CAP], F16)
        S = sb("S", [128, 2, CAP], F16)
        le = sb("le", [128, NP])
        sg_junk = sb("sg_junk", [128, NP])
        nstar = sb("nstar", [128, 2, T])
        signs = sb("signs", [128, 2])
        flat = sb("flat", [128, T])
        vac = sb("vac", [128, T])
        ridx = sb("ridx", [128, U, T], U32)
        xg = sb("xg", [128, U, T, ROW])
        sv = sb("sv", [128, 2, T, 2])
        wt = sb("wt", [128, 5, T])
        wgt = sb("wgt", [128, 2, T])
        xT = sb("xT", [128, 2, CAP])
        wr = sb("wr", [128, 4, 2 * HID])
        w2r = sb("w2r", [HID, 4, D])
        sg = sb("sg", [HID, 2, CAP])
        asg = sb("asg", [HID, CAP])
        hh = sb("hh", [HID, 2, CAP])
        ys = sb("ys", [128, 2, T, D])
        p_n = [ps(f"p_n{t}", [128, 512]) for t in range(T)]
        p_b = ps("p_b", [128, 512])
        p_x, p_a, p_z, p_y = (ps(n, [128, 512]) for n in ("p_x", "p_a", "p_z", "p_y"))

        w_in = [sem(f"w_in{i}") for i in range(4)]
        gathered = [sem(f"gathered{i}") for i in range(U)]
        names = ("iotas m_ok c_ok tot_ok exc_ps exc_ok past_ok S_ok sel_ps cnt0 cnt1 n1 fl vc ridx_ok T_ps T_sb a_ps z_ps "
                 "sv_ok w_ok sg_ok asg_ok h_ok y_ps ys_ok added wk passed").split()
        (iotas, m_ok, c_ok, tot_ok, exc_ps, exc_ok, past_ok, S_ok, sel_ps, cnt0, cnt1, n1, fl, vc, ridx_ok, T_ps, T_sb,
         a_ps, z_ps, sv_ok, w_ok, sg_ok, asg_ok, h_ok, y_ps, ys_ok, added, wk, passed) = (sem(n) for n in names)
        block = ctx.enter_context(nc.Block())

        def slots(eng, slot):
            for s in range(U):
                slot(s, s)
            with eng.Fori(1, E // U) as c:
                for q in range(U):
                    slot(U * c + q, q)
            for s in range(E, E + L_SC):
                slot(s, s % U)

        def live(s, lag):
            return not isinstance(s, int) or 0 <= s - lag < E

        @block.sync
        def _(sp):
            def slot(s, q):
                if live(s, 0):
                    wait(sp, z_ps, s - 3)
                    sp.dma_start(wr[:, q % 4, :], w13[bass.ds(s, 1), :, :].rearrange("a p n -> (a p) n")).then_inc(w_in[q % 4], 16)
                    wait(sp, y_ps, s - 3)
                    sp.dma_start(w2r[:, q % 4, :], w2[bass.ds(s, 1), :, :].rearrange("a p n -> (a p) n")).then_inc(w_in[q % 4], 16)
            slots(sp, slot)

        @block.gpsimd
        def _(pool):
            nc.gpsimd.iota(ecol[:], [[1, E]], base=0, channel_multiplier=0, allow_small_or_imprecise_dtypes=True).then_inc(iotas, 1)
            nc.gpsimd.iota(slot_row[:], [[1, CAP]], base=0, channel_multiplier=0, allow_small_or_imprecise_dtypes=True).then_inc(iotas, 1)
            nc.gpsimd.iota(slot_col[:], [[128, T]], base=0, channel_multiplier=1, allow_small_or_imprecise_dtypes=True).then_inc(iotas, 1)
            nc.gpsimd.iota(empty_row[:], [[128, T]], base=B * NP, channel_multiplier=1, allow_small_or_imprecise_dtypes=True).then_inc(iotas, 1)
            nc.gpsimd.iota(one_on[:], [[0, 1]], base=1, channel_multiplier=1, allow_small_or_imprecise_dtypes=True).then_inc(iotas, 1)
            nc.gpsimd.memset(before[:], 1.0).then_inc(iotas, 1)
            pool.wait_ge(iotas, 6)
            nc.gpsimd.tensor_copy(rowp1[:], one_on[:]).then_inc(iotas, 1)
            nc.gpsimd.tensor_scalar(slot_half[:], slot_col[:], 0.5, None, ALU.add).then_inc(iotas, 1)
            nc.gpsimd.affine_select(out=before[:], in_=before[:], compare_op=ALU.is_gt, fill=0.0, base=0,
                                    pattern=[[1, 128]], channel_multiplier=-1).then_inc(iotas, 1)

            last_row = pool.to_reg(ROWS - 1)

            def slot(s, q):
                if live(s, L_SC):
                    g, r = s - L_SC, (q - L_SC) % U
                    pool.wait_ge(ys_ok, T * (g + 1))
                    wait(pool, added, 16 * T * g)
                    pool.sem_inc(passed, 1)
                    for t in range(T):
                        nc.gpsimd.indirect_dma_start(out, bass.IndirectOffsetOnAxis(ap=ridx[:, r, t:t + 1], axis=0),
                                                     ys[:, r % 2, t, :], None, bounds_check=last_row, oob_is_err=True,
                                                     compute_op=ALU.add).then_inc(added, 16)
                if live(s, L_IDX):
                    g, r = s - L_IDX, (q - L_IDX) % U
                    wait(pool, w_ok, g - U + 1)
                    pool.wait_ge(ridx_ok, g + 1)
                    pool.sem_inc(passed, 1)
                    for t in range(T):
                        nc.gpsimd.indirect_dma_start(xg[:, r, t, :], None, scratch["x3"],
                                                     bass.IndirectOffsetOnAxis(ap=ridx[:, r, t:t + 1], axis=0),
                                                     bounds_check=last_row, oob_is_err=True).then_inc(gathered[r], 16)
            slots(pool, slot)
            pool.wait_ge(added, 16 * T * E)

        @block.scalar
        def _(act):
            act.wait_ge(iotas, 9)

            def slot(s, q):
                if live(s, L_IDX):
                    g = s - L_IDX
                    act.wait_ge(sel_ps, g + 1)
                    wait(act, n1, g - 1)
                    nc.scalar.activation(sg_junk[:], p_n[1][:], ACT.Sign, bias=slot_half[:, 1:2], scale=-1.0,
                                         accum_out=signs[:, (q - 1) % 2:(q - 1) % 2 + 1]).then_inc(cnt1, 1)
                if live(s, L_H):
                    g, q2 = s - L_H, q % 2
                    act.wait_ge(a_ps, g + 1)
                    wait(act, asg_ok, g - 1)
                    nc.scalar.activation(sg[:, q2, :], p_a[0:HID, 0:CAP], ACT.Sigmoid).then_inc(sg_ok, 1)
                if live(s, L_T):
                    g, q2, r = s - L_T, (q - L_T) % 2, (q - L_T) % U
                    act.wait_ge(gathered[r], 4 * (g - r) + 16 * T)
                    wait(act, w_ok, g - 1)
                    nc.scalar.activation(sv[:, q2, :, :], xg[:, r, :, D:D + 2], ACT.Sigmoid).then_inc(sv_ok, 1)
                    act.wait_ge(T_ps, g + 1)
                    wait(act, z_ps, g - 1)
                    nc.scalar.activation(xT[:, q2, :], p_x[:, 0:CAP], ACT.Copy).then_inc(T_sb, 1)
                if live(s, L_Y):
                    g, q2 = s - L_Y, (q - L_Y) % 2
                    act.wait_ge(y_ps, g + 1)
                    act.wait_ge(w_ok, g + 1)
                    wait(act, added, 16 * T * (g - 1))
                    for t in range(T):
                        nc.scalar.activation(ys[:, q2, t, :], p_y[:, t * D:(t + 1) * D], ACT.Identity,
                                             scale=wgt[:, q2, t:t + 1]).then_inc(ys_ok, 1)
            slots(act, slot)

        @block.vector
        def _(dve):
            dve.wait_ge(iotas, 9)
            with dve.Fori(0, E // 2) as c:
                for q in range(2):
                    e = 2 * c + q
                    wait(dve, c_ok, e - 1 if q else e)
                    nc.vector.tensor_scalar(is0[:, q, :], top[:, 0, :], ecol[:, bass.ds(e, 1)], None, ALU.is_equal).then_inc(m_ok, 1)
                    nc.vector.tensor_scalar(is1[:, q, :], top[:, 1, :], ecol[:, bass.ds(e, 1)], None, ALU.is_equal).then_inc(m_ok, 1)
                    dve.wait_ge(m_ok, 2 * (e + 1))
                    nc.vector.tensor_tensor_scan(cnt[:, bass.ds(e, 1), :].rearrange("p a n -> p (a n)"), is0[:, q, :], is1[:, q, :],
                                                 0.0, ALU.add, ALU.add).then_inc(c_ok, 1)
            dve.wait_ge(c_ok, E)
            nc.vector.tensor_copy(tot[:], cnt[:, :, NP - 1]).then_inc(tot_ok, 1)
            dve.wait_ge(exc_ps, 1)
            dve.wait_ge(tot_ok, 1)
            nc.vector.tensor_copy(exc[:], p_b[:, 0:E]).then_inc(exc_ok, 1)
            nc.vector.tensor_tensor(inc[:], tot[:], p_b[:, 0:E], ALU.add).then_inc(exc_ok, 1)
            nc.vector.tensor_scalar(exc16[:], p_b[:, 0:E], 4.0 * CAP, None, ALU.min).then_inc(exc_ok, 1)
            dve.wait_ge(exc_ok, 3)

            def slot(s, q):
                if live(s, L_SEL):
                    wait(dve, S_ok, s)
                    nc.vector.tensor_scalar(past[:], slot_row[:], inc[:, bass.ds(s, 1)], None, ALU.is_ge).then_inc(past_ok, 1)
                    wait(dve, past_ok, s + 1)
                    wait(dve, sel_ps, s - 1)
                    nc.vector.scalar_tensor_tensor(out=S[:, q % 2, :], in0=slot_row[:], scalar=exc[:, bass.ds(s, 1)],
                                                   in1=past[:], op0=ALU.is_ge, op1=ALU.subtract).then_inc(S_ok, 1)
                if live(s, L_IDX):
                    g, q2, r = s - L_IDX, (q - L_IDX) % 2, (q - L_IDX) % U
                    dve.wait_ge(sel_ps, g + 1)
                    wait(dve, fl, g - 1)
                    wait(dve, cnt0, g)
                    nc.vector.tensor_scalar(le[:], p_n[0][:], slot_col[:, 0:1], 0.0, ALU.is_le, ALU.add,
                                            accum_out=nstar[:, q2, 0:1]).then_inc(cnt0, 1)
                    dve.wait_ge(cnt1, g + 1)
                    nc.vector.tensor_scalar(nstar[:, q2, 1:2], signs[:, q2:q2 + 1], 0.5, NP / 2, ALU.mult, ALU.add).then_inc(n1, 1)
                    wait(dve, ridx_ok, g)
                    nc.vector.scalar_tensor_tensor(out=vac[:], in0=p_b[:, 0:T], scalar=0.0, in1=empty_row[:],
                                                   op0=ALU.is_equal, op1=ALU.mult).then_inc(vc, 1)
                    dve.wait_ge(cnt0, g + 1)
                    dve.wait_ge(n1, g + 1)
                    nc.vector.scalar_tensor_tensor(out=flat[:], in0=p_b[:, 0:T], scalar=float(NP), in1=nstar[:, q2, :],
                                                   op0=ALU.mult, op1=ALU.add).then_inc(fl, 1)
                    dve.wait_ge(fl, g + 1)
                    dve.wait_ge(vc, g + 1)
                    wait(dve, added, 16 * T * (g - U + 1))
                    nc.vector.scalar_tensor_tensor(out=ridx[:, r, :], in0=flat[:], scalar=float(-NP), in1=vac[:],
                                                   op0=ALU.add, op1=ALU.add).then_inc(ridx_ok, 1)
                if live(s, L_H):
                    g, q2 = s - L_H, q % 2
                    wait(dve, sg_ok, g + 1)
                    wait(dve, h_ok, g)
                    nc.vector.tensor_tensor(asg[:], sg[:, q2, :], p_a[0:HID, 0:CAP], ALU.mult).then_inc(asg_ok, 1)
                    wait(dve, asg_ok, g + 1)
                    wait(dve, z_ps, g + 1)
                    wait(dve, y_ps, g - 1)
                    nc.vector.tensor_tensor(hh[:, q2, :], asg[:], p_z[0:HID, 0:CAP], ALU.mult).then_inc(h_ok, 1)
                if live(s, L_H):
                    g, q2, r = s - L_H, q % 2, (q - L_H) % U
                    s1, s2, e1 = sv[:, q2, :, 0], sv[:, q2, :, 1], xg[:, r, :, D + 2]
                    me = ecol[:, bass.ds(g, 1)]
                    dve.wait_ge(sv_ok, g + 1)
                    wait(dve, w_ok, g)
                    nc.vector.scalar_tensor_tensor(out=wt[:, 0, :], in0=e1, scalar=me, in1=s1, op0=ALU.is_equal,
                                                   op1=ALU.mult).then_inc(wk, 1)
                    nc.vector.scalar_tensor_tensor(out=wt[:, 1, :], in0=e1, scalar=me, in1=s2, op0=ALU.not_equal,
                                                   op1=ALU.mult).then_inc(wk, 1)
                    nc.vector.scalar_tensor_tensor(out=wt[:, 2, :], in0=s1, scalar=1e-20, in1=s2, op0=ALU.add,
                                                   op1=ALU.add).then_inc(wk, 1)
                    dve.wait_ge(wk, 5 * g + 3)
                    nc.vector.tensor_tensor(wt[:, 3, :], wt[:, 0, :], wt[:, 1, :], ALU.add).then_inc(wk, 1)
                    nc.vector.reciprocal(wt[:, 4, :], wt[:, 2, :]).then_inc(wk, 1)
                    dve.wait_ge(wk, 5 * g + 5)
                    wait(dve, ys_ok, T * (g - 1))
                    nc.vector.scalar_tensor_tensor(out=wgt[:, q2, :], in0=wt[:, 3, :], scalar=ROUTE_SCALE, in1=wt[:, 4, :],
                                                   op0=ALU.mult, op1=ALU.mult).then_inc(w_ok, 1)
            slots(dve, slot)

        @block.tensor
        def _(pe):
            pe.wait_ge(iotas, 9)
            pe.wait_ge(tot_ok, 1)
            nc.tensor.matmul(p_b[:, 0:E], before[:], tot[:], start=True, stop=True).then_inc(exc_ps, 1)
            pe.wait_ge(exc_ok, 3)

            def slot(s, q):
                if live(s, L_SEL):
                    q2 = q % 2
                    pe.wait_ge(S_ok, s + 1)
                    wait(pe, cnt0, s)
                    wait(pe, cnt1, s)
                    wait(pe, fl, s)
                    for t in range(T):
                        St = S[:, q2, t * 128:(t + 1) * 128]
                        nc.tensor.matmul(p_n[t][:], St, cnt[:, bass.ds(s, 1), :].rearrange("p a n -> p (a n)"), start=True, stop=False)
                        nc.tensor.matmul(p_n[t][:], St, exc16[:, bass.ds(s, 1)].to_broadcast([128, NP]), start=False, stop=True)
                        ins = nc.tensor.matmul(p_b[:, t:t + 1], St, rowp1[:], start=True, stop=True)
                    ins.then_inc(sel_ps, 1)
                if live(s, L_Y):
                    g, q2 = s - L_Y, (q - L_Y) % 2
                    pe.wait_ge(h_ok, g + 1)
                    wait(pe, ys_ok, T * g)
                    for t in range(T):
                        ins = nc.tensor.matmul(p_y[:, t * D:(t + 1) * D], hh[:, q2, t * 128:(t + 1) * 128], w2r[:, (q - L_Y) % 4, :],
                                               start=True, stop=True)
                    ins.then_inc(y_ps, 1)
                if live(s, L_T):
                    g, q2, r = s - L_T, (q - L_T) % 2, (q - L_T) % U
                    pe.wait_ge(gathered[r], 4 * (g - r) + 16 * T)
                    wait(pe, T_sb, g)
                    for t in range(T):
                        ins = nc.tensor.transpose(p_x[:, t * 128:(t + 1) * 128], xg[:, r, t, 0:D], ident[:])
                    ins.then_inc(T_ps, 1)
                    pe.wait_ge(T_sb, g + 1)
                    pe.wait_ge(w_in[r % 4], 8 * (g - r % 4) + 32)
                    wait(pe, asg_ok, g)
                    nc.tensor.matmul(p_a[0:HID, 0:CAP], wr[:, r % 4, 0:HID], xT[:, q2, :], start=True, stop=True).then_inc(a_ps, 1)
                    wait(pe, h_ok, g)
                    nc.tensor.matmul(p_z[0:HID, 0:CAP], wr[:, r % 4, HID:2 * HID], xT[:, q2, :], start=True, stop=True).then_inc(z_ps, 1)
            slots(pe, slot)


def kernel(**inputs):
    import numpy as np
    import concourse.bacc as bacc
    from concourse.bass_utils import run_bass_kernel_spmd

    a = {k.replace("L0_", "").replace("tok_", "").replace("attn_", "").replace("ffn_", ""): np.asarray(v)
         for k, v in inputs.items()}
    x = a["x"]
    steps = (FG * GR + 1) * STRIDE
    arrays = {
        "x": np.pad(x, ((0, 0), (0, steps - x.shape[1]), (0, 0)), mode="edge").reshape(B, steps * C),
        "W": a["W"].reshape(C, PATCH, D).transpose(1, 0, 2).reshape(C * PATCH, D),
        "b": a["b"], "ln_g": a["ln_g"], "ln_b": a["ln_b"],
        "posA": np.pad(a["pos_emb"][0, :FIRST], ((0, GR), (0, 0))).reshape(1, -1),
        "pos": np.pad(a["pos_emb"][0], ((0, NP - STEPS), (0, 0))),
        "type_emb": a["type_emb"], "Br": a["B_real"], "Bi": a["B_img"],
        "nu": a["nu"], "theta": a["theta"], "delta": a["delta"], "h0r": a["h0_real"], "h0i": a["h0_img"],
        "gate_w": a["gate_w"], "w13": np.concatenate([a["w1"], a["w3"]], axis=2), "w2": a["w2"],
        "sw1": a["sw1"], "sw3": a["sw3"], "sw2": a["sw2"],
    }
    nc = bacc.Bacc("TRN2", target_bir_lowering=False, num_devices=1)
    fed, args = {}, []
    for name, v in arrays.items():
        v = np.ascontiguousarray(v)
        fed[f"in_{name}"] = v
        args.append(nc.dram_tensor(f"in_{name}", v.shape, mybir.dt.from_np(v.dtype), kind="ExternalInput").ap())
    out = nc.dram_tensor("out_rows", (ROWS, D), F32, kind="ExternalOutput").ap()
    tower(nc, *args, out)
    r = run_bass_kernel_spmd(nc, [fed], core_ids=[0])
    return r.results[0]["out_rows"][:B * NP].reshape(B, NP, D)[:, :STEPS]
```

```python
from contextlib import ExitStack

import concourse.bass as bass
from concourse import mybir

F32 = mybir.dt.float32
F16 = mybir.dt.float16
BF16 = mybir.dt.bfloat16
U32 = mybir.dt.uint32
ALU = mybir.AluOpType
ACT = mybir.ActivationFunctionType
AX = mybir.AxisListType.X

B, D = 128, 128
STEPS = 511
NP = 512
C, PATCH, STRIDE = 8, 16, 8
SEG = STRIDE * C
FIRST = 128
GR, CH = 4, 16
NG = NP // GR
NC_A = FIRST // CH
NC = NP // CH
E, HID, CAP = 64, 64, 256
ROUTE_SCALE = 2.5
EPS = 1e-5
ROW = D + 4
ROWS = B * NP + CAP
FG = FIRST // GR + 1
HALF_PI = 1.5707963267948966


def wait(eng, sem, value):
    if isinstance(value, int) and value <= 0:
        return
    eng.wait_ge(sem, value)


def tower(nc, x, W, b, ln_g, ln_b, posA, pos, type_emb, Br, Bi, nu, theta, delta, h0r, h0i,
          gate_w, w13, w2, sw1, sw3, sw2, out):
    u_dram = nc.dram_tensor("u_dram", [128, FG, GR * 2 * 128], F32, kind="Internal").ap()
    h1_dram = nc.dram_tensor("h1_dram", [128, FG, GR * 128], F32, kind="Internal").ap()
    rT_dram = nc.dram_tensor("rT_dram", [NP - FIRST, 128], F32, kind="Internal").ap()
    x3_dram = nc.dram_tensor("x3_dram", [ROWS, ROW], F32, kind="Internal").ap()
    scratch = dict(u=u_dram, h1=h1_dram, rT=rT_dram, x3=x3_dram)
    with ExitStack() as ctx:
        def sb(name, shape, dt=F32):
            return ctx.enter_context(nc.sbuf_tensor(name, shape, dt))

        keep = dict(
            sems=ctx,
            ident=sb("ident", [128, 128]), ones=sb("ones", [128, 128]),
            turn=sb("turn", [128, CH, 2, 128]),
            Bj=sb("Bj", [128, CH, 2, 128]),
            colC=sb("colC", [128, CH + 1]), colS=sb("colS", [128, CH + 1]),
            decay=sb("decay", [128, 1]),
            base=sb("base", [128, 128]),
            carry=sb("carry", [128, 2, 128]),
            top=sb("top", [128, 2, NP]),
            eps=sb("eps", [128, GR]), minus=sb("minus", [128, GR]),
            halfneg=sb("halfneg", [128, NP]),
            g2=sb("g2", [128, 2 * GR, 2, 128]),
        )
        setup(nc, keep, W, Br, Bi, nu, theta, delta, h0r, h0i)
        front(nc, keep, scratch, x, W, b, ln_g, ln_b, posA, type_emb)
        with ExitStack() as inner:
            A = inner.enter_context(nc.sbuf_tensor("A", [128, CH, 2, 128], F32))
            P = inner.enter_context(nc.sbuf_tensor("P", [128, NP - FIRST, 2], F32))
            keep["A"], keep["P"] = A, P
            between(nc, keep, scratch, pos)
            scan(nc, keep, scratch, pos, gate_w, sw1, sw3, sw2, out)
        routed(nc, keep, scratch, w13, w2, out)


def setup(nc, keep, W, Br, Bi, nu, theta, delta, h0r, h0i):
    ident, ones, turn, Bj = keep["ident"], keep["ones"], keep["turn"], keep["Bj"]
    colC, colS, decay, carry = keep["colC"], keep["colS"], keep["decay"], keep["carry"]
    with ExitStack() as ctx:
        def sb(name, shape, dt=F32):
            return ctx.enter_context(nc.sbuf_tensor(name, shape, dt))

        def sem(name):
            return keep["sems"].enter_context(nc.semaphore("c_" + name))

        cols = sb("cols", [128, 8])
        tmp = sb("s_tmp", [128, 4, CH])
        Bw = sb("Bw", [128, 2, 128])
        dB = sb("dB", [128, 2, 128])
        diag_delta = sb("diag_delta", [128, 128])
        zeros = sb("zeros", [128, 128])
        t4 = sb("t4", [128, 4, GR, 128])
        ps = ctx.enter_context(nc.psum_tensor("s_ps", [128, 2, GR, 128], F32))
        psd = ctx.enter_context(nc.psum_tensor("s_psd", [128, 512], F32))
        s_in, s_id, s_act, s_dve, s_diag, s_bc, s_bcu, s_pd = (
            sem(n) for n in ("s_in", "s_id", "s_act", "s_dve", "s_diag", "s_bc", "s_bcu", "s_pd"))
        block = ctx.enter_context(nc.Block())

        @block.sync
        def _(sp):
            for i, v in enumerate((nu, theta, delta, h0r, h0i)):
                sp.dma_start(cols[:, i:i + 1], v.rearrange("(p a) -> p a", a=1)).then_inc(s_in, 16)
            sp.dma_start(Bw[:, 0, :], Br).then_inc(s_in, 16)
            sp.dma_start(Bw[:, 1, :], Bi).then_inc(s_in, 16)
            sp.wait_ge(s_in, 112)

        @block.gpsimd
        def _(pool):
            nc.gpsimd.memset(ident[:], 0.0).then_inc(s_id, 1)
            nc.gpsimd.memset(ones[:], 1.0).then_inc(s_id, 1)
            nc.gpsimd.memset(zeros[:], 0.0).then_inc(s_id, 1)
            nc.gpsimd.memset(keep["halfneg"][:], -0.5).then_inc(s_id, 1)
            nc.gpsimd.memset(keep["eps"][:], EPS)
            nc.gpsimd.memset(keep["minus"][:], -1.0)
            nc.gpsimd.memset(cols[:, 5:6], HALF_PI).then_inc(s_id, 1)
            pool.wait_ge(s_id, 5)
            nc.gpsimd.affine_select(out=ident[:], in_=ident[:], compare_op=ALU.not_equal, fill=1.0, base=0,
                                    pattern=[[-1, 128]], channel_multiplier=1).then_inc(s_id, 1)

        @block.scalar
        def _(act):
            act.wait_ge(s_in, 112)
            act.wait_ge(s_id, 5)
            nc.scalar.activation(cols[:, 6:7], cols[:, 0:1], ACT.Exp).then_inc(s_act, 1)
            act.wait_ge(s_act, 1)
            nc.scalar.activation(decay[:], cols[:, 6:7], ACT.Exp, scale=-1.0).then_inc(s_act, 1)
            nc.scalar.activation(colC[:, 1:2], cols[:, 1:2], ACT.Sin, bias=cols[:, 5:6]).then_inc(s_act, 1)
            nc.scalar.activation(colS[:, 1:2], cols[:, 1:2], ACT.Sin).then_inc(s_act, 1)

        @block.vector
        def _(dve):
            done = [0]

            def then(ins):
                done[0] += 1
                ins.then_inc(s_dve, 1)
                dve.wait_ge(s_dve, done[0])

            nc.vector.memset(colC[:, 0:1], 1.0).then_inc(s_dve, 1)
            nc.vector.memset(colS[:, 0:1], 0.0).then_inc(s_dve, 1)
            done[0] = 2
            dve.wait_ge(s_dve, 2)
            dve.wait_ge(s_act, 4)
            k = 1
            while k < CH:
                a, o = slice(1, k + 1), slice(k + 1, 2 * k + 1)
                then(nc.vector.tensor_scalar(tmp[:, 0, 0:k], colS[:, a], colS[:, k:k + 1], None, ALU.mult))
                then(nc.vector.tensor_scalar(tmp[:, 1, 0:k], colC[:, a], colS[:, k:k + 1], None, ALU.mult))
                then(nc.vector.scalar_tensor_tensor(out=colC[:, o], in0=colC[:, a], scalar=colC[:, k:k + 1],
                                                    in1=tmp[:, 0, 0:k], op0=ALU.mult, op1=ALU.subtract))
                then(nc.vector.scalar_tensor_tensor(out=colS[:, o], in0=colS[:, a], scalar=colC[:, k:k + 1],
                                                    in1=tmp[:, 1, 0:k], op0=ALU.mult, op1=ALU.add))
                k *= 2
            then(nc.vector.tensor_scalar(tmp[:, 0, 0:1], cols[:, 4:5], colS[:, 1:2], None, ALU.mult))
            then(nc.vector.tensor_scalar(tmp[:, 1, 0:1], cols[:, 3:4], colS[:, 1:2], None, ALU.mult))
            then(nc.vector.scalar_tensor_tensor(out=tmp[:, 2, 0:1], in0=cols[:, 3:4], scalar=colC[:, 1:2],
                                                in1=tmp[:, 0, 0:1], op0=ALU.mult, op1=ALU.subtract))
            then(nc.vector.scalar_tensor_tensor(out=tmp[:, 3, 0:1], in0=cols[:, 4:5], scalar=colC[:, 1:2],
                                                in1=tmp[:, 1, 0:1], op0=ALU.mult, op1=ALU.add))
            dve.wait_ge(s_id, 6)
            for c in range(2):
                then(nc.vector.tensor_scalar(carry[:, c, :], zeros[:], tmp[:, 2 + c, 0:1], None, ALU.add))
            then(nc.vector.tensor_scalar(diag_delta[:], ident[:], cols[:, 2:3], None, ALU.mult))
            for j in range(CH):
                nc.vector.tensor_scalar(turn[:, j, 0, :], ident[:], colC[:, j:j + 1], None,
                                        ALU.mult).then_inc(s_diag, 1)
                nc.vector.tensor_scalar(turn[:, j, 1, :], ident[:], colS[:, j:j + 1], -1.0,
                                        ALU.mult, ALU.mult).then_inc(s_diag, 1)
            dve.wait_ge(s_pd, 1)
            for c in range(2):
                then(nc.vector.tensor_tensor(dB[:, c, :], Bw[:, c, :], psd[:, 0:128], ALU.mult))
            for q in range(CH // GR):
                dve.wait_ge(s_bc, q + 1)
                bre = dB[:, 0, :].unsqueeze(1).to_broadcast([128, GR, 128])
                bim = dB[:, 1, :].unsqueeze(1).to_broadcast([128, GR, 128])
                for i, (p, w) in enumerate(((0, bre), (1, bim), (0, bim), (1, bre))):
                    ins = nc.vector.tensor_tensor(t4[:, i, :, :], ps[:, p, :, :], w, ALU.mult)
                    ins.then_inc(s_dve, 1)
                    done[0] += 1
                dve.wait_ge(s_dve, done[0])
                js = slice(q * GR, (q + 1) * GR)
                then(nc.vector.tensor_tensor(Bj[:, js, 0, :], t4[:, 0, :, :], t4[:, 1, :, :], ALU.subtract))
                ins = nc.vector.tensor_tensor(Bj[:, js, 1, :], t4[:, 2, :, :], t4[:, 3, :, :], ALU.add)
                then(ins)
                nc.vector.memset(tmp[:, 0, 0:1], 0.0).then_inc(s_bcu, 1)

        @block.tensor
        def _(pe):
            pe.wait_ge(s_id, 6)
            pe.wait_ge(s_diag, 1)
            nc.tensor.matmul(psd[:, 0:128], ones[:], diag_delta[:], start=True, stop=True).then_inc(s_pd, 1)
            pe.wait_ge(s_diag, 2 * CH)
            for q in range(CH // GR):
                wait(pe, s_bcu, q)
                for p in range(2):
                    ins = nc.tensor.matmul(ps[:, p, :, :], ones[:], turn[:, q * GR:(q + 1) * GR, p, :],
                                           start=True, stop=True)
                ins.then_inc(s_bc, 1)


def front(nc, keep, scratch, x, W, b, ln_g, ln_b, posA, type_emb):
    ident, Bj, base = keep["ident"], keep["Bj"], keep["base"]
    L_T, L_H, L_BN = 0, 1, 1
    L_Z, L_AFF, L_E = 2, 3, 4
    L_TYPE, L_MT, L_ROW = 2, 3, 4
    L_V, L_XN, L_XT, L_U, L_OUT = 5, 6, 7, 8, 9
    L_H1ST, L_UST = 6, 10
    AHEAD = 1
    used = []
    PEEL = 3
    LAST = FG + L_UST
    with ExitStack() as ctx:
        def sb(name, shape, dt=F32):
            return ctx.enter_context(nc.sbuf_tensor(name, shape, dt))

        def ps(name, shape):
            return ctx.enter_context(nc.psum_tensor(name, shape, F32))

        def sem(name):
            used.append(nc.alloc_semaphore(name="f_" + name))
            return used[-1]

        XW = (GR + 1) * SEG
        xg = sb("xg", [128, 4, XW])
        rows = sb("rows", [17, 4, GR * 128])
        Wp = sb("Wp", [128, 128])
        brow = sb("brow", [1, 128])
        lng = sb("lng", [128, 128])
        lnb = sb("lnb", [128, 128])
        pT = sb("pT", [128, 2, GR, 128])
        hst = sb("hst", [128, GR, 6])
        gst = sb("gst", [128, GR, 6])
        pst = sb("pst", [128, GR, 6])
        OF_H, OF_G, OF_P = range(3)
        mv = sb("mv", [128, 2, 3, GR, 2])
        var = sb("var_in", [128, 2, 3, GR])
        negm = sb("negm", [128, 2, 2, GR])
        rs = sb("rs", [128, 2, 3, GR])
        nmr = sb("nmr", [128, 2, 2, GR])
        expo = sb("expo", [128, 3, GR])
        eps2 = sb("eps2", [128, 2, GR])
        minus2 = sb("minus2", [128, 2, GR])
        bessel = sb("bessel", [128, GR])
        z0 = sb("z0", [128, 2, GR, 128])
        z1 = sb("z1", [128, 2, GR, 128])
        z2 = sb("z2", [128, 2, GR, 128])
        er = sb("er", [128, 2, GR, 128])
        h1 = sb("h1", [128, 4, GR, 128])
        seg = sb("seg", [128, 2, GR + 1])
        pmm = sb("pmm", [128, 2, GR])
        rng = sb("rng", [128, 2, GR])
        tm = sb("tm", [128, 2, GR])
        mask = sb("mask", [128, 2, 17])
        mT = sb("mT", [17, 2, 128])
        xn = sb("xn", [128, 2, GR, 128])
        xnT = sb("xnT", [128, 2, GR, 128])
        us = sb("us", [128, 4, GR, 2, 128])
        p_pT, p_T, p_m, p_xT = (ps(n, [128, 512]) for n in ("p_pT", "p_T", "p_m", "p_xT"))
        p_H = ps("p_H", [128, 2, 512])
        p_u = ps("p_u", [128, GR, 2, 128])

        consts, pool_c, mv_zero = sem("consts"), sem("pool_c"), sem("mv_zero")
        x_in = [sem(f"x_in{i}") for i in range(4)]
        row_in = [sem(f"row_in{i}") for i in range(4)]
        h1_out = [sem(f"h1_out{i}") for i in range(4)]
        u_out = [sem(f"u_out{i}") for i in range(4)]
        (pT_ps, pT_sb, h_ps, hbn, hag, z_0, z_1, z_2, e_ok, segs, pbn, pag, pmm_ok, range_ok, tmk, m_ok,
         m_ps, m_sb, T_ps, h1_ok, gbn, gag, mv_used, rs_ok, nmr_ok, xn_ok, xT_ps, xT_sb, u_ps, u_sb, base_ok) = (
            sem(n) for n in
            "pT_ps pT_sb h_ps hbn hag z_0 z_1 z_2 e_ok segs pbn pag pmm_ok range_ok tmk m_ok "
            "m_ps m_sb T_ps h1_ok gbn gag mv_used rs_ok nmr_ok xn_ok xT_ps xT_sb u_ps u_sb base_ok".split())
        block = ctx.enter_context(nc.Block())

        def slots(eng, slot):
            for s in range(4 * PEEL):
                slot(s, s % 4)
            with eng.Fori(PEEL, FIRST // CH) as c:
                for q in range(4):
                    slot(4 * c + q, q)
            for s in range(FIRST // GR, LAST):
                slot(s, s % 4)

        def live(s, lag):
            return not isinstance(s, int) or 0 <= s - lag < FG

        def stats(s):
            return not isinstance(s, int) or s >= L_BN + 1

        @block.sync
        def _(sp):
            def load_x(g, r):
                wait(sp, segs, 2 * (g - 3))
                wait(sp, pT_ps, g - 3)
                sp.dma_start(xg[:, r, :], x[:, bass.ds(g * (GR * SEG), XW)]).then_inc(x_in[r], 16)

            for g in range(AHEAD):
                load_x(g, g)
            sp.dma_start(Wp[:], W).then_inc(consts, 16)
            sp.dma_start(brow[:], b.rearrange("(a n) -> a n", a=1)).then_inc(consts, 16)
            sp.dma_start(lng[:], ln_g.partition_broadcast(128)).then_inc(consts, 16)
            sp.dma_start(lnb[:], ln_b.partition_broadcast(128)).then_inc(consts, 16)
            sp.wait_ge(pool_c, 2)
            for r in range(4):
                for i in range(GR):
                    sp.dma_start(rows[4 * i:4 * i + 4, r, i * 128:(i + 1) * 128], type_emb).then_inc(consts, 16)

            def slot(s, q):
                if live(s, -AHEAD):
                    load_x(s + AHEAD, (q + AHEAD) % 4)
                if live(s, 1):
                    g, r = s - 1, (q - 1) % 4
                    wait(sp, T_ps, g - 3)
                    sp.dma_start(rows[16:17, r, :], posA[:, bass.ds(g * (GR * 128), GR * 128)]).then_inc(row_in[r], 16)
                if live(s, L_H1ST):
                    g, r = s - L_H1ST, (q - L_H1ST) % 4
                    wait(sp, h1_ok, g + 1)
                    sp.dma_start(scratch["h1"][:, bass.ds(g, 1), :].rearrange("p a n -> p (a n)"),
                                 h1[:, r, :, :].rearrange("p a n -> p (a n)")).then_inc(h1_out[r], 16)
                if live(s, L_UST):
                    g, r = s - L_UST, (q - L_UST) % 4
                    wait(sp, u_sb, 2 * (g + 1))
                    sp.dma_start(scratch["u"][:, bass.ds(g, 1), :].rearrange("p a n -> p (a n)"),
                                 us[:, r, :, :, :].rearrange("p a c n -> p (a c n)")).then_inc(u_out[r], 16)
            slots(sp, slot)
            for i in range(4):
                sp.wait_ge(h1_out[i], 16 * ((FG - i + 3) // 4))
                sp.wait_ge(u_out[i], 16 * ((FG - i + 3) // 4))

        @block.gpsimd
        def _(pool):
            nc.gpsimd.memset(rows[:], 0.0).then_inc(pool_c, 1)
            nc.gpsimd.memset(mask[:], 1.0).then_inc(pool_c, 1)
            nc.gpsimd.memset(expo[:, 0:2, :], -0.5).then_inc(pool_c, 1)
            nc.gpsimd.memset(expo[:, 2, :], 0.5).then_inc(pool_c, 1)
            nc.gpsimd.memset(eps2[:], EPS).then_inc(pool_c, 1)
            nc.gpsimd.memset(minus2[:], -1.0).then_inc(pool_c, 1)
            nc.gpsimd.memset(bessel[:], D / (D - 1.0)).then_inc(pool_c, 1)
            nc.gpsimd.memset(mv[:], 1.0).then_inc(mv_zero, 1)
            pool.wait_ge(pool_c, 7)
            pool.wait_ge(mv_zero, 1)
            pool.wait_ge(consts, 64 + 256)

            def slot(s, q):
                if stats(s):
                    n, m, k = s - L_BN, (q - 1) % 2, q % 2
                    if live(s, L_BN + 1):
                        wait(pool, hag, 4 * (s - L_BN))
                        wait(pool, pag, 4 * (s - L_BN))
                    if live(s, L_V + 1):
                        wait(pool, gag, 4 * (s - L_V))
                    wait(pool, rs_ok, n - 1)
                    nc.gpsimd.tensor_tensor(var[:, k, 0:2, :], mv[:, m, 0:2, :, 1], eps2[:], ALU.add).then_inc(mv_used, 1)
                    nc.gpsimd.tensor_tensor(var[:, k, 2, :], mv[:, m, 2, :, 1], bessel[:], ALU.mult).then_inc(mv_used, 1)
                    wait(pool, nmr_ok, n - 1)
                    nc.gpsimd.tensor_tensor(negm[:, k, :, :], mv[:, m, 0:2, :, 0], minus2[:], ALU.mult).then_inc(mv_used, 1)
                    wait(pool, mv_used, 3 * n)
                    if live(s, L_XN + 2):
                        wait(pool, xn_ok, 4 * (s - L_XN - 1))
                    if live(s, L_Z + 2):
                        wait(pool, z_0, 4 * (s - L_Z - 1))
                        wait(pool, tmk, 5 * (s - L_TYPE - 1))
                    nc.gpsimd.tensor_tensor(rs[:, k, :, :], var[:, k, :, :], expo[:], ALU.pow).then_inc(rs_ok, 1)
                    wait(pool, rs_ok, n)
                    nc.gpsimd.tensor_tensor(nmr[:, k, :, :], negm[:, k, :, :], rs[:, k, 0:2, :], ALU.mult).then_inc(nmr_ok, 1)
                if live(s, L_AFF):
                    g, q2 = s - L_AFF, (q - L_AFF) % 2
                    wait(pool, z_0, 4 * (g + 1))
                    wait(pool, z_2, g - 1)
                    nc.gpsimd.tensor_tensor(z1[:, q2, :, :], z0[:, q2, :, :],
                                            lng[:].unsqueeze(1).to_broadcast([128, GR, 128]), ALU.mult).then_inc(z_1, 1)
                    wait(pool, z_1, g + 1)
                    wait(pool, e_ok, g - 1)
                    nc.gpsimd.tensor_tensor(z2[:, q2, :, :], z1[:, q2, :, :],
                                            lnb[:].unsqueeze(1).to_broadcast([128, GR, 128]), ALU.add).then_inc(z_2, 1)
            slots(pool, slot)

        @block.scalar
        def _(act):
            def slot(s, q):
                if live(s, L_OUT):
                    g, r = s - L_OUT, (q - L_OUT) % 4
                    wait(act, u_ps, g + 1)
                    if not isinstance(s, int) or g >= 4:
                        act.wait_ge(u_out[r], 4 * (g - r))
                    nc.scalar.activation(us[:, r, 0:2, :, :], p_u[:, 0:2, :, :], ACT.Copy).then_inc(u_sb, 1)
                if live(s, L_T):
                    wait(act, pT_ps, s + 1)
                    wait(act, h_ps, s - 1)
                    nc.scalar.activation(pT[:, q % 2, :, :], p_pT[:].rearrange("p (a n) -> p a n", a=GR),
                                         ACT.Copy).then_inc(pT_sb, 1)
                if live(s, L_E):
                    g, q2 = s - L_E, (q - L_E) % 2
                    wait(act, z_2, g + 1)
                    wait(act, h1_ok, g - 1)
                    nc.scalar.activation(er[:, q2, :, :], z2[:, q2, :, :], ACT.Gelu).then_inc(e_ok, 1)
                if live(s, L_MT):
                    g, q2 = s - L_MT, (q - L_MT) % 2
                    wait(act, m_ps, g + 1)
                    wait(act, T_ps, g - 1)
                    nc.scalar.activation(mT[:, q2, :], p_m[0:17, 0:128], ACT.Copy).then_inc(m_sb, 1)
                if live(s, L_XN):
                    g, q2 = s - L_XN, (q - L_XN) % 2
                    wait(act, nmr_ok, s - L_BN)
                    wait(act, xT_ps, g - 1)
                    for i in range(GR):
                        nc.scalar.activation(xn[:, q2, i, :], h1[:, (q - L_XN) % 4, i, :], ACT.Identity,
                                             bias=nmr[:, q % 2, OF_G, i:i + 1], scale=rs[:, q % 2, OF_G, i:i + 1]).then_inc(xn_ok, 1)
                if live(s, L_Z):
                    g, q2 = s - L_Z, (q - L_Z) % 2
                    wait(act, nmr_ok, s - L_BN)
                    wait(act, z_1, g - 1)
                    for i in range(GR):
                        nc.scalar.activation(z0[:, q2, i, :], p_H[:, q2, i * 128:(i + 1) * 128], ACT.Identity,
                                             bias=nmr[:, q % 2, OF_H, i:i + 1], scale=rs[:, q % 2, OF_H, i:i + 1]).then_inc(z_0, 1)
            slots(act, slot)

        @block.vector
        def _(dve):
            dve.wait_ge(consts, 64 + 256)
            dve.wait_ge(mv_zero, 1)

            def slot(s, q):
                if live(s, L_OUT):
                    g, r = s - L_OUT, (q - L_OUT) % 4
                    wait(dve, u_ps, g + 1)
                    if not isinstance(s, int) or g >= 4:
                        dve.wait_ge(u_out[r], 4 * (g - r))
                    nc.vector.tensor_copy(us[:, r, 2:4, :, :], p_u[:, 2:4, :, :]).then_inc(u_sb, 1)
                if live(s, L_V):
                    g, q2, r = s - L_V, (q - L_V) % 2, (q - L_V) % 4
                    wait(dve, e_ok, g + 1)
                    wait(dve, T_ps, g + 1)
                    hs = h1[:, r, :, :]
                    if not isinstance(s, int) or g >= 4:
                        dve.wait_ge(h1_out[r], 4 * (g - r))
                    wait(dve, xn_ok, 4 * (g - 3))
                    nc.vector.tensor_tensor(hs, er[:, q2, :, :], p_T[:].rearrange("p (a n) -> p a n", a=GR),
                                            ALU.add).then_inc(h1_ok, 1)
                if live(s, L_BN):
                    g, q2 = s - L_BN, (q - L_BN) % 2
                    wait(dve, h_ps, g + 1)
                    wait(dve, hag, 4 * g)
                    for i in range(GR):
                        nc.vector.bn_stats(hst[:, i, :], p_H[:, q2, i * 128:(i + 1) * 128]).then_inc(hbn, 1)
                if live(s, L_V):
                    wait(dve, h1_ok, (s - L_V) + 1)
                    wait(dve, gag, 4 * (s - L_V))
                    for i in range(GR):
                        nc.vector.bn_stats(gst[:, i, :], h1[:, (q - L_V) % 4, i, :]).then_inc(gbn, 1)
                if live(s, L_BN):
                    wait(dve, hbn, 4 * (s - L_BN) + 4)
                if live(s, L_V):
                    wait(dve, gbn, 4 * (s - L_V) + 4)
                wait(dve, mv_used, 3 * (s - L_BN - 1))
                if live(s, L_XT):
                    g, q2 = s - L_XT, (q - L_XT) % 2
                    wait(dve, xT_ps, g + 1)
                    wait(dve, u_ps, g - 1)
                    nc.vector.tensor_copy(xnT[:, q2, :, :], p_xT[:].rearrange("p (a n) -> p a n", a=GR)).then_inc(xT_sb, 1)
                if live(s, L_BN):
                    for i in range(GR):
                        nc.vector.bn_aggr(mv[:, q % 2, OF_H, i, :], hst[:, i, :]).then_inc(hag, 1)
                if live(s, L_V):
                    for i in range(GR):
                        nc.vector.bn_aggr(mv[:, q % 2, OF_G, i, :], gst[:, i, :]).then_inc(gag, 1)
                if live(s, L_BN):
                    g, r = s - L_BN, (q - L_BN) % 4
                    dve.wait_ge(x_in[r], 4 * (g - r) + 16)
                    wait(dve, pag, 4 * g)
                    for i in range(GR):
                        nc.vector.bn_stats(pst[:, i, :], xg[:, r, i * SEG:(i + 2) * SEG]).then_inc(pbn, 1)
                    win = xg[:, r, :].rearrange("p (a n) -> p a n", n=SEG)
                    wait(dve, pmm_ok, 2 * g)
                    nc.vector.tensor_reduce(seg[:, 0, :], win, AX, ALU.max).then_inc(segs, 1)
                    wait(dve, pbn, 4 * (g + 1))
                    nc.vector.tensor_reduce(seg[:, 1, :], win, AX, ALU.min).then_inc(segs, 1)
                    for i in range(GR):
                        nc.vector.bn_aggr(mv[:, q % 2, OF_P, i, :], pst[:, i, :]).then_inc(pag, 1)
                    wait(dve, segs, 2 * (g + 1))
                    wait(dve, range_ok, g)
                    for i, op in enumerate((ALU.max, ALU.min)):
                        nc.vector.tensor_tensor(pmm[:, i, :], seg[:, i, 0:GR], seg[:, i, 1:GR + 1], op).then_inc(pmm_ok, 1)
                if live(s, L_TYPE):
                    g, q2 = s - L_TYPE, (q - L_TYPE) % 2
                    std = rs[:, q % 2, OF_P, :]
                    mk = mask[:, q2, 0:16].rearrange("p (a k) -> p a k", k=4)
                    dve.wait_ge(range_ok, g + 1)
                    wait(dve, tmk, 5 * g)
                    nc.vector.tensor_scalar(tm[:, 0, :], rng[:, q2, :], 0.5, None, ALU.is_lt).then_inc(tmk, 1)
                    wait(dve, rs_ok, s - L_BN)
                    wait(dve, m_ps, g - 1)
                    wait(dve, tmk, 5 * g + 1)
                    nc.vector.scalar_tensor_tensor(out=mk[:, :, 0], in0=std, scalar=0.1, in1=tm[:, 0, :],
                                                   op0=ALU.is_lt, op1=ALU.mult).then_inc(tmk, 1)
                    nc.vector.scalar_tensor_tensor(out=tm[:, 1, :], in0=std, scalar=0.3, in1=tm[:, 0, :],
                                                   op0=ALU.is_lt, op1=ALU.mult).then_inc(tmk, 1)
                    nc.vector.tensor_scalar(mk[:, :, 3], tm[:, 0, :], -1.0, 1.0, ALU.mult, ALU.add)
                if live(s, L_BN):
                    g, q2 = s - L_BN, (q - L_BN) % 2
                    wait(dve, pmm_ok, 2 * (g + 1))
                    nc.vector.tensor_tensor(rng[:, q2, :], pmm[:, 0, :], pmm[:, 1, :], ALU.subtract).then_inc(range_ok, 1)
                if live(s, L_TYPE):
                    g, q2 = s - L_TYPE, (q - L_TYPE) % 2
                    mk = mask[:, q2, 0:16].rearrange("p (a k) -> p a k", k=4)
                    wait(dve, tmk, 5 * g + 3)
                    nc.vector.tensor_tensor(mk[:, :, 1], tm[:, 1, :], mk[:, :, 0], ALU.subtract).then_inc(tmk, 1)
                    nc.vector.tensor_tensor(mk[:, :, 2], tm[:, 0, :], tm[:, 1, :], ALU.subtract).then_inc(tmk, 1)
            slots(dve, slot)
            dve.wait_ge(h1_ok, FG)
            nc.vector.tensor_copy(base[:], h1[:, (FG - 1) % 4, 0, :]).then_inc(base_ok, 1)

        @block.tensor
        def _(pe):
            pe.wait_ge(consts, 64 + 256)

            def slot(s, q):
                if live(s, L_T):
                    pe.wait_ge(x_in[q], 4 * (s - q) + 16)
                    wait(pe, pT_sb, s)
                    for i in range(GR):
                        ins = nc.tensor.transpose(p_pT[:, i * 128:(i + 1) * 128], xg[:, q, i * SEG:(i + 2) * SEG], ident[:])
                    ins.then_inc(pT_ps, 1)
                if live(s, L_H):
                    g, q2 = s - L_H, (q - L_H) % 2
                    wait(pe, z_0, 4 * (g - 1))
                    wait(pe, hbn, 4 * (g - 1))
                    wait(pe, pT_sb, g + 1)
                    for i in range(GR):
                        o = p_H[:, q2, i * 128:(i + 1) * 128]
                        nc.tensor.matmul(o, keep["ones"][0:1, :], brow[:], start=True, stop=False)
                        ins = nc.tensor.matmul(o, pT[:, q2, i, :], Wp[:], start=False, stop=True)
                    ins.then_inc(h_ps, 1)
                if live(s, L_MT):
                    g, q2 = s - L_MT, (q - L_MT) % 2
                    wait(pe, tmk, 5 * (g + 1))
                    wait(pe, m_sb, g)
                    nc.tensor.transpose(p_m[0:17, 0:128], mask[:, q2, :], ident[:]).then_inc(m_ps, 1)
                if live(s, L_XT):
                    g, q2 = s - L_XT, (q - L_XT) % 2
                    wait(pe, xn_ok, 4 * (g + 1))
                    wait(pe, xT_sb, g)
                    for i in range(GR):
                        ins = nc.tensor.transpose(p_xT[:, i * 128:(i + 1) * 128], xn[:, q2, i, :], ident[:])
                    ins.then_inc(xT_ps, 1)
                if live(s, L_ROW):
                    g, q2, r = s - L_ROW, (q - L_ROW) % 2, (q - L_ROW) % 4
                    wait(pe, m_sb, g + 1)
                    wait(pe, h1_ok, g)
                    pe.wait_ge(row_in[r], 4 * (g - r) + 16)
                    nc.tensor.matmul(p_T[:], mT[:, q2, :], rows[:, r, :], start=True, stop=True).then_inc(T_ps, 1)
                if live(s, L_U):
                    g, q2 = s - L_U, (q - L_U) % 2
                    wait(pe, xT_sb, g + 1)
                    wait(pe, u_sb, 2 * g)
                    for i in range(GR):
                        j = GR * ((q - L_U) % 4) + i
                        for c in range(2):
                            ins = nc.tensor.matmul(p_u[:, i, c, :], Bj[:, j, c, :], xnT[:, q2, i, :], start=True, stop=True)
                    ins.then_inc(u_ps, 1)
            slots(pe, slot)

    nc.all_engine_barrier()
    nc.clear_and_free_semaphores(used)
    nc.all_engine_barrier()


def between(nc, keep, scratch, pos):
    ident, ones, Bj, base, A, P = (keep[k] for k in ("ident", "ones", "Bj", "base", "A", "P"))
    NB = NP - FIRST
    T = NB // 128
    with ExitStack() as ctx:
        def sb(name, shape, dt=F32):
            return ctx.enter_context(nc.sbuf_tensor(name, shape, dt))

        def ps(name, shape):
            return ctx.enter_context(nc.psum_tensor(name, shape, F32))

        def sem(name):
            return keep["sems"].enter_context(nc.semaphore("b_" + name))

        cen = sb("cen", [128, T + 1, 128])
        raw = sb("raw", [128, T + 1, 128])
        bst = sb("bst", [128, T + 1, 6])
        bmv = sb("bmv", [128, T + 1, 2])
        cT = sb("cT", [128, T + 1, 128])
        twice = sb("twice", [128, 128])
        sq = sb("sq", [128, NB])
        var = sb("var", [128, 2, NB])
        R = sb("R", [128, T, 128])
        RT = sb("RT", [128, T, 128])
        p_c, p_v = ps("p_c", [128, 512]), ps("p_v", [128, 512])
        p_A = ps("p_A", [128, 2, 8, 128])
        p_P = ps("p_P", [128, 2, 512])
        names = "pos_in raw_ok st mv cen_ok c_ps c_sb tw sq_ok v_ps var_1 var_2 R_ok R_ps RT_ok RT_out A_ps A_sb P_ps P_sb".split()
        (pos_in, raw_ok, st, mv, cen_ok, c_ps, c_sb, tw, sq_ok, v_ps, var_1, var_2, R_ok, R_ps, RT_ok, RT_out,
         A_ps, A_sb, P_ps, P_sb) = (sem(n) for n in names)
        block = ctx.enter_context(nc.Block())

        @block.sync
        def _(sp):
            sp.dma_start(raw[:, 0:T, :], pos[FIRST:NP, :].rearrange("(t p) n -> p t n", p=128)).then_inc(pos_in, 16)
            sp.wait_ge(RT_ok, 1)
            sp.dma_start(scratch["rT"].rearrange("(t p) n -> p t n", p=128), RT[:]).then_inc(RT_out, 16)
            sp.wait_ge(RT_out, 16)

        @block.gpsimd
        def _(pool):
            nc.gpsimd.tensor_copy(raw[:, T, :], base[:]).then_inc(raw_ok, 1)
            pool.wait_ge(var_2, 1)
            nc.gpsimd.tensor_tensor(R[:].rearrange("p t n -> p (t n)"), var[:, 1, :], keep["halfneg"][:, 0:NB],
                                    ALU.pow).then_inc(R_ok, 1)

        @block.scalar
        def _(act):
            act.wait_ge(c_ps, 1)
            nc.scalar.activation(cT[:], p_c[:].rearrange("p (t n) -> p t n", n=128), ACT.Copy).then_inc(c_sb, 1)
            for q in range(4):
                act.wait_ge(A_ps, q + 1)
                nc.scalar.activation(A[:, 4 * q:4 * q + 4, :, :].rearrange("p a c n -> p (a c) n"), p_A[:, q % 2, :, :],
                                     ACT.Copy).then_inc(A_sb, 1)
            act.wait_ge(R_ps, 1)
            nc.scalar.activation(RT[:], p_c[:, 0:NB].rearrange("p (t n) -> p t n", n=128), ACT.Copy).then_inc(RT_ok, 1)

        @block.vector
        def _(dve):
            dve.wait_ge(pos_in, 16)
            dve.wait_ge(raw_ok, 1)
            for t in range(T + 1):
                nc.vector.bn_stats(bst[:, t, :], raw[:, t, :]).then_inc(st, 1)
            dve.wait_ge(st, T + 1)
            for t in range(T + 1):
                nc.vector.bn_aggr(bmv[:, t, :], bst[:, t, :]).then_inc(mv, 1)
            dve.wait_ge(mv, T + 1)
            for t in range(T + 1):
                nc.vector.tensor_scalar(cen[:, t, :], raw[:, t, :], bmv[:, t, 0:1], None, ALU.subtract).then_inc(cen_ok, 1)
            dve.wait_ge(c_sb, 1)
            nc.vector.tensor_scalar(twice[:], cT[:, T, :], 2.0, None, ALU.mult).then_inc(tw, 1)
            pT = cT[:, 0:T, :].rearrange("p t n -> p (t n)")
            nc.vector.tensor_tensor(sq[:], pT, pT, ALU.mult).then_inc(sq_ok, 1)
            dve.wait_ge(v_ps, 1)
            nc.vector.tensor_scalar(var[:, 0, :], p_v[:, 0:NB], 1.0 / D, bmv[:, T, 1:2], ALU.mult, ALU.add).then_inc(var_1, 1)
            dve.wait_ge(var_1, 1)
            nc.vector.tensor_scalar(var[:, 1, :], var[:, 0, :], 0.0, EPS, ALU.max, ALU.add).then_inc(var_2, 1)
            dve.wait_ge(P_ps, 1)
            view = P[:].rearrange("p (k j) c -> p j c k", j=CH)
            for h in range(2):
                nc.vector.tensor_copy(view[:, 8 * h:8 * h + 8, :, :],
                                      p_P[:, h, 0:8 * 2 * (NB // CH)].rearrange("p (j c k) -> p j c k", j=8, c=2)).then_inc(P_sb, 1)

        @block.tensor
        def _(pe):
            pe.wait_ge(cen_ok, T + 1)
            for t in range(T + 1):
                ins = nc.tensor.transpose(p_c[:, t * 128:(t + 1) * 128], cen[:, t, :], ident[:])
            ins.then_inc(c_ps, 1)
            pe.wait_ge(c_sb, 1)
            pe.wait_ge(tw, 1)
            pT = cT[:, 0:T, :].rearrange("p t n -> p (t n)")
            nc.tensor.matmul(p_v[:, 0:NB], twice[:], pT, start=True, stop=False)
            pe.wait_ge(sq_ok, 1)
            nc.tensor.matmul(p_v[:, 0:NB], ones[:], sq[:], start=False, stop=True).then_inc(v_ps, 1)
            for q in range(4):
                wait(pe, A_sb, q - 1)
                for i in range(4):
                    for c in range(2):
                        ins = nc.tensor.matmul(p_A[:, q % 2, 2 * i + c, :], Bj[:, 4 * q + i, c, :], cT[:, T, :],
                                               start=True, stop=True)
                ins.then_inc(A_ps, 1)
            K = NB // CH
            for j in range(CH):
                for c in range(2):
                    o = ((j % 8) * 2 + c) * K
                    ins = nc.tensor.matmul(p_P[:, j // 8, o:o + K], Bj[:, j, c, :],
                                           pT.rearrange("p (k j) -> p j k", j=CH)[:, j, :], start=True, stop=True)
            ins.then_inc(P_ps, 1)
            pe.wait_ge(R_ok, 1)
            for t in range(T):
                ins = nc.tensor.transpose(p_c[:, t * 128:(t + 1) * 128], R[:, t, :], ident[:])
            ins.then_inc(R_ps, 1)


def scan(nc, keep, scratch, pos, gate_w, sw1, sw3, sw2, out):
    ident, turn, decay, base, carry, g2, top, halfneg, A, P, colC, colS = (keep[k] for k in (
        "ident", "turn", "decay", "base", "carry", "g2", "top", "halfneg", "A", "P", "colC", "colS"))
    L_Y, L_H2, L_X3, L_FF, L_HS, L_OUT, L_ST = 1, 2, 3, 4, 5, 6, 8
    with ExitStack() as ctx:
        def sb(name, shape, dt=F32):
            return ctx.enter_context(nc.sbuf_tensor(name, shape, dt))

        def ps(name, shape):
            return ctx.enter_context(nc.psum_tensor(name, shape, F32))

        def sem(name):
            return keep["sems"].enter_context(nc.semaphore("m_" + name))

        gT = sb("gT", [128, E])
        w13 = sb("w13", [128, 2, 128])
        w2s = sb("w2s", [128, 128])
        gnat = sb("gnat", [E, 128])
        ub = sb("ub", [128, 4, GR, 2, 128])
        h1 = sb("h1b", [128, 4, GR, 128])
        posb = sb("posb", [128, 4, GR, 128])
        Rb = sb("Rb", [128, 4, GR, 128])
        ap_ = sb("ap_", [128, 2, GR * 2, 128])
        tre = sb("tre", [128, 2, 128])
        h2 = sb("h2", [128, 4, GR, 128])
        st3 = sb("st3", [128, GR, 6])
        mv3 = sb("mv3", [128, 2, GR, 2])
        t3 = sb("t3", [128, 2, 2, GR])
        r3 = sb("r3", [128, 2, 2, GR])
        x3 = sb("x3", [128, 4, GR, ROW])
        xTs = sb("xTs", [128, 2, GR * 128])
        sa = sb("sa", [128, 2, GR * 128])
        hs = sb("hs", [128, 2, GR * 128])
        mx = sb("mx", [128, 4, GR, 8])
        ix = sb("ix", [128, 4, GR, 8], U32)
        ob = sb("ob", [128, 2, GR * 128])
        zr = sb("zr", [128, 2 * ROW])
        none = sb("none", [128, 2, NP - STEPS])
        p_y = ps("p_y", [128, 2, 512])
        p_xT, p_a, p_z, p_s = (ps(n, [128, 512]) for n in ("p_xT3", "p_a", "p_z", "p_s"))
        p_l = ps("p_l", [128, 2, 512])

        consts, prep, gt_ps, gt_sb, zeros_out = sem("consts"), sem("prep"), sem("gt_ps"), sem("gt_sb"), sem("zeros_out")
        u_in, h1_in, pos_in, R_in, x3_out = ([sem(f"{n}{i}") for i in range(4)] for n in ("u_in", "h1_in", "pos_in", "R_in", "x3_out"))
        o_out = [sem(f"o_out{i}") for i in range(2)]
        names = ("ap_ok ap_act u_pool h1_pool rec turned y_ps h2_ok bn ag r3a r3b r3c r3d x3_ok xT_ps xT_sb lg_ps a_ps z_ps "
                 "silu_ok hs_ok sh_ps out_ok mx_ok ix_ok aug").split()
        (ap_ok, ap_act, u_pool, h1_pool, rec, turned, y_ps, h2_ok, bn, ag, r3a, r3b, r3c, r3d, x3_ok, xT_ps, xT_sb, lg_ps, a_ps,
         z_ps, silu_ok, hs_ok, sh_ps, out_ok, mx_ok, ix_ok, aug) = (sem(n) for n in names)
        block = ctx.enter_context(nc.Block())
        GA = FIRST // GR
        ACT_STEPS = 3

        def slots(eng, slot, lag):
            for s in range(8):
                slot(s, s % 4, 0)
            with eng.Fori(2, NC_A) as c:
                for q in range(4):
                    slot(4 * c + q, q, 0)
            for s in range(GA, GA + 4):
                slot(s, s % 4, 1)
            with eng.Fori(NC_A + 1, NC - 1) as c:
                for q in range(4):
                    slot(4 * c + q, q, 1)
            for s in range(NG - 4, NG + lag):
                slot(s, s % 4, 1)

        def live(s, lag):
            return not isinstance(s, int) or 0 <= s - lag < NG

        @block.sync
        def _(sp):
            sp.dma_start(gnat[:], gate_w).then_inc(consts, 16)
            sp.dma_start(w13[:, 0, :], sw1).then_inc(consts, 16)
            sp.dma_start(w13[:, 1, :], sw3).then_inc(consts, 16)
            sp.dma_start(w2s[:], sw2).then_inc(consts, 16)
            sp.wait_ge(prep, 2)
            sp.dma_start(scratch["x3"][B * NP:ROWS, :].rearrange("(p a) n -> p (a n)", p=128), zr[:]).then_inc(zeros_out, 16)
            sp.dma_start(out[B * NP:ROWS, :].rearrange("(p a) n -> p (a n)", p=128), zr[:, 0:2 * D]).then_inc(zeros_out, 16)

            def slot(s, q, region):
                if region == 0 and live(s, 0):
                    wait(sp, rec, 4 * (s - 3))
                    sp.dma_start(ub[:, q, :, :, :].rearrange("p a c n -> p (a c n)"),
                                 scratch["u"][:, bass.ds(s, 1), :].rearrange("p a n -> p (a n)")).then_inc(u_in[q], 16)
                    wait(sp, h2_ok, s - 3)
                    sp.dma_start(h1[:, q, :, :].rearrange("p a n -> p (a n)"),
                                 scratch["h1"][:, bass.ds(s, 1), :].rearrange("p a n -> p (a n)")).then_inc(h1_in[q], 16)
                elif live(s, 0):
                    wait(sp, rec, 4 * (s - 3))
                    sp.dma_start(Rb[:, q, :, :].rearrange("p a n -> p (a n)"),
                                 scratch["rT"].rearrange("n b -> (n b)")[bass.ds((s - GA) * (GR * 128), GR * 128)]
                                 .partition_broadcast(128)).then_inc(R_in[q], 16)
                    wait(sp, h2_ok, s - 3)
                    sp.dma_start(posb[:, q, :, :].rearrange("p a n -> p (a n)"),
                                 pos.rearrange("n d -> (n d)")[bass.ds(s * (GR * 128), GR * 128)]
                                 .partition_broadcast(128)).then_inc(pos_in[q], 16)
                if live(s, L_ST):
                    g = s - L_ST
                    sp.wait_ge(aug, 3 * (g + 1))
                    sp.dma_start(scratch["x3"][0:B * NP, :].rearrange("(b n) r -> b (n r)", b=128)[:, bass.ds(g * (GR * ROW), GR * ROW)],
                                 x3[:, (q - L_ST) % 4, :, :].rearrange("p a n -> p (a n)")).then_inc(x3_out[(q - L_ST) % 4], 16)
                    sp.wait_ge(out_ok, g + 1)
                    sp.dma_start(out[0:B * NP, :].rearrange("(b n) r -> b (n r)", b=128)[:, bass.ds(g * (GR * D), GR * D)],
                                 ob[:, (q - L_ST) % 2, :]).then_inc(o_out[(q - L_ST) % 2], 16)
            slots(sp, slot, L_ST)
            sp.wait_ge(zeros_out, 32)
            for r in range(4):
                sp.wait_ge(x3_out[r], 4 * NG)
            for r in range(2):
                sp.wait_ge(o_out[r], 8 * NG)

        @block.gpsimd
        def _(pool):
            nc.gpsimd.memset(x3[:], 0.0).then_inc(prep, 1)
            nc.gpsimd.memset(zr[:], 0.0).then_inc(prep, 1)
            nc.gpsimd.memset(none[:], 99.0).then_inc(prep, 1)
            pool.wait_ge(prep, 3)

            def scan_input(s, q):
                n = s - GA
                wait(pool, u_pool, n - 1)
                k = GR - ACT_STEPS
                cols = P[:, bass.ds(n * GR + ACT_STEPS, k), :].rearrange("p a c -> p (a c)").unsqueeze(2).to_broadcast([128, 2 * k, 128])
                nc.gpsimd.tensor_tensor(ap_[:, q % 2, 2 * ACT_STEPS:, :], A[:, GR * q + ACT_STEPS:GR * (q + 1), :, :]
                                        .rearrange("p a c n -> p (a c) n"), cols, ALU.add).then_inc(ap_ok, 1)
                pool.wait_ge(R_in[q], 4 * (n - q) + 16)
                wait(pool, rec, 4 * (s - 3))
                wait(pool, ap_ok, n + 1)
                wait(pool, ap_act, 2 * ACT_STEPS * (n + 1))
                nc.gpsimd.tensor_tensor(ub[:, q, :, :, :], ap_[:, q % 2, :, :].rearrange("p (a c) n -> p a c n", c=2),
                                        Rb[:, q, :, :].unsqueeze(2).to_broadcast([128, GR, 2, 128]),
                                        ALU.mult).then_inc(u_pool, 1)
                pool.wait_ge(pos_in[q], 4 * (n - q) + 16)
                wait(pool, h2_ok, s - 3)
                nc.gpsimd.tensor_tensor(h1[:, q, :, :], posb[:, q, :, :],
                                        base[:].unsqueeze(1).to_broadcast([128, GR, 128]), ALU.add).then_inc(h1_pool, 1)

            def slot(s, q, region):
                if isinstance(s, int) and s == GA:
                    scan_input(s, q)
                if live(s, L_X3):
                    g, q2 = s - L_X3, (q - L_X3) % 2
                    pool.wait_ge(ag, 4 * (g + 1))
                    nc.gpsimd.tensor_tensor(t3[:, q2, 0, :], mv3[:, q2, :, 1], keep["eps"][:], ALU.add).then_inc(r3a, 1)
                    nc.gpsimd.tensor_tensor(t3[:, q2, 1, :], mv3[:, q2, :, 0], keep["minus"][:], ALU.mult).then_inc(r3b, 1)
                    pool.wait_ge(r3a, g + 1)
                    wait(pool, x3_ok, 4 * (g - 1))
                    nc.gpsimd.tensor_tensor(r3[:, q2, 0, :], t3[:, q2, 0, :], halfneg[:, 0:GR], ALU.pow).then_inc(r3c, 1)
                    pool.wait_ge(r3b, g + 1)
                    pool.wait_ge(r3c, g + 1)
                    nc.gpsimd.tensor_tensor(r3[:, q2, 1, :], t3[:, q2, 1, :], r3[:, q2, 0, :], ALU.mult).then_inc(r3d, 1)
                if region == 1 and live(s + 1, 0):
                    scan_input(s + 1, (q + 1) % 4)
            slots(pool, slot, L_X3)

        @block.scalar
        def _(act):
            act.wait_ge(gt_ps, 1)
            nc.scalar.activation(gT[:], p_l[:, 0, 0:E], ACT.Copy).then_inc(gt_sb, 1)
            act.wait_ge(prep, 1)

            def add_positions(s, q):
                n = s - GA
                wait(act, u_pool, n - 1)
                for i in range(ACT_STEPS):
                    for c in range(2):
                        nc.scalar.activation(ap_[:, q % 2, 2 * i + c, :], A[:, GR * q + i, c, :], ACT.Identity,
                                             bias=P[:, bass.ds(n * GR + i, 1), c]).then_inc(ap_act, 1)

            def slot(s, q, region):
                if isinstance(s, int) and s == GA:
                    add_positions(s, q)
                    add_positions(s + 1, q + 1)
                if live(s, L_OUT):
                    g, r = s - L_OUT, (q - L_OUT) % 4
                    act.wait_ge(ix_ok, 4 * (g + 1))
                    nc.scalar.activation(x3[:, r, :, D:D + 2], mx[:, r, :, 0:2], ACT.Copy).then_inc(aug, 1)
                    nc.scalar.activation(x3[:, r, :, D + 2:D + 3], ix[:, r, :, 0:1], ACT.Copy).then_inc(aug, 1)
                    nc.scalar.activation(top[:, :, bass.ds(g * GR, GR)], ix[:, r, :, 0:2].rearrange("p a k -> p k a"),
                                         ACT.Copy).then_inc(aug, 1)
                if live(s, L_X3):
                    g, q2, r = s - L_X3, (q - L_X3) % 2, (q - L_X3) % 4
                    act.wait_ge(r3d, g + 1)
                    if not isinstance(s, int) or g >= 4:
                        act.wait_ge(x3_out[r], 4 * (g - r))
                    for i in range(GR):
                        nc.scalar.activation(x3[:, r, i, 0:D], h2[:, r, i, :], ACT.Identity,
                                             bias=r3[:, q2, 1, i:i + 1], scale=r3[:, q2, 0, i:i + 1]).then_inc(x3_ok, 1)
                if region == 1 and live(s + 2, 0):
                    add_positions(s + 2, (q + 2) % 4)
                if live(s, L_FF):
                    g, q2 = s - L_FF, (q - L_FF) % 2
                    act.wait_ge(a_ps, g + 1)
                    wait(act, hs_ok, g - 1)
                    nc.scalar.activation(sa[:, q2, :], p_a[:], ACT.Silu).then_inc(silu_ok, 1)
                if live(s, L_X3):
                    g, q2 = s - L_X3, (q - L_X3) % 2
                    act.wait_ge(xT_ps, g + 1)
                    wait(act, z_ps, g - 1)
                    nc.scalar.activation(xTs[:, q2, :], p_xT[:], ACT.Copy).then_inc(xT_sb, 1)
            slots(act, slot, L_OUT)
            act.wait_ge(aug, 3 * NG)
            nc.scalar.activation(top[:, :, STEPS:NP], none[:], ACT.Copy)

        @block.vector
        def _(dve):

            def slot(s, q, region):
                if live(s, L_OUT):
                    g, r, o = s - L_OUT, (q - L_OUT) % 4, (q - L_OUT) % 2
                    dve.wait_ge(sh_ps, g + 1)
                    if not isinstance(s, int) or g >= 2:
                        dve.wait_ge(o_out[o], 8 * (g - o))
                    nc.vector.tensor_tensor(ob[:, o, :], h2[:, r, :, :].rearrange("p a n -> p (a n)"), p_s[:], ALU.add).then_inc(out_ok, 1)
                if live(s, L_HS):
                    g, q2 = s - L_HS, (q - L_HS) % 2
                    dve.wait_ge(silu_ok, g + 1)
                    dve.wait_ge(z_ps, g + 1)
                    dve.wait_ge(lg_ps, g + 1)
                    wait(dve, aug, 3 * (g - 3))
                    wait(dve, sh_ps, g - 1)
                    nc.vector.tensor_tensor(hs[:, q2, :], sa[:, q2, :], p_z[:], ALU.mult).then_inc(hs_ok, 1)
                if live(s, L_H2):
                    g, q2, r = s - L_H2, (q - L_H2) % 2, (q - L_H2) % 4
                    dve.wait_ge(y_ps, g + 1)
                    wait(dve, out_ok, g - 3)
                    if region == 0 or isinstance(s, int) and g < GA:
                        dve.wait_ge(h1_in[r], 4 * (g - r) + 16)
                    else:
                        dve.wait_ge(h1_pool, g + 1 - GA)
                    nc.vector.tensor_tensor(h2[:, r, :, :], p_y[:, q2, :].rearrange("p (a n) -> p a n", a=GR),
                                            h1[:, r, :, :], ALU.add).then_inc(h2_ok, 1)
                if live(s, 0) and q == 0 and not (isinstance(s, int) and s == 0):
                    dve.wait_ge(rec, 4 * s)
                    k = s - 4
                    last = g2[:, 2 * GR - 1, :, :]
                    nc.vector.tensor_scalar(tre[:, 0, :], last[:, 1, :], colS[:, CH:CH + 1], None, ALU.mult).then_inc(turned, 1)
                    nc.vector.tensor_scalar(tre[:, 1, :], last[:, 0, :], colS[:, CH:CH + 1], None, ALU.mult).then_inc(turned, 1)
                    dve.wait_ge(turned, k + 1)
                    nc.vector.scalar_tensor_tensor(out=carry[:, 0, :], in0=last[:, 0, :], scalar=colC[:, CH:CH + 1],
                                                   in1=tre[:, 0, :], op0=ALU.mult, op1=ALU.subtract).then_inc(turned, 1)
                    dve.wait_ge(turned, k + 2)
                    nc.vector.scalar_tensor_tensor(out=carry[:, 1, :], in0=last[:, 1, :], scalar=colC[:, CH:CH + 1],
                                                   in1=tre[:, 1, :], op0=ALU.mult, op1=ALU.add).then_inc(turned, 1)
                g5, half, r5 = s - L_HS, (q - L_HS) % 2, (q - L_HS) % 4
                g2_, q2, r2 = s - L_H2, (q - L_H2) % 2, (q - L_H2) % 4
                for i in range(GR):
                    lg = p_l[:, half, i * E:(i + 1) * E]
                    if live(s, L_HS):
                        nc.vector.max(mx[:, r5, i, :], lg).then_inc(mx_ok, 1)
                    if live(s, L_H2):
                        if i == 0:
                            dve.wait_ge(h2_ok, g2_ + 1)
                            wait(dve, r3d, g2_ - 1)
                        else:
                            wait(dve, bn, 4 * g2_ + i)
                    if live(s, L_HS):
                        dve.wait_ge(mx_ok, 4 * g5 + i + 1)
                    if live(s, L_H2):
                        nc.vector.bn_stats(st3[:, i, :], h2[:, r2, i, :]).then_inc(bn, 1)
                        if i:
                            nc.vector.bn_aggr(mv3[:, q2, i - 1, :], st3[:, i - 1, :]).then_inc(ag, 1)
                    if live(s, L_HS):
                        nc.vector.max_index(ix[:, r5, i, :], mx[:, r5, i, :], lg).then_inc(ix_ok, 1)
                    if i == GR - 1 and live(s, L_H2):
                        dve.wait_ge(bn, 4 * g2_ + GR)
                    if live(s, 0):
                        if i == 0:
                            if region == 0:
                                dve.wait_ge(u_in[q], 4 * (s - q) + 16)
                            else:
                                dve.wait_ge(u_pool, s + 1 - GA)
                            wait(dve, y_ps, s - 1)
                        wait(dve, rec, 4 * s + i)
                        if q == 0 and i == 0 and not (isinstance(s, int) and s == 0):
                            dve.wait_ge(turned, s)
                        k = (q % 2) * GR + i
                        prev = carry[:] if q == 0 and i == 0 else g2[:, (k - 1) % (2 * GR), :, :]
                        nc.vector.scalar_tensor_tensor(out=g2[:, k, :, :], in0=prev, scalar=decay[:, 0:1],
                                                       in1=ub[:, q, i, :, :], op0=ALU.mult, op1=ALU.add).then_inc(rec, 1)
                if live(s, L_H2):
                    nc.vector.bn_aggr(mv3[:, q2, GR - 1, :], st3[:, GR - 1, :]).then_inc(ag, 1)
            slots(dve, slot, L_OUT)

        @block.tensor
        def _(pe):
            pe.wait_ge(consts, 64)
            nc.tensor.transpose(p_l[:, 0, 0:E], gnat[:], ident[0:E, 0:E]).then_inc(gt_ps, 1)
            pe.wait_ge(gt_sb, 1)

            def slot(s, q, region):
                if live(s, L_Y):
                    g, q2 = s - L_Y, (q - L_Y) % 2
                    pe.wait_ge(rec, 4 * (g + 1))
                    wait(pe, h2_ok, g - 1)
                    for i in range(GR):
                        j, o = GR * ((q - L_Y) % 4) + i, p_y[:, q2, i * 128:(i + 1) * 128]
                        nc.tensor.matmul(o, g2[:, q2 * GR + i, 0, :], turn[:, j, 0, :], start=True, stop=False)
                        ins = nc.tensor.matmul(o, g2[:, q2 * GR + i, 1, :], turn[:, j, 1, :], start=False, stop=True)
                    ins.then_inc(y_ps, 1)
                if live(s, L_FF):
                    g, q2 = s - L_FF, (q - L_FF) % 2
                    pe.wait_ge(xT_sb, g + 1)
                    wait(pe, silu_ok, g)
                    nc.tensor.matmul(p_a[:], w13[:, 0, :], xTs[:, q2, :], start=True, stop=True).then_inc(a_ps, 1)
                    wait(pe, ix_ok, 4 * (g - 1))
                    for i in range(GR):
                        ins = nc.tensor.matmul(p_l[:, q2, i * E:(i + 1) * E], xTs[:, q2, i * 128:(i + 1) * 128],
                                               gT[:], start=True, stop=True)
                    ins.then_inc(lg_ps, 1)
                    wait(pe, hs_ok, g)
                    nc.tensor.matmul(p_z[:], w13[:, 1, :], xTs[:, q2, :], start=True, stop=True).then_inc(z_ps, 1)
                if live(s, L_HS):
                    g, q2 = s - L_HS, (q - L_HS) % 2
                    pe.wait_ge(hs_ok, g + 1)
                    wait(pe, out_ok, g)
                    for i in range(GR):
                        ins = nc.tensor.matmul(p_s[:, i * 128:(i + 1) * 128], hs[:, q2, i * 128:(i + 1) * 128], w2s[:],
                                               start=True, stop=True)
                    ins.then_inc(sh_ps, 1)
                if live(s, L_X3):
                    g, r = s - L_X3, (q - L_X3) % 4
                    pe.wait_ge(x3_ok, 4 * (g + 1))
                    wait(pe, xT_sb, g)
                    for i in range(GR):
                        ins = nc.tensor.transpose(p_xT[:, i * 128:(i + 1) * 128], x3[:, r, i, 0:D], ident[:])
                    ins.then_inc(xT_ps, 1)
            slots(pe, slot, L_ST)


def routed(nc, keep, scratch, w13, w2, out):
    ident, top = keep["ident"], keep["top"]
    T = CAP // 128
    L_CNT, L_EXC, L_SEL, L_IDX = 0, 1, 2, 3
    L_W, L_T, L_A, L_H, L_Y, L_YS, L_SC = 4, 5, 6, 7, 8, 9, 10
    U = 8
    with ExitStack() as ctx:
        def sb(name, shape, dt=F32):
            return ctx.enter_context(nc.sbuf_tensor("r_" + name, shape, dt))

        def ps(name, shape):
            return ctx.enter_context(nc.psum_tensor("r_" + name, shape, F32))

        def sem(name):
            return keep["sems"].enter_context(nc.semaphore("r_" + name))

        cnt = sb("cnt", [128, 4, NP], F16)
        is0 = sb("is0", [128, 2, NP], BF16)
        is1 = sb("is1", [128, 2, NP], BF16)
        off = sb("off", [128, NP])
        ecol = sb("ecol", [128, E])
        slot_row = sb("slot_row", [128, CAP])
        slot_col = sb("slot_col", [128, T])
        slot_half = sb("slot_half", [128, T])
        empty_row = sb("empty_row", [128, T])
        necol = sb("necol", [128, E])
        before = sb("before", [128, 128], F16)
        upto = sb("upto", [128, 128], F16)
        one_on = sb("one_on", [128, 1])
        one_b = sb("one_b", [128, 1])
        rowp1 = sb("rowp1", [128, 1], F16)
        ei = sb("ei", [128, 4, 2])
        exc16 = sb("exc16", [128, 4], F16)
        past = sb("past", [128, CAP], F16)
        S = sb("S", [128, 2, CAP], F16)
        le = sb("le", [128, NP])
        sg_junk = sb("sg_junk", [128, NP])
        nstar = sb("nstar", [128, 2, T])
        signs = sb("signs", [128, 2])
        flat = sb("flat", [128, T])
        vac = sb("vac", [128, T])
        ridx = sb("ridx", [128, U, T], U32)
        xg = sb("xg", [128, U, T, ROW])
        sv = sb("sv", [128, 2, T, 2])
        wt = sb("wt", [128, 5, T])
        wgt = sb("wgt", [128, 4, T])
        xT = sb("xT", [128, 2, CAP])
        wr = sb("wr", [128, 4, 2 * HID])
        w2r = sb("w2r", [HID, 4, D])
        sg = sb("sg", [HID, 2, CAP])
        asg = sb("asg", [HID, CAP])
        hh = sb("hh", [HID, 2, CAP])
        ys = sb("ys", [128, 2, T, D])
        p_n = [ps(f"p_n{t}", [128, 512]) for t in range(T)]
        p_b, p_e, p_x, p_y = (ps(n, [128, 512]) for n in ("p_b", "p_e", "p_x", "p_y"))
        p_az = ps("p_az", [128, 2, 2, CAP])

        w_in = [sem(f"w_in{i}") for i in range(4)]
        gathered = [sem(f"gathered{i}") for i in range(U)]
        names = ("iotas m0_ok off_ok m1_ok c_ok exc_ps exc_ok past_ok S_ok sel_ps cnt0 cnt1 n1 fl vc ridx_ok T_ps T_sb az_ps "
                 "sv_ok w_ok sg_ok asg_ok h_ok y_ps ys_ok added wk passed").split()
        (iotas, m0_ok, off_ok, m1_ok, c_ok, exc_ps, exc_ok, past_ok, S_ok, sel_ps, cnt0, cnt1, n1, fl, vc, ridx_ok, T_ps, T_sb,
         az_ps, sv_ok, w_ok, sg_ok, asg_ok, h_ok, y_ps, ys_ok, added, wk, passed) = (sem(n) for n in names)
        block = ctx.enter_context(nc.Block())

        def slots(eng, slot):
            for s in range(2 * U):
                slot(s, s % U)
            with eng.Fori(2, E // U) as c:
                for q in range(U):
                    slot(U * c + q, q)
            for s in range(E, E + L_SC):
                slot(s, s % U)

        def live(s, lag):
            return not isinstance(s, int) or 0 <= s - lag < E

        @block.sync
        def _(sp):
            def slot(s, q):
                if live(s, L_W):
                    g, r = s - L_W, (q - L_W) % 4
                    wait(sp, az_ps, g - 3)
                    sp.dma_start(wr[:, r, :], w13[bass.ds(g, 1), :, :].rearrange("a p n -> (a p) n")).then_inc(w_in[r], 16)
                    wait(sp, y_ps, g - 3)
                    sp.dma_start(w2r[:, r, :], w2[bass.ds(g, 1), :, :].rearrange("a p n -> (a p) n")).then_inc(w_in[r], 16)
            slots(sp, slot)

        @block.gpsimd
        def _(pool):
            nc.gpsimd.iota(ecol[:], [[1, E]], base=0, channel_multiplier=0, allow_small_or_imprecise_dtypes=True).then_inc(iotas, 1)
            nc.gpsimd.iota(slot_row[:], [[1, CAP]], base=0, channel_multiplier=0, allow_small_or_imprecise_dtypes=True).then_inc(iotas, 1)
            nc.gpsimd.iota(slot_col[:], [[128, T]], base=0, channel_multiplier=1, allow_small_or_imprecise_dtypes=True).then_inc(iotas, 1)
            nc.gpsimd.iota(empty_row[:], [[128, T]], base=B * NP, channel_multiplier=1, allow_small_or_imprecise_dtypes=True).then_inc(iotas, 1)
            nc.gpsimd.iota(one_on[:], [[0, 1]], base=1, channel_multiplier=1, allow_small_or_imprecise_dtypes=True).then_inc(iotas, 1)
            nc.gpsimd.iota(necol[:], [[-1, E]], base=0, channel_multiplier=0, allow_small_or_imprecise_dtypes=True).then_inc(iotas, 1)
            nc.gpsimd.memset(before[:], 1.0).then_inc(iotas, 1)
            nc.gpsimd.memset(upto[:], 1.0).then_inc(iotas, 1)
            nc.gpsimd.memset(one_b[:], 1.0).then_inc(iotas, 1)
            pool.wait_ge(iotas, 9)
            nc.gpsimd.tensor_copy(rowp1[:], one_on[:]).then_inc(iotas, 1)
            nc.gpsimd.tensor_scalar(slot_half[:], slot_col[:], 0.5, None, ALU.add).then_inc(iotas, 1)
            nc.gpsimd.affine_select(out=before[:], in_=before[:], compare_op=ALU.is_gt, fill=0.0, base=0,
                                    pattern=[[1, 128]], channel_multiplier=-1).then_inc(iotas, 1)
            nc.gpsimd.affine_select(out=upto[:], in_=upto[:], compare_op=ALU.is_ge, fill=0.0, base=0,
                                    pattern=[[1, 128]], channel_multiplier=-1).then_inc(iotas, 1)

            last_row = pool.to_reg(ROWS - 1)

            def slot(s, q):
                if live(s, L_SC):
                    g, r = s - L_SC, (q - L_SC) % U
                    pool.wait_ge(ys_ok, T * (g + 1))
                    wait(pool, added, 16 * T * g)
                    pool.sem_inc(passed, 1)
                    for t in range(T):
                        nc.gpsimd.indirect_dma_start(out, bass.IndirectOffsetOnAxis(ap=ridx[:, r, t:t + 1], axis=0),
                                                     ys[:, r % 2, t, :], None, bounds_check=last_row, oob_is_err=True,
                                                     compute_op=ALU.add).then_inc(added, 16)
                if live(s, L_IDX):
                    g, r = s - L_IDX, (q - L_IDX) % U
                    wait(pool, w_ok, g - U + 1)
                    pool.wait_ge(ridx_ok, g + 1)
                    pool.sem_inc(passed, 1)
                    for t in range(T):
                        nc.gpsimd.indirect_dma_start(xg[:, r, t, :], None, scratch["x3"],
                                                     bass.IndirectOffsetOnAxis(ap=ridx[:, r, t:t + 1], axis=0),
                                                     bounds_check=last_row, oob_is_err=True).then_inc(gathered[r], 16)
            slots(pool, slot)
            pool.wait_ge(added, 16 * T * E)

        @block.scalar
        def _(act):
            act.wait_ge(iotas, 13)

            def slot(s, q):
                if live(s, L_IDX):
                    g = s - L_IDX
                    act.wait_ge(sel_ps, g + 1)
                    wait(act, n1, g - 1)
                    nc.scalar.activation(sg_junk[:], p_n[1][:], ACT.Sign, bias=slot_half[:, 1:2], scale=-1.0,
                                         accum_out=signs[:, (q - L_IDX) % 2:(q - L_IDX) % 2 + 1]).then_inc(cnt1, 1)
                if live(s, L_H):
                    g, q2 = s - L_H, (q - L_H) % 2
                    act.wait_ge(az_ps, g + 1)
                    wait(act, asg_ok, g - 1)
                    nc.scalar.activation(sg[:, q2, :], p_az[0:HID, q2, 0, :], ACT.Sigmoid).then_inc(sg_ok, 1)
                if live(s, L_YS):
                    g, q2 = s - L_YS, (q - L_YS) % 2
                    act.wait_ge(y_ps, g + 1)
                    act.wait_ge(w_ok, g + 1)
                    wait(act, added, 16 * T * (g - 1))
                    for t in range(T):
                        nc.scalar.activation(ys[:, q2, t, :], p_y[:, t * D:(t + 1) * D], ACT.Identity,
                                             scale=wgt[:, (q - L_YS) % 4, t:t + 1]).then_inc(ys_ok, 1)
                if live(s, L_T):
                    g, q2, r = s - L_T, (q - L_T) % 2, (q - L_T) % U
                    act.wait_ge(T_ps, g + 1)
                    wait(act, az_ps, g - 1)
                    nc.scalar.activation(xT[:, q2, :], p_x[:, 0:CAP], ACT.Copy).then_inc(T_sb, 1)
                    act.wait_ge(gathered[r], 4 * (g - r) + 16 * T)
                    wait(act, w_ok, g - 1)
                    nc.scalar.activation(sv[:, q2, :, :], xg[:, r, :, D:D + 2], ACT.Sigmoid).then_inc(sv_ok, 1)
                if live(s, L_CNT):
                    wait(act, m1_ok, s)
                    nc.scalar.activation(off[:], top[:, 1, :], ACT.Square, bias=necol[:, bass.ds(s, 1)], scale=1.0).then_inc(off_ok, 1)
                    wait(act, off_ok, s + 1)
                    wait(act, c_ok, s - 1)
                    nc.scalar.activation(is1[:, q % 2, :], off[:], ACT.Relu, bias=one_b[:], scale=-1.0).then_inc(m1_ok, 1)
            slots(act, slot)

        @block.vector
        def _(dve):
            dve.wait_ge(iotas, 13)
            def slot(s, q):
                if live(s, L_IDX):
                    g, q2, r = s - L_IDX, (q - L_IDX) % 2, (q - L_IDX) % U
                    dve.wait_ge(sel_ps, g + 1)
                    wait(dve, fl, g - 1)
                    wait(dve, cnt0, g)
                    nc.vector.tensor_scalar(le[:], p_n[0][:], slot_col[:, 0:1], 0.0, ALU.is_le, ALU.add,
                                            accum_out=nstar[:, q2, 0:1]).then_inc(cnt0, 1)
                    wait(dve, ridx_ok, g)
                    nc.vector.scalar_tensor_tensor(out=vac[:], in0=p_b[:, 0:T], scalar=0.0, in1=empty_row[:],
                                                   op0=ALU.is_equal, op1=ALU.mult).then_inc(vc, 1)
                if live(s, L_CNT):
                    wait(dve, c_ok, s - 1)
                    nc.vector.tensor_scalar(is0[:, q % 2, :], top[:, 0, :], ecol[:, bass.ds(s, 1)], None, ALU.is_equal).then_inc(m0_ok, 1)
                if live(s, L_H):
                    g, q2 = s - L_H, (q - L_H) % 2
                    wait(dve, sg_ok, g + 1)
                    wait(dve, h_ok, g)
                    nc.vector.tensor_tensor(asg[:], sg[:, q2, :], p_az[0:HID, q2, 0, :], ALU.mult).then_inc(asg_ok, 1)
                    wait(dve, asg_ok, g + 1)
                    wait(dve, y_ps, g - 1)
                    nc.vector.tensor_tensor(hh[:, q2, :], asg[:], p_az[0:HID, q2, 1, :], ALU.mult).then_inc(h_ok, 1)
                if live(s, L_IDX):
                    g, q2, r = s - L_IDX, (q - L_IDX) % 2, (q - L_IDX) % U
                    dve.wait_ge(cnt1, g + 1)
                    nc.vector.tensor_scalar(nstar[:, q2, 1:2], signs[:, q2:q2 + 1], 0.5, NP / 2, ALU.mult, ALU.add).then_inc(n1, 1)
                    dve.wait_ge(cnt0, g + 1)
                    dve.wait_ge(n1, g + 1)
                    nc.vector.scalar_tensor_tensor(out=flat[:], in0=p_b[:, 0:T], scalar=float(NP), in1=nstar[:, q2, :],
                                                   op0=ALU.mult, op1=ALU.add).then_inc(fl, 1)
                    dve.wait_ge(fl, g + 1)
                    dve.wait_ge(vc, g + 1)
                    wait(dve, added, 16 * T * (g - U + 1))
                    nc.vector.scalar_tensor_tensor(out=ridx[:, r, :], in0=flat[:], scalar=float(-NP), in1=vac[:],
                                                   op0=ALU.add, op1=ALU.add).then_inc(ridx_ok, 1)
                if live(s, L_SEL):
                    g, q2, r = s - L_SEL, (q - L_SEL) % 2, (q - L_SEL) % 4
                    wait(dve, exc_ok, 2 * (g + 1))
                    wait(dve, S_ok, g)
                    nc.vector.tensor_scalar(past[:], slot_row[:], ei[:, r, 1:2], None, ALU.is_ge).then_inc(past_ok, 1)
                    wait(dve, sel_ps, g - 1)
                    wait(dve, past_ok, g + 1)
                    nc.vector.scalar_tensor_tensor(out=S[:, q2, :], in0=slot_row[:], scalar=ei[:, r, 0:1],
                                                   in1=past[:], op0=ALU.is_ge, op1=ALU.subtract).then_inc(S_ok, 1)
                if live(s, L_A):
                    g, q2, r = s - L_A, (q - L_A) % 2, (q - L_A) % U
                    s1, s2, e1 = sv[:, q2, :, 0], sv[:, q2, :, 1], xg[:, r, :, D + 2]
                    me = ecol[:, bass.ds(g, 1)]
                    dve.wait_ge(sv_ok, g + 1)
                    wait(dve, w_ok, g)
                    nc.vector.scalar_tensor_tensor(out=wt[:, 0, :], in0=e1, scalar=me, in1=s1, op0=ALU.is_equal,
                                                   op1=ALU.mult).then_inc(wk, 1)
                    nc.vector.scalar_tensor_tensor(out=wt[:, 1, :], in0=e1, scalar=me, in1=s2, op0=ALU.not_equal,
                                                   op1=ALU.mult).then_inc(wk, 1)
                    nc.vector.scalar_tensor_tensor(out=wt[:, 2, :], in0=s1, scalar=1e-20, in1=s2, op0=ALU.add,
                                                   op1=ALU.add).then_inc(wk, 1)
                    dve.wait_ge(wk, 5 * g + 3)
                    nc.vector.tensor_tensor(wt[:, 3, :], wt[:, 0, :], wt[:, 1, :], ALU.add).then_inc(wk, 1)
                    nc.vector.reciprocal(wt[:, 4, :], wt[:, 2, :]).then_inc(wk, 1)
                    dve.wait_ge(wk, 5 * g + 5)
                    wait(dve, ys_ok, T * (g - 3))
                    nc.vector.scalar_tensor_tensor(out=wgt[:, (q - L_A) % 4, :], in0=wt[:, 3, :], scalar=ROUTE_SCALE, in1=wt[:, 4, :],
                                                   op0=ALU.mult, op1=ALU.mult).then_inc(w_ok, 1)
                if live(s, L_EXC):
                    g, r = s - L_EXC, (q - L_EXC) % 4
                    wait(dve, exc_ps, g + 1)
                    wait(dve, sel_ps, g - 3)
                    wait(dve, S_ok, g - 3)
                    nc.vector.tensor_copy(ei[:, r, :], p_e[:, 0:2]).then_inc(exc_ok, 1)
                    nc.vector.tensor_scalar(exc16[:, r:r + 1], p_e[:, 0:1], 4.0 * CAP, None, ALU.min).then_inc(exc_ok, 1)
                if live(s, L_CNT):
                    wait(dve, m0_ok, s + 1)
                    wait(dve, m1_ok, s + 1)
                    wait(dve, sel_ps, s - 3)
                    nc.vector.tensor_tensor_scan(cnt[:, q % 4, :], is0[:, q % 2, :], is1[:, q % 2, :],
                                                 0.0, ALU.add, ALU.add).then_inc(c_ok, 1)
            slots(dve, slot)

        @block.tensor
        def _(pe):
            pe.wait_ge(iotas, 13)

            def slot(s, q):
                if live(s, L_EXC):
                    g, r = s - L_EXC, (q - L_EXC) % 4
                    wait(pe, c_ok, g + 1)
                    wait(pe, exc_ok, 2 * g)
                    nc.tensor.matmul(p_e[:, 0:1], before[:], cnt[:, r, NP - 1:NP], start=True, stop=True)
                    nc.tensor.matmul(p_e[:, 1:2], upto[:], cnt[:, r, NP - 1:NP], start=True, stop=True).then_inc(exc_ps, 1)
                if live(s, L_T):
                    g, q2, r = s - L_T, (q - L_T) % 2, (q - L_T) % U
                    pe.wait_ge(gathered[r], 4 * (g - r) + 16 * T)
                    wait(pe, T_sb, g)
                    for t in range(T):
                        ins = nc.tensor.transpose(p_x[:, t * 128:(t + 1) * 128], xg[:, r, t, 0:D], ident[:])
                    ins.then_inc(T_ps, 1)
                if live(s, L_A):
                    g, q2, r = s - L_A, (q - L_A) % 2, (q - L_A) % 4
                    pe.wait_ge(T_sb, g + 1)
                    pe.wait_ge(w_in[r], 8 * (g - r) + 32)
                    wait(pe, h_ok, g - 1)
                    nc.tensor.matmul(p_az[0:HID, q2, 0, :], wr[:, r, 0:HID], xT[:, q2, :], start=True, stop=True)
                    nc.tensor.matmul(p_az[0:HID, q2, 1, :], wr[:, r, HID:2 * HID], xT[:, q2, :], start=True, stop=True).then_inc(az_ps, 1)
                if live(s, L_Y):
                    g, q2 = s - L_Y, (q - L_Y) % 2
                    pe.wait_ge(h_ok, g + 1)
                    wait(pe, ys_ok, T * g)
                    for t in range(T):
                        ins = nc.tensor.matmul(p_y[:, t * D:(t + 1) * D], hh[:, q2, t * 128:(t + 1) * 128], w2r[:, (q - L_Y) % 4, :],
                                               start=True, stop=True)
                    ins.then_inc(y_ps, 1)
                if live(s, L_SEL):
                    g, q2, r = s - L_SEL, (q - L_SEL) % 2, (q - L_SEL) % 4
                    pe.wait_ge(S_ok, g + 1)
                    wait(pe, cnt0, g)
                    wait(pe, cnt1, g)
                    wait(pe, fl, g)
                    for t in range(T):
                        St = S[:, q2, t * 128:(t + 1) * 128]
                        nc.tensor.matmul(p_n[t][:], St, cnt[:, r, :], start=True, stop=False)
                        nc.tensor.matmul(p_n[t][:], St, exc16[:, r:r + 1].to_broadcast([128, NP]), start=False, stop=True)
                        ins = nc.tensor.matmul(p_b[:, t:t + 1], St, rowp1[:], start=True, stop=True)
                    ins.then_inc(sel_ps, 1)
            slots(pe, slot)


def kernel(**inputs):
    import numpy as np
    import concourse.bacc as bacc
    from concourse.bass_utils import run_bass_kernel_spmd

    a = {k.replace("L0_", "").replace("tok_", "").replace("attn_", "").replace("ffn_", ""): np.asarray(v)
         for k, v in inputs.items()}
    x = a["x"]
    steps = (FG * GR + 1) * STRIDE
    arrays = {
        "x": np.pad(x, ((0, 0), (0, steps - x.shape[1]), (0, 0)), mode="edge").reshape(B, steps * C),
        "W": a["W"].reshape(C, PATCH, D).transpose(1, 0, 2).reshape(C * PATCH, D),
        "b": a["b"], "ln_g": a["ln_g"], "ln_b": a["ln_b"],
        "posA": np.pad(a["pos_emb"][0, :FIRST], ((0, GR), (0, 0))).reshape(1, -1),
        "pos": np.pad(a["pos_emb"][0], ((0, NP - STEPS), (0, 0))),
        "type_emb": a["type_emb"], "Br": a["B_real"], "Bi": a["B_img"],
        "nu": a["nu"], "theta": a["theta"], "delta": a["delta"], "h0r": a["h0_real"], "h0i": a["h0_img"],
        "gate_w": a["gate_w"], "w13": np.concatenate([a["w1"], a["w3"]], axis=2), "w2": a["w2"],
        "sw1": a["sw1"], "sw3": a["sw3"], "sw2": a["sw2"],
    }
    nc = bacc.Bacc("TRN2", target_bir_lowering=False, num_devices=1)
    fed, args = {}, []
    for name, v in arrays.items():
        v = np.ascontiguousarray(v)
        fed[f"in_{name}"] = v
        args.append(nc.dram_tensor(f"in_{name}", v.shape, mybir.dt.from_np(v.dtype), kind="ExternalInput").ap())
    out = nc.dram_tensor("out_rows", (ROWS, D), F32, kind="ExternalOutput").ap()
    tower(nc, *args, out)
    r = run_bass_kernel_spmd(nc, [fed], core_ids=[0])
    return r.results[0]["out_rows"][:B * NP].reshape(B, NP, D)[:, :STEPS]
```

```python
from contextlib import ExitStack

import concourse.bass as bass
from concourse import mybir

F32 = mybir.dt.float32
F16 = mybir.dt.float16
BF16 = mybir.dt.bfloat16
U32 = mybir.dt.uint32
ALU = mybir.AluOpType
ACT = mybir.ActivationFunctionType
AX = mybir.AxisListType.X

B, D = 128, 128
STEPS = 511
NP = 512
C, PATCH, STRIDE = 8, 16, 8
SEG = STRIDE * C
FIRST = 128
GR, CH = 4, 16
NG = NP // GR
NC_A = FIRST // CH
NC = NP // CH
E, HID, CAP = 64, 64, 256
ROUTE_SCALE = 2.5
EPS = 1e-5
ROW = D + 4
ROWS = B * NP + CAP
FG = FIRST // GR + 1
HALF_PI = 1.5707963267948966


def wait(eng, sem, value):
    if isinstance(value, int) and value <= 0:
        return
    eng.wait_ge(sem, value)


def tower(nc, x, W, b, ln_g, ln_b, posA, pos, type_emb, Br, Bi, nu, theta, delta, h0r, h0i,
          gate_w, w13, w2, sw1, sw3, sw2, out):
    u_dram = nc.dram_tensor("u_dram", [128, FG, GR * 2 * 128], F32, kind="Internal").ap()
    h1_dram = nc.dram_tensor("h1_dram", [128, FG, GR * 128], F32, kind="Internal").ap()
    rT_dram = nc.dram_tensor("rT_dram", [NP - FIRST, 128], F32, kind="Internal").ap()
    x3_dram = nc.dram_tensor("x3_dram", [ROWS, ROW], F32, kind="Internal").ap()
    scratch = dict(u=u_dram, h1=h1_dram, rT=rT_dram, x3=x3_dram)
    with ExitStack() as ctx:
        def sb(name, shape, dt=F32):
            return ctx.enter_context(nc.sbuf_tensor(name, shape, dt))

        keep = dict(
            sems=ctx,
            ident=sb("ident", [128, 128]), ones=sb("ones", [128, 128]),
            turn=sb("turn", [128, CH, 2, 128]),
            Bj=sb("Bj", [128, CH, 2, 128]),
            colC=sb("colC", [128, CH + 1]), colS=sb("colS", [128, CH + 1]),
            decay=sb("decay", [128, 1]),
            base=sb("base", [128, 128]),
            carry=sb("carry", [128, 2, 128]),
            top=sb("top", [128, 2, NP]),
            eps=sb("eps", [128, GR]), minus=sb("minus", [128, GR]),
            halfneg=sb("halfneg", [128, GR]),
            g2=sb("g2", [128, 2 * GR, 2, 128]),
            raw=sb("raw", [128, (NP - FIRST) // 128 + 1, 128]),
            xg=sb("xg", [128, 4, (GR + 1) * SEG]),
            rows=sb("rows", [4 * GR + 1, 4, GR * 128]),
            Wp=sb("Wp", [128, 128]), brow=sb("brow", [1, 128]),
            lng=sb("lng", [128, 128]), lnb=sb("lnb", [128, 128]),
            ub=sb("ub", [128, 4, GR, 2, 128]),
            h1=sb("h1b", [128, 4, GR, 128]),
            gnat=sb("gnat", [E, 128]), sw13=sb("sw13", [128, 2, 128]), sw2=sb("sw2s", [128, 128]),
            ecol=sb("ecol", [128, E]), necol=sb("necol", [128, E]),
            slot_row=sb("slot_row", [128, CAP]),
            slot_col=sb("slot_col", [128, CAP // 128]), slot_half=sb("slot_half", [128, CAP // 128]),
            empty_row=sb("empty_row", [128, CAP // 128]),
            before=sb("before", [128, 128], F16),
            upto=sb("upto", [128, 128], F16),
            one_on=sb("one_on", [128, 1]), one_b=sb("one_b", [128, 1]), rowp1=sb("rowp1", [128, 1], F16),
        )
        front_sems = {n: nc.alloc_semaphore(name="f_" + n) for n in ("consts", "type_in", "rows_zero", "x_in0", "x_in1", "x_in2", "x_in3")}
        pos_in = ctx.enter_context(nc.semaphore("b_pos_in"))
        scan_sems = {n: ctx.enter_context(nc.semaphore("m_" + n)) for n in
                     ("consts", "u_in0", "u_in1", "u_in2", "u_in3", "h1_in0", "h1_in1", "h1_in2", "h1_in3")}
        setup(nc, keep, front_sems, x, W, b, ln_g, ln_b, type_emb, Br, Bi, nu, theta, delta, h0r, h0i)
        front(nc, keep, front_sems, scratch, x, posA, pos, pos_in)
        with ExitStack() as inner:
            A = inner.enter_context(nc.sbuf_tensor("A", [128, CH, 2, 128], F32))
            P = inner.enter_context(nc.sbuf_tensor("P", [128, NP - FIRST, 2], F32))
            keep["A"], keep["P"] = A, P
            between(nc, keep, scan_sems, scratch, pos_in, gate_w, sw1, sw3, sw2)
            scan(nc, keep, scan_sems, scratch, pos, out)
        routed(nc, keep, scratch, w13, w2, out)


def load_patches(sp, keep, x_in, x, g, r):
    sp.dma_start(keep["xg"][:, r, :], x[:, bass.ds(g * (GR * SEG), (GR + 1) * SEG)]).then_inc(x_in[r], 16)


def setup(nc, keep, front_sems, x, W, b, ln_g, ln_b, type_emb, Br, Bi, nu, theta, delta, h0r, h0i):
    ident, ones, turn, Bj = keep["ident"], keep["ones"], keep["turn"], keep["Bj"]
    colC, colS, decay, carry = keep["colC"], keep["colS"], keep["decay"], keep["carry"]
    with ExitStack() as ctx:
        def sb(name, shape, dt=F32):
            return ctx.enter_context(nc.sbuf_tensor(name, shape, dt))

        def sem(name):
            return keep["sems"].enter_context(nc.semaphore("c_" + name))

        cols = sb("cols", [128, 8])
        tmp = sb("s_tmp", [128, 4, CH])
        Bw = sb("Bw", [128, 2, 128])
        dB = sb("dB", [128, 2, 128])
        diag_delta = sb("diag_delta", [128, 128])
        zeros = sb("zeros", [128, 128])
        t4 = sb("t4", [128, 2, 4, GR, 128])
        ps = ctx.enter_context(nc.psum_tensor("s_ps", [128, 2, 2, GR, 128], F32))
        negS = sb("negS", [128, CH + 1])
        psd = ctx.enter_context(nc.psum_tensor("s_psd", [128, 512], F32))
        s_in, s_id, s_act, s_dve, s_diag, s_dd, s_cos, s_bc, s_prod, s_pd, s_dB, s_Bj = (
            sem("s_" + n) for n in "in id act dve diag dd cos bc prod pd dB Bj".split())
        block = ctx.enter_context(nc.Block())

        @block.sync
        def _(sp):
            for i, v in enumerate((nu, theta, delta, h0r, h0i)):
                sp.dma_start(cols[:, i:i + 1], v.rearrange("(p a) -> p a", a=1)).then_inc(s_in, 16)
            sp.dma_start(Bw[:, 0, :], Br).then_inc(s_in, 16)
            sp.dma_start(Bw[:, 1, :], Bi).then_inc(s_in, 16)
            f = front_sems
            x_in = [f[f"x_in{r}"] for r in range(4)]
            load_patches(sp, keep, x_in, x, 0, 0)
            sp.dma_start(keep["Wp"][:], W).then_inc(f["consts"], 16)
            sp.dma_start(keep["brow"][:], b.rearrange("(a n) -> a n", a=1)).then_inc(f["consts"], 16)
            sp.dma_start(keep["lng"][:], ln_g.partition_broadcast(128)).then_inc(f["consts"], 16)
            sp.dma_start(keep["lnb"][:], ln_b.partition_broadcast(128)).then_inc(f["consts"], 16)
            load_patches(sp, keep, x_in, x, 1, 1)
            sp.wait_ge(f["rows_zero"], 1)
            for r in range(4):
                for i in range(GR):
                    sp.dma_start(keep["rows"][4 * i:4 * i + 4, r, i * 128:(i + 1) * 128], type_emb).then_inc(f["type_in"], 16)
            sp.wait_ge(s_in, 112)

        @block.gpsimd
        def _(pool):
            nc.gpsimd.memset(ident[:], 0.0).then_inc(s_id, 1)
            nc.gpsimd.memset(ones[:], 1.0).then_inc(s_id, 1)
            nc.gpsimd.memset(zeros[:], 0.0).then_inc(s_id, 1)
            nc.gpsimd.memset(keep["halfneg"][:], -0.5).then_inc(s_id, 1)
            nc.gpsimd.memset(keep["eps"][:], EPS)
            nc.gpsimd.memset(keep["minus"][:], -1.0)
            nc.gpsimd.memset(cols[:, 5:6], HALF_PI).then_inc(s_id, 1)
            nc.gpsimd.memset(keep["rows"][:], 0.0).then_inc(front_sems["rows_zero"], 1)
            pool.wait_ge(s_id, 5)
            nc.gpsimd.affine_select(out=ident[:], in_=ident[:], compare_op=ALU.not_equal, fill=1.0, base=0,
                                    pattern=[[-1, 128]], channel_multiplier=1).then_inc(s_id, 1)
            for q in range(CH // GR):
                pool.wait_ge(s_prod, 4 * (q + 1))
                js, t = slice(q * GR, (q + 1) * GR), q % 2
                nc.gpsimd.tensor_tensor(Bj[:, js, 0, :], t4[:, t, 0, :, :], t4[:, t, 1, :, :], ALU.subtract).then_inc(s_Bj, 1)
                nc.gpsimd.tensor_tensor(Bj[:, js, 1, :], t4[:, t, 2, :, :], t4[:, t, 3, :, :], ALU.add).then_inc(s_Bj, 1)

        @block.scalar
        def _(act):
            act.wait_ge(s_in, 112)
            act.wait_ge(s_id, 5)
            nc.scalar.activation(cols[:, 6:7], cols[:, 0:1], ACT.Exp).then_inc(s_act, 1)
            act.wait_ge(s_act, 1)
            nc.scalar.activation(decay[:], cols[:, 6:7], ACT.Exp, scale=-1.0).then_inc(s_act, 1)
            nc.scalar.activation(colC[:, 1:2], cols[:, 1:2], ACT.Sin, bias=cols[:, 5:6]).then_inc(s_act, 1)
            nc.scalar.activation(colS[:, 1:2], cols[:, 1:2], ACT.Sin).then_inc(s_act, 1)
            act.wait_ge(s_id, 6)
            act.wait_ge(s_cos, 1)
            for j in range(CH):
                nc.scalar.activation(turn[:, j, 1, :], ident[:], ACT.Copy, scale=negS[:, j:j + 1]).then_inc(s_diag, 1)

        @block.vector
        def _(dve):
            done = [0]

            def then(ins):
                done[0] += 1
                ins.then_inc(s_dve, 1)
                dve.wait_ge(s_dve, done[0])

            nc.vector.memset(colC[:, 0:1], 1.0).then_inc(s_dve, 1)
            nc.vector.memset(colS[:, 0:1], 0.0).then_inc(s_dve, 1)
            done[0] = 2
            dve.wait_ge(s_dve, 2)
            dve.wait_ge(s_act, 4)
            k = 1
            while k < CH:
                a, o = slice(1, k + 1), slice(k + 1, 2 * k + 1)
                then(nc.vector.tensor_scalar(tmp[:, 0, 0:k], colS[:, a], colS[:, k:k + 1], None, ALU.mult))
                then(nc.vector.tensor_scalar(tmp[:, 1, 0:k], colC[:, a], colS[:, k:k + 1], None, ALU.mult))
                then(nc.vector.scalar_tensor_tensor(out=colC[:, o], in0=colC[:, a], scalar=colC[:, k:k + 1],
                                                    in1=tmp[:, 0, 0:k], op0=ALU.mult, op1=ALU.subtract))
                then(nc.vector.scalar_tensor_tensor(out=colS[:, o], in0=colS[:, a], scalar=colC[:, k:k + 1],
                                                    in1=tmp[:, 1, 0:k], op0=ALU.mult, op1=ALU.add))
                k *= 2
            then(nc.vector.tensor_scalar(tmp[:, 0, 0:1], cols[:, 4:5], colS[:, 1:2], None, ALU.mult))
            then(nc.vector.tensor_scalar(tmp[:, 1, 0:1], cols[:, 3:4], colS[:, 1:2], None, ALU.mult))
            then(nc.vector.scalar_tensor_tensor(out=tmp[:, 2, 0:1], in0=cols[:, 3:4], scalar=colC[:, 1:2],
                                                in1=tmp[:, 0, 0:1], op0=ALU.mult, op1=ALU.subtract))
            then(nc.vector.scalar_tensor_tensor(out=tmp[:, 3, 0:1], in0=cols[:, 4:5], scalar=colC[:, 1:2],
                                                in1=tmp[:, 1, 0:1], op0=ALU.mult, op1=ALU.add))
            nc.vector.tensor_scalar(negS[:], colS[:], -1.0, None, ALU.mult).then_inc(s_cos, 1)
            dve.wait_ge(s_id, 6)
            nc.vector.tensor_scalar(diag_delta[:], ident[:], cols[:, 2:3], None, ALU.mult).then_inc(s_dd, 1)
            for j in range(CH):
                nc.vector.tensor_scalar(turn[:, j, 0, :], ident[:], colC[:, j:j + 1], None, ALU.mult).then_inc(s_diag, 1)
            dve.wait_ge(s_pd, 1)
            for c in range(2):
                nc.vector.tensor_tensor(dB[:, c, :], Bw[:, c, :], psd[:, 0:128], ALU.mult).then_inc(s_dB, 1)
            dve.wait_ge(s_dB, 2)
            for q in range(CH // GR):
                dve.wait_ge(s_bc, q + 1)
                wait(dve, s_Bj, 2 * (q - 1))
                bre = dB[:, 0, :].unsqueeze(1).to_broadcast([128, GR, 128])
                bim = dB[:, 1, :].unsqueeze(1).to_broadcast([128, GR, 128])
                for i, (p, w) in enumerate(((0, bre), (1, bim), (0, bim), (1, bre))):
                    nc.vector.tensor_tensor(t4[:, q % 2, i, :, :], ps[:, q % 2, p, :, :], w, ALU.mult).then_inc(s_prod, 1)
            for c in range(2):
                nc.vector.tensor_scalar(carry[:, c, :], zeros[:], tmp[:, 2 + c, 0:1], None, ALU.add)

        @block.tensor
        def _(pe):
            pe.wait_ge(s_id, 6)
            pe.wait_ge(s_dd, 1)
            nc.tensor.matmul(psd[:, 0:128], ones[:], diag_delta[:], start=True, stop=True).then_inc(s_pd, 1)
            pe.wait_ge(s_diag, 2 * CH)
            for q in range(CH // GR):
                wait(pe, s_prod, 4 * (q - 1))
                for p in range(2):
                    ins = nc.tensor.matmul(ps[:, q % 2, p, :, :], ones[:], turn[:, q * GR:(q + 1) * GR, p, :],
                                           start=True, stop=True)
                ins.then_inc(s_bc, 1)


def front(nc, keep, front_sems, scratch, x, posA, pos, pos_in):
    ident, Bj, base = keep["ident"], keep["Bj"], keep["base"]
    L_T, L_H, L_BN = 0, 1, 1
    L_Z, L_AFF, L_E = 2, 3, 4
    L_TYPE, L_MT, L_MTS, L_ROW = 2, 3, 4, 4
    L_V, L_XN, L_XT, L_U, L_OUT = 5, 6, 7, 8, 9
    L_H1ST, L_UST = 6, 10
    AHEAD = 1
    used = []
    PEEL = 4
    LAST = FG + L_UST
    with ExitStack() as ctx:
        def sb(name, shape, dt=F32):
            return ctx.enter_context(nc.sbuf_tensor(name, shape, dt))

        def ps(name, shape):
            return ctx.enter_context(nc.psum_tensor(name, shape, F32))

        def sem(name):
            used.append(nc.alloc_semaphore(name="f_" + name))
            return used[-1]

        xg, rows, Wp, brow, lng, lnb = (keep[k] for k in ("xg", "rows", "Wp", "brow", "lng", "lnb"))
        pT = sb("pT", [128, 2, GR, 128])
        hst = sb("hst", [128, GR, 6])
        gst = sb("gst", [128, GR, 6])
        pst = sb("pst", [128, GR, 6])
        OF_H, OF_G, OF_P = range(3)
        mv = sb("mv", [128, 2, 3, GR, 2])
        var = sb("var_in", [128, 2, 3, GR])
        negm = sb("negm", [128, 2, 2, GR])
        rs = sb("rs", [128, 2, 3, GR])
        nmr = sb("nmr", [128, 2, 2, GR])
        expo = sb("expo", [128, 3, GR])
        eps2 = sb("eps2", [128, 2, GR])
        minus2 = sb("minus2", [128, 2, GR])
        bessel = sb("bessel", [128, GR])
        z0 = sb("z0", [128, 2, GR, 128])
        z1 = sb("z1", [128, 2, GR, 128])
        z2 = sb("z2", [128, 2, GR, 128])
        er = sb("er", [128, 2, GR, 128])
        h1 = sb("h1", [128, 4, GR, 128])
        seg = sb("seg", [128, 2, GR + 1])
        pmm = sb("pmm", [128, 2, GR])
        rng = sb("rng", [128, 2, GR])
        tm = sb("tm", [128, 2, GR])
        mask = sb("mask", [128, 2, 17])
        mT = sb("mT", [17, 2, 128])
        xn = sb("xn", [128, 2, GR, 128])
        xnT = sb("xnT", [128, 2, GR, 128])
        us = sb("us", [128, 4, GR, 2, 128])
        p_pT, p_T, p_m, p_xT = (ps(n, [128, 512]) for n in ("p_pT", "p_T", "p_m", "p_xT"))
        p_H = ps("p_H", [128, 2, 512])
        p_u = ps("p_u", [128, GR, 2, 128])

        used.extend(front_sems.values())
        consts, type_in = front_sems["consts"], front_sems["type_in"]
        pool_c, mv_zero = sem("pool_c"), sem("mv_zero")
        x_in = [front_sems[f"x_in{i}"] for i in range(4)]
        row_in = [sem(f"row_in{i}") for i in range(4)]
        h1_out = [sem(f"h1_out{i}") for i in range(4)]
        u_out = [sem(f"u_out{i}") for i in range(4)]
        (pT_ps, pT_sb, h_ps, hbn, hag, z_0, z_1, z_2, e_ok, segs, pbn, pag, pmm_ok, range_ok, tmk,
         m_ps, m_sb, T_ps, h1_ok, gbn, gag, mv_used, rs_ok, nmr_ok, xn_ok, xT_ps, xT_sb, u_ps, u_sb) = (
            sem(n) for n in
            "pT_ps pT_sb h_ps hbn hag z_0 z_1 z_2 e_ok segs pbn pag pmm_ok range_ok tmk "
            "m_ps m_sb T_ps h1_ok gbn gag mv_used rs_ok nmr_ok xn_ok xT_ps xT_sb u_ps u_sb".split())
        block = ctx.enter_context(nc.Block())

        def slots(eng, slot):
            for s in range(4 * PEEL):
                slot(s, s % 4)
            with eng.Fori(PEEL, FIRST // CH) as c:
                for q in range(4):
                    slot(4 * c + q, q)
            for s in range(FIRST // GR, LAST):
                slot(s, s % 4)

        def live(s, lag):
            return not isinstance(s, int) or 0 <= s - lag < FG

        def stats(s):
            return not isinstance(s, int) or s >= L_BN + 1

        @block.sync
        def _(sp):
            def load_x(g, r):
                wait(sp, segs, 2 * (g - 3))
                wait(sp, pT_ps, g - 3)
                load_patches(sp, keep, x_in, x, g, r)

            def slot(s, q):
                if live(s, -AHEAD) and not (isinstance(s, int) and s < AHEAD):
                    load_x(s + AHEAD, (q + AHEAD) % 4)
                if live(s, 1):
                    g, r = s - 1, (q - 1) % 4
                    wait(sp, T_ps, g - 3)
                    sp.dma_start(rows[16:17, r, :], posA[:, bass.ds(g * (GR * 128), GR * 128)]).then_inc(row_in[r], 16)
                if live(s, L_H1ST):
                    g, r = s - L_H1ST, (q - L_H1ST) % 4
                    wait(sp, h1_ok, g + 1)
                    sp.dma_start(scratch["h1"][:, bass.ds(g, 1), :].rearrange("p a n -> p (a n)"),
                                 h1[:, r, :, :].rearrange("p a n -> p (a n)")).then_inc(h1_out[r], 16)
                if live(s, L_UST):
                    g, r = s - L_UST, (q - L_UST) % 4
                    wait(sp, u_sb, g + 1)
                    sp.dma_start(scratch["u"][:, bass.ds(g, 1), :].rearrange("p a n -> p (a n)"),
                                 us[:, r, :, :, :].rearrange("p a c n -> p (a c n)")).then_inc(u_out[r], 16)
            sp.dma_start(keep["raw"][:, 0:(NP - FIRST) // 128, :],
                         pos[FIRST:NP, :].rearrange("(t p) n -> p t n", p=128)).then_inc(pos_in, 16)
            slots(sp, slot)
            for i in range(4):
                sp.wait_ge(h1_out[i], 16 * ((FG - i + 3) // 4))
                sp.wait_ge(u_out[i], 16 * ((FG - i + 3) // 4))

        @block.gpsimd
        def _(pool):
            nc.gpsimd.memset(mask[:], 1.0).then_inc(pool_c, 1)
            nc.gpsimd.memset(expo[:, 0:2, :], -0.5).then_inc(pool_c, 1)
            nc.gpsimd.memset(expo[:, 2, :], 0.5).then_inc(pool_c, 1)
            nc.gpsimd.memset(eps2[:], EPS).then_inc(pool_c, 1)
            nc.gpsimd.memset(minus2[:], -1.0).then_inc(pool_c, 1)
            nc.gpsimd.memset(bessel[:], D / (D - 1.0)).then_inc(pool_c, 1)
            nc.gpsimd.memset(mv[:], 1.0).then_inc(mv_zero, 1)
            pool.wait_ge(pool_c, 6)
            pool.wait_ge(mv_zero, 1)
            pool.wait_ge(consts, 64)

            def slot(s, q):
                if stats(s):
                    n, m, k = s - L_BN, (q - 1) % 2, q % 2
                    if live(s, L_BN + 1):
                        wait(pool, hag, 4 * (s - L_BN))
                        wait(pool, pag, 4 * (s - L_BN))
                    if live(s, L_V + 1):
                        wait(pool, gag, 4 * (s - L_V))
                    wait(pool, rs_ok, n - 1)
                    nc.gpsimd.tensor_tensor(var[:, k, 0:2, :], mv[:, m, 0:2, :, 1], eps2[:], ALU.add).then_inc(mv_used, 1)
                    nc.gpsimd.tensor_tensor(var[:, k, 2, :], mv[:, m, 2, :, 1], bessel[:], ALU.mult).then_inc(mv_used, 1)
                    wait(pool, nmr_ok, n - 1)
                    nc.gpsimd.tensor_tensor(negm[:, k, :, :], mv[:, m, 0:2, :, 0], minus2[:], ALU.mult).then_inc(mv_used, 1)
                    wait(pool, mv_used, 3 * n)
                    if live(s, L_XN + 2):
                        wait(pool, xn_ok, 4 * (s - L_XN - 1))
                    if live(s, L_Z + 2):
                        wait(pool, z_0, 4 * (s - L_Z - 1))
                        wait(pool, tmk, 5 * (s - L_TYPE - 1))
                    nc.gpsimd.tensor_tensor(rs[:, k, :, :], var[:, k, :, :], expo[:], ALU.pow).then_inc(rs_ok, 1)
                    wait(pool, rs_ok, n)
                    nc.gpsimd.tensor_tensor(nmr[:, k, :, :], negm[:, k, :, :], rs[:, k, 0:2, :], ALU.mult).then_inc(nmr_ok, 1)
                if live(s, L_AFF):
                    g, q2 = s - L_AFF, (q - L_AFF) % 2
                    wait(pool, z_0, 4 * (g + 1))
                    wait(pool, z_2, g - 1)
                    nc.gpsimd.tensor_tensor(z1[:, q2, :, :], z0[:, q2, :, :],
                                            lng[:].unsqueeze(1).to_broadcast([128, GR, 128]), ALU.mult).then_inc(z_1, 1)
                    wait(pool, z_1, g + 1)
                    wait(pool, e_ok, g - 1)
                    nc.gpsimd.tensor_tensor(z2[:, q2, :, :], z1[:, q2, :, :],
                                            lnb[:].unsqueeze(1).to_broadcast([128, GR, 128]), ALU.add).then_inc(z_2, 1)
            slots(pool, slot)

        @block.scalar
        def _(act):
            def slot(s, q):
                if live(s, L_OUT):
                    g, r = s - L_OUT, (q - L_OUT) % 4
                    wait(act, u_ps, g + 1)
                    if not isinstance(s, int) or g >= 4:
                        act.wait_ge(u_out[r], 4 * (g - r))
                    nc.scalar.activation(us[:, r, :, :, :], p_u[:], ACT.Copy).then_inc(u_sb, 1)
                if live(s, L_T):
                    wait(act, pT_ps, s + 1)
                    wait(act, h_ps, s - 1)
                    nc.scalar.activation(pT[:, q % 2, :, :], p_pT[:].rearrange("p (a n) -> p a n", a=GR),
                                         ACT.Copy).then_inc(pT_sb, 1)
                if live(s, L_MTS):
                    g, q2 = s - L_MTS, (q - L_MTS) % 2
                    wait(act, m_ps, g + 1)
                    wait(act, T_ps, g - 1)
                    nc.scalar.activation(mT[:, q2, :], p_m[0:17, 0:128], ACT.Copy).then_inc(m_sb, 1)
                if live(s, L_E):
                    g, q2 = s - L_E, (q - L_E) % 2
                    wait(act, z_2, g + 1)
                    wait(act, h1_ok, g - 1)
                    nc.scalar.activation(er[:, q2, :, :], z2[:, q2, :, :], ACT.Gelu).then_inc(e_ok, 1)
                if live(s, L_Z):
                    g, q2 = s - L_Z, (q - L_Z) % 2
                    wait(act, nmr_ok, s - L_BN)
                    wait(act, z_1, g - 1)
                    for i in range(GR):
                        nc.scalar.activation(z0[:, q2, i, :], p_H[:, q2, i * 128:(i + 1) * 128], ACT.Identity,
                                             bias=nmr[:, q % 2, OF_H, i:i + 1], scale=rs[:, q % 2, OF_H, i:i + 1]).then_inc(z_0, 1)
                if live(s, L_XN):
                    g, q2 = s - L_XN, (q - L_XN) % 2
                    wait(act, nmr_ok, s - L_BN)
                    wait(act, xT_ps, g - 1)
                    for i in range(GR):
                        nc.scalar.activation(xn[:, q2, i, :], h1[:, (q - L_XN) % 4, i, :], ACT.Identity,
                                             bias=nmr[:, q % 2, OF_G, i:i + 1], scale=rs[:, q % 2, OF_G, i:i + 1]).then_inc(xn_ok, 1)
                if live(s, L_XT):
                    g, q2 = s - L_XT, (q - L_XT) % 2
                    wait(act, xT_ps, g + 1)
                    wait(act, u_ps, g - 1)
                    nc.scalar.activation(xnT[:, q2, :, :], p_xT[:].rearrange("p (a n) -> p a n", a=GR), ACT.Copy).then_inc(xT_sb, 1)
            slots(act, slot)

        @block.vector
        def _(dve):
            dve.wait_ge(mv_zero, 1)

            def slot(s, q):
                if live(s, L_V):
                    g, q2, r = s - L_V, (q - L_V) % 2, (q - L_V) % 4
                    wait(dve, e_ok, g + 1)
                    wait(dve, T_ps, g + 1)
                    hs = h1[:, r, :, :]
                    if not isinstance(s, int) or g >= 4:
                        dve.wait_ge(h1_out[r], 4 * (g - r))
                    wait(dve, xn_ok, 4 * (g - 3))
                    nc.vector.tensor_tensor(hs, er[:, q2, :, :], p_T[:].rearrange("p (a n) -> p a n", a=GR),
                                            ALU.add).then_inc(h1_ok, 1)
                if live(s, L_BN):
                    g, r = s - L_BN, (q - L_BN) % 4
                    dve.wait_ge(x_in[r], 4 * (g - r) + 16)
                    wait(dve, pag, 4 * g)
                    for i in range(GR):
                        nc.vector.bn_stats(pst[:, i, :], xg[:, r, i * SEG:(i + 2) * SEG]).then_inc(pbn, 1)
                if live(s, L_V):
                    wait(dve, h1_ok, (s - L_V) + 1)
                    wait(dve, gag, 4 * (s - L_V))
                    for i in range(GR):
                        nc.vector.bn_stats(gst[:, i, :], h1[:, (q - L_V) % 4, i, :]).then_inc(gbn, 1)
                if live(s, L_BN):
                    g, q2 = s - L_BN, (q - L_BN) % 2
                    wait(dve, h_ps, g + 1)
                    wait(dve, hag, 4 * g)
                    for i in range(GR):
                        nc.vector.bn_stats(hst[:, i, :], p_H[:, q2, i * 128:(i + 1) * 128]).then_inc(hbn, 1)
                if live(s, L_BN):
                    g, r = s - L_BN, (q - L_BN) % 4
                    win = xg[:, r, :].rearrange("p (a n) -> p a n", n=SEG)
                    wait(dve, pmm_ok, 2 * g)
                    wait(dve, mv_used, 3 * (s - L_BN - 1))
                    if live(s, L_V):
                        wait(dve, gbn, 4 * (s - L_V) + 4)
                    wait(dve, pbn, 4 * (g + 1))
                    nc.vector.tensor_reduce(seg[:, 0, :], win, AX, ALU.max).then_inc(segs, 1)
                    if live(s, L_V):
                        for i in range(GR):
                            nc.vector.bn_aggr(mv[:, q % 2, OF_G, i, :], gst[:, i, :]).then_inc(gag, 1)
                    wait(dve, hbn, 4 * g + 4)
                    nc.vector.tensor_reduce(seg[:, 1, :], win, AX, ALU.min).then_inc(segs, 1)
                    for i in range(GR):
                        nc.vector.bn_aggr(mv[:, q % 2, OF_H, i, :], hst[:, i, :]).then_inc(hag, 1)
                    for i in range(GR):
                        nc.vector.bn_aggr(mv[:, q % 2, OF_P, i, :], pst[:, i, :]).then_inc(pag, 1)
                    wait(dve, segs, 2 * (g + 1))
                    wait(dve, range_ok, g)
                    for i, op in enumerate((ALU.max, ALU.min)):
                        nc.vector.tensor_tensor(pmm[:, i, :], seg[:, i, 0:GR], seg[:, i, 1:GR + 1], op).then_inc(pmm_ok, 1)
                if live(s, L_V) and not live(s, L_BN):
                    wait(dve, gbn, 4 * (s - L_V) + 4)
                    wait(dve, mv_used, 3 * (s - L_BN - 1))
                    for i in range(GR):
                        nc.vector.bn_aggr(mv[:, q % 2, OF_G, i, :], gst[:, i, :]).then_inc(gag, 1)
                if live(s, L_TYPE):
                    g, q2 = s - L_TYPE, (q - L_TYPE) % 2
                    std = rs[:, q % 2, OF_P, :]
                    mk = mask[:, q2, 0:16].rearrange("p (a k) -> p a k", k=4)
                    dve.wait_ge(range_ok, g + 1)
                    wait(dve, tmk, 5 * g)
                    nc.vector.tensor_scalar(tm[:, 0, :], rng[:, q2, :], 0.5, None, ALU.is_lt).then_inc(tmk, 1)
                    wait(dve, rs_ok, s - L_BN)
                    wait(dve, m_ps, g - 1)
                    wait(dve, tmk, 5 * g + 1)
                    nc.vector.scalar_tensor_tensor(out=mk[:, :, 0], in0=std, scalar=0.1, in1=tm[:, 0, :],
                                                   op0=ALU.is_lt, op1=ALU.mult).then_inc(tmk, 1)
                    nc.vector.scalar_tensor_tensor(out=tm[:, 1, :], in0=std, scalar=0.3, in1=tm[:, 0, :],
                                                   op0=ALU.is_lt, op1=ALU.mult).then_inc(tmk, 1)
                    nc.vector.tensor_scalar(mk[:, :, 3], tm[:, 0, :], -1.0, 1.0, ALU.mult, ALU.add)
                if live(s, L_BN):
                    g, q2 = s - L_BN, (q - L_BN) % 2
                    wait(dve, pmm_ok, 2 * (g + 1))
                    nc.vector.tensor_tensor(rng[:, q2, :], pmm[:, 0, :], pmm[:, 1, :], ALU.subtract).then_inc(range_ok, 1)
                if live(s, L_TYPE):
                    g, q2 = s - L_TYPE, (q - L_TYPE) % 2
                    mk = mask[:, q2, 0:16].rearrange("p (a k) -> p a k", k=4)
                    wait(dve, tmk, 5 * g + 3)
                    nc.vector.tensor_tensor(mk[:, :, 1], tm[:, 1, :], mk[:, :, 0], ALU.subtract).then_inc(tmk, 1)
                    nc.vector.tensor_tensor(mk[:, :, 2], tm[:, 0, :], tm[:, 1, :], ALU.subtract).then_inc(tmk, 1)
            slots(dve, slot)
            dve.wait_ge(h1_ok, FG)
            nc.vector.tensor_copy(base[:], h1[:, (FG - 1) % 4, 0, :])

        @block.tensor
        def _(pe):
            pe.wait_ge(consts, 64)

            def slot(s, q):
                if live(s, L_T):
                    pe.wait_ge(x_in[q], 4 * (s - q) + 16)
                    wait(pe, pT_sb, s)
                    for i in range(GR):
                        ins = nc.tensor.transpose(p_pT[:, i * 128:(i + 1) * 128], xg[:, q, i * SEG:(i + 2) * SEG], ident[:])
                    ins.then_inc(pT_ps, 1)
                if live(s, L_H):
                    g, q2 = s - L_H, (q - L_H) % 2
                    wait(pe, z_0, 4 * (g - 1))
                    wait(pe, hbn, 4 * (g - 1))
                    wait(pe, pT_sb, g + 1)
                    for i in range(GR):
                        o = p_H[:, q2, i * 128:(i + 1) * 128]
                        nc.tensor.matmul(o, keep["ones"][0:1, :], brow[:], start=True, stop=False)
                        ins = nc.tensor.matmul(o, pT[:, q2, i, :], Wp[:], start=False, stop=True)
                    ins.then_inc(h_ps, 1)
                if live(s, L_XT):
                    g, q2 = s - L_XT, (q - L_XT) % 2
                    wait(pe, xn_ok, 4 * (g + 1))
                    wait(pe, xT_sb, g)
                    for i in range(GR):
                        ins = nc.tensor.transpose(p_xT[:, i * 128:(i + 1) * 128], xn[:, q2, i, :], ident[:])
                    ins.then_inc(xT_ps, 1)
                if live(s, L_ROW):
                    g, q2, r = s - L_ROW, (q - L_ROW) % 2, (q - L_ROW) % 4
                    if isinstance(s, int) and s == L_ROW:
                        pe.wait_ge(type_in, 16 * 4 * GR)
                    wait(pe, m_sb, g + 1)
                    wait(pe, h1_ok, g)
                    pe.wait_ge(row_in[r], 4 * (g - r) + 16)
                    nc.tensor.matmul(p_T[:], mT[:, q2, :], rows[:, r, :], start=True, stop=True).then_inc(T_ps, 1)
                if live(s, L_U):
                    g, q2 = s - L_U, (q - L_U) % 2
                    wait(pe, xT_sb, g + 1)
                    wait(pe, u_sb, g)
                    for i in range(GR):
                        j = GR * ((q - L_U) % 4) + i
                        for c in range(2):
                            ins = nc.tensor.matmul(p_u[:, i, c, :], Bj[:, j, c, :], xnT[:, q2, i, :], start=True, stop=True)
                    ins.then_inc(u_ps, 1)
                if live(s, L_MT):
                    g, q2 = s - L_MT, (q - L_MT) % 2
                    wait(pe, tmk, 5 * (g + 1))
                    wait(pe, m_sb, g)
                    nc.tensor.transpose(p_m[0:17, 0:128], mask[:, q2, :], ident[:]).then_inc(m_ps, 1)
            slots(pe, slot)

    nc.all_engine_barrier()
    nc.clear_and_free_semaphores(used)
    nc.all_engine_barrier()


def between(nc, keep, scan_sems, scratch, pos_in, gate_w, sw1, sw3, sw2):
    ident, ones, Bj, base, A, P = (keep[k] for k in ("ident", "ones", "Bj", "base", "A", "P"))
    NB = NP - FIRST
    T = NB // 128
    with ExitStack() as ctx:
        def sb(name, shape, dt=F32):
            return ctx.enter_context(nc.sbuf_tensor(name, shape, dt))

        def ps(name, shape):
            return ctx.enter_context(nc.psum_tensor(name, shape, F32))

        def sem(name):
            return keep["sems"].enter_context(nc.semaphore("b_" + name))

        cen = sb("cen", [128, T + 1, 128])
        raw = keep["raw"]
        bst = sb("bst", [128, T + 1, 6])
        bmv = sb("bmv", [128, T + 1, 2])
        cT = sb("cT", [128, T + 1, 128])
        twice = sb("twice", [128, 128])
        sq = sb("sq", [128, NB])
        var = sb("var", [128, 2, NB])
        root = sb("root", [128, NB])
        newton = sb("newton", [128, 4, NB])
        R = sb("R", [128, T, 128])
        RT = sb("RT", [128, T, 128])
        p_c, p_v = ps("p_c", [128, 512]), ps("p_v", [128, 512])
        p_A = ps("p_A", [128, 2, 8, 128])
        p_P = ps("p_P", [128, 2, 512])
        names = "raw_ok st mv cen_ok c_ps c_sb tw sq_ok v_ps var_1 var_2 root_ok nw R_ok R_ps RT_ok RT_out A_ps A_sb P_ps P_sb".split()
        (raw_ok, st, mv, cen_ok, c_ps, c_sb, tw, sq_ok, v_ps, var_1, var_2, root_ok, nw, R_ok, R_ps, RT_ok, RT_out,
         A_ps, A_sb, P_ps, P_sb) = (sem(n) for n in names)
        block = ctx.enter_context(nc.Block())

        @block.sync
        def _(sp):
            m = scan_sems
            for g in range(4):
                sp.dma_start(keep["ub"][:, g, :, :, :].rearrange("p a c n -> p (a c n)"), scratch["u"][:, g, :]).then_inc(m[f"u_in{g}"], 16)
                sp.dma_start(keep["h1"][:, g, :, :].rearrange("p a n -> p (a n)"), scratch["h1"][:, g, :]).then_inc(m[f"h1_in{g}"], 16)
            sp.dma_start(keep["gnat"][:], gate_w).then_inc(m["consts"], 16)
            sp.dma_start(keep["sw13"][:, 0, :], sw1).then_inc(m["consts"], 16)
            sp.dma_start(keep["sw13"][:, 1, :], sw3).then_inc(m["consts"], 16)
            sp.dma_start(keep["sw2"][:], sw2).then_inc(m["consts"], 16)
            sp.wait_ge(RT_ok, 1)
            sp.dma_start(scratch["rT"].rearrange("(t p) n -> p t n", p=128), RT[:]).then_inc(RT_out, 16)
            sp.wait_ge(RT_out, 16)

        @block.gpsimd
        def _(pool):
            nc.gpsimd.tensor_copy(raw[:, T, :], base[:]).then_inc(raw_ok, 1)

        @block.scalar
        def _(act):
            act.wait_ge(c_ps, 1)
            nc.scalar.activation(cT[:], p_c[:].rearrange("p (t n) -> p t n", n=128), ACT.Copy).then_inc(c_sb, 1)
            act.wait_ge(var_2, 1)
            nc.scalar.activation(root[:], var[:, 1, :], ACT.Sqrt).then_inc(root_ok, 1)
            for q in range(4):
                act.wait_ge(A_ps, q + 1)
                nc.scalar.activation(A[:, 4 * q:4 * q + 4, :, :].rearrange("p a c n -> p (a c) n"), p_A[:, q % 2, :, :],
                                     ACT.Copy).then_inc(A_sb, 1)
            act.wait_ge(R_ps, 1)
            nc.scalar.activation(RT[:], p_c[:, 0:NB].rearrange("p (t n) -> p t n", n=128), ACT.Copy).then_inc(RT_ok, 1)

        @block.vector
        def _(dve):
            dve.wait_ge(pos_in, 16)
            dve.wait_ge(raw_ok, 1)
            for t in range(T + 1):
                nc.vector.bn_stats(bst[:, t, :], raw[:, t, :]).then_inc(st, 1)
            dve.wait_ge(st, T + 1)
            for t in range(T + 1):
                nc.vector.bn_aggr(bmv[:, t, :], bst[:, t, :]).then_inc(mv, 1)
            dve.wait_ge(mv, T + 1)
            for t in range(T + 1):
                nc.vector.tensor_scalar(cen[:, t, :], raw[:, t, :], bmv[:, t, 0:1], None, ALU.subtract).then_inc(cen_ok, 1)
            dve.wait_ge(c_sb, 1)
            nc.vector.tensor_scalar(twice[:], cT[:, T, :], 2.0, None, ALU.mult).then_inc(tw, 1)
            pT = cT[:, 0:T, :].rearrange("p t n -> p (t n)")
            nc.vector.tensor_tensor(sq[:], pT, pT, ALU.mult).then_inc(sq_ok, 1)
            dve.wait_ge(v_ps, 1)
            nc.vector.tensor_scalar(var[:, 0, :], p_v[:, 0:NB], 1.0 / D, bmv[:, T, 1:2], ALU.mult, ALU.add).then_inc(var_1, 1)
            dve.wait_ge(var_1, 1)
            nc.vector.tensor_scalar(var[:, 1, :], var[:, 0, :], 0.0, EPS, ALU.max, ALU.add).then_inc(var_2, 1)
            dve.wait_ge(root_ok, 1)
            nc.vector.reciprocal(newton[:, 0, :], root[:]).then_inc(nw, 1)
            dve.wait_ge(nw, 1)
            nc.vector.tensor_tensor(newton[:, 1, :], newton[:, 0, :], newton[:, 0, :], ALU.mult).then_inc(nw, 1)
            dve.wait_ge(nw, 2)
            nc.vector.tensor_tensor(newton[:, 2, :], newton[:, 1, :], var[:, 1, :], ALU.mult).then_inc(nw, 1)
            dve.wait_ge(nw, 3)
            nc.vector.tensor_scalar(newton[:, 3, :], newton[:, 2, :], -0.5, 1.5, ALU.mult, ALU.add).then_inc(nw, 1)
            dve.wait_ge(nw, 4)
            nc.vector.tensor_tensor(R[:].rearrange("p t n -> p (t n)"), newton[:, 0, :], newton[:, 3, :], ALU.mult).then_inc(R_ok, 1)
            dve.wait_ge(P_ps, 1)
            view = P[:].rearrange("p (k j) c -> p j c k", j=CH)
            for h in range(2):
                nc.vector.tensor_copy(view[:, 8 * h:8 * h + 8, :, :],
                                      p_P[:, h, 0:8 * 2 * (NB // CH)].rearrange("p (j c k) -> p j c k", j=8, c=2)).then_inc(P_sb, 1)

        @block.tensor
        def _(pe):
            pe.wait_ge(cen_ok, T + 1)
            for t in range(T + 1):
                ins = nc.tensor.transpose(p_c[:, t * 128:(t + 1) * 128], cen[:, t, :], ident[:])
            ins.then_inc(c_ps, 1)
            pe.wait_ge(c_sb, 1)
            pe.wait_ge(tw, 1)
            pT = cT[:, 0:T, :].rearrange("p t n -> p (t n)")
            nc.tensor.matmul(p_v[:, 0:NB], twice[:], pT, start=True, stop=False)
            pe.wait_ge(sq_ok, 1)
            nc.tensor.matmul(p_v[:, 0:NB], ones[:], sq[:], start=False, stop=True).then_inc(v_ps, 1)
            for q in range(4):
                wait(pe, A_sb, q - 1)
                for i in range(4):
                    for c in range(2):
                        ins = nc.tensor.matmul(p_A[:, q % 2, 2 * i + c, :], Bj[:, 4 * q + i, c, :], cT[:, T, :],
                                               start=True, stop=True)
                ins.then_inc(A_ps, 1)
            pe.wait_ge(R_ok, 1)
            for t in range(T):
                ins = nc.tensor.transpose(p_c[:, t * 128:(t + 1) * 128], R[:, t, :], ident[:])
            ins.then_inc(R_ps, 1)
            K = NB // CH
            for j in range(CH):
                for c in range(2):
                    o = ((j % 8) * 2 + c) * K
                    ins = nc.tensor.matmul(p_P[:, j // 8, o:o + K], Bj[:, j, c, :],
                                           pT.rearrange("p (k j) -> p j k", j=CH)[:, j, :], start=True, stop=True)
            ins.then_inc(P_ps, 1)


def scan(nc, keep, scan_sems, scratch, pos, out):
    ident, turn, decay, base, carry, g2, top, halfneg, A, P, colC, colS = (keep[k] for k in (
        "ident", "turn", "decay", "base", "carry", "g2", "top", "halfneg", "A", "P", "colC", "colS"))
    L_Y, L_H2, L_X3, L_FF, L_HS, L_OUT, L_ST = 1, 2, 3, 4, 5, 6, 8
    with ExitStack() as ctx:
        def sb(name, shape, dt=F32):
            return ctx.enter_context(nc.sbuf_tensor(name, shape, dt))

        def ps(name, shape):
            return ctx.enter_context(nc.psum_tensor(name, shape, F32))

        def sem(name):
            return keep["sems"].enter_context(nc.semaphore("m_" + name))

        gT = sb("gT", [128, E])
        w13, w2s, gnat, ub, h1 = (keep[k] for k in ("sw13", "sw2", "gnat", "ub", "h1"))
        posb = sb("posb", [128, 4, GR, 128])
        Rb = sb("Rb", [128, 4, GR, 128])
        ap_ = sb("ap_", [128, 2, GR * 2, 128])
        tre = sb("tre", [128, 2, 128])
        h2 = sb("h2", [128, 4, GR, 128])
        st3 = sb("st3", [128, GR, 6])
        mv3 = sb("mv3", [128, 2, GR, 2])
        t3 = sb("t3", [128, 2, 2, GR])
        r3 = sb("r3", [128, 2, 2, GR])
        x3 = sb("x3", [128, 4, GR, ROW])
        xTs = sb("xTs", [128, 2, GR * 128])
        sa = sb("sa", [128, 2, GR * 128])
        hs = sb("hs", [128, 2, GR * 128])
        mx = sb("mx", [128, 4, GR, 8])
        ix = sb("ix", [128, 4, GR, 8], U32)
        ob = sb("ob", [128, 2, GR * 128])
        zr = sb("zr", [128, 2 * ROW])
        none = sb("none", [128, 2, NP - STEPS])
        p_y = ps("p_y", [128, 2, 512])
        p_xT, p_a, p_z, p_s = (ps(n, [128, 512]) for n in ("p_xT3", "p_a", "p_z", "p_s"))
        p_l = ps("p_l", [128, 2, 512])

        consts = scan_sems["consts"]
        u_in, h1_in = ([scan_sems[f"{n}{i}"] for i in range(4)] for n in ("u_in", "h1_in"))
        prep, iotas, gt_ps, gt_sb, zeros_out = (sem(n) for n in ("prep", "iotas", "gt_ps", "gt_sb", "zeros_out"))
        pos_in, R_in, x3_out = ([sem(f"{n}{i}") for i in range(4)] for n in ("pos_in", "R_in", "x3_out"))
        o_out = [sem(f"o_out{i}") for i in range(2)]
        names = ("ap_ok ap_act u_pool h1_pool rec turned y_ps h2_ok bn ag r3a r3b r3c r3d x3_ok xT_ps xT_sb lg_ps a_ps z_ps "
                 "silu_ok hs_ok sh_ps out_ok mx_ok ix_ok aug").split()
        (ap_ok, ap_act, u_pool, h1_pool, rec, turned, y_ps, h2_ok, bn, ag, r3a, r3b, r3c, r3d, x3_ok, xT_ps, xT_sb, lg_ps, a_ps,
         z_ps, silu_ok, hs_ok, sh_ps, out_ok, mx_ok, ix_ok, aug) = (sem(n) for n in names)
        ecol, necol, slot_row, slot_col, slot_half, empty_row, before, upto, one_on, one_b, rowp1 = (keep[k] for k in
            ("ecol necol slot_row slot_col slot_half empty_row before upto one_on one_b rowp1").split())
        block = ctx.enter_context(nc.Block())
        GA = FIRST // GR
        ACT_STEPS = 3

        def slots(eng, slot, lag):
            for s in range(12):
                slot(s, s % 4, 0)
            with eng.Fori(3, NC_A) as c:
                for q in range(4):
                    slot(4 * c + q, q, 0)
            for s in range(GA, GA + 4):
                slot(s, s % 4, 1)
            with eng.Fori(0, (NC - NC_A - 2) // 2) as c:
                for q in range(8):
                    slot(8 * c + (GA + 4 + q), q % 4, 1)
            for s in range(NG - 4, NG + lag):
                slot(s, s % 4, 1)

        def live(s, lag):
            return not isinstance(s, int) or 0 <= s - lag < NG

        @block.sync
        def _(sp):
            sp.wait_ge(prep, 2)
            sp.dma_start(scratch["x3"][B * NP:ROWS, :].rearrange("(p a) n -> p (a n)", p=128), zr[:]).then_inc(zeros_out, 16)
            sp.dma_start(out[B * NP:ROWS, :].rearrange("(p a) n -> p (a n)", p=128), zr[:, 0:2 * D]).then_inc(zeros_out, 16)

            def slot(s, q, region):
                if isinstance(s, int) and s < 4:
                    pass
                elif region == 0 and live(s, 0):
                    wait(sp, rec, 4 * (s - 3))
                    sp.dma_start(ub[:, q, :, :, :].rearrange("p a c n -> p (a c n)"),
                                 scratch["u"][:, bass.ds(s, 1), :].rearrange("p a n -> p (a n)")).then_inc(u_in[q], 16)
                    wait(sp, h2_ok, s - 3)
                    sp.dma_start(h1[:, q, :, :].rearrange("p a n -> p (a n)"),
                                 scratch["h1"][:, bass.ds(s, 1), :].rearrange("p a n -> p (a n)")).then_inc(h1_in[q], 16)
                elif live(s, 0):
                    wait(sp, rec, 4 * (s - 3))
                    sp.dma_start(Rb[:, q, :, :].rearrange("p a n -> p (a n)"),
                                 scratch["rT"].rearrange("n b -> (n b)")[bass.ds((s - GA) * (GR * 128), GR * 128)]
                                 .partition_broadcast(128)).then_inc(R_in[q], 16)
                    wait(sp, h2_ok, s - 3)
                    sp.dma_start(posb[:, q, :, :].rearrange("p a n -> p (a n)"),
                                 pos.rearrange("n d -> (n d)")[bass.ds(s * (GR * 128), GR * 128)]
                                 .partition_broadcast(128)).then_inc(pos_in[q], 16)
                if live(s, L_ST):
                    g = s - L_ST
                    sp.wait_ge(aug, 3 * (g + 1))
                    sp.dma_start(scratch["x3"][0:B * NP, :].rearrange("(b n) r -> b (n r)", b=128)[:, bass.ds(g * (GR * ROW), GR * ROW)],
                                 x3[:, (q - L_ST) % 4, :, :].rearrange("p a n -> p (a n)")).then_inc(x3_out[(q - L_ST) % 4], 16)
                    sp.wait_ge(out_ok, g + 1)
                    sp.dma_start(out[0:B * NP, :].rearrange("(b n) r -> b (n r)", b=128)[:, bass.ds(g * (GR * D), GR * D)],
                                 ob[:, (q - L_ST) % 2, :]).then_inc(o_out[(q - L_ST) % 2], 16)
            slots(sp, slot, L_ST)
            sp.wait_ge(zeros_out, 32)
            for r in range(4):
                sp.wait_ge(x3_out[r], 4 * NG)
            for r in range(2):
                sp.wait_ge(o_out[r], 8 * NG)

        @block.gpsimd
        def _(pool):
            nc.gpsimd.memset(x3[:], 0.0).then_inc(prep, 1)
            nc.gpsimd.memset(zr[:], 0.0).then_inc(prep, 1)
            nc.gpsimd.memset(none[:], 99.0).then_inc(prep, 1)
            pool.wait_ge(prep, 3)
            T = CAP // 128
            nc.gpsimd.iota(ecol[:], [[1, E]], base=0, channel_multiplier=0, allow_small_or_imprecise_dtypes=True).then_inc(iotas, 1)
            nc.gpsimd.iota(slot_row[:], [[1, CAP]], base=0, channel_multiplier=0, allow_small_or_imprecise_dtypes=True).then_inc(iotas, 1)
            nc.gpsimd.iota(slot_col[:], [[128, T]], base=0, channel_multiplier=1, allow_small_or_imprecise_dtypes=True).then_inc(iotas, 1)
            nc.gpsimd.iota(empty_row[:], [[128, T]], base=B * NP, channel_multiplier=1, allow_small_or_imprecise_dtypes=True).then_inc(iotas, 1)
            nc.gpsimd.iota(one_on[:], [[0, 1]], base=1, channel_multiplier=1, allow_small_or_imprecise_dtypes=True).then_inc(iotas, 1)
            nc.gpsimd.iota(necol[:], [[-1, E]], base=0, channel_multiplier=0, allow_small_or_imprecise_dtypes=True).then_inc(iotas, 1)
            nc.gpsimd.memset(before[:], 1.0).then_inc(iotas, 1)
            nc.gpsimd.memset(upto[:], 1.0).then_inc(iotas, 1)
            nc.gpsimd.memset(one_b[:], 1.0).then_inc(iotas, 1)
            pool.wait_ge(iotas, 9)
            nc.gpsimd.tensor_copy(rowp1[:], one_on[:]).then_inc(iotas, 1)
            nc.gpsimd.tensor_scalar(slot_half[:], slot_col[:], 0.5, None, ALU.add).then_inc(iotas, 1)
            nc.gpsimd.affine_select(out=before[:], in_=before[:], compare_op=ALU.is_gt, fill=0.0, base=0,
                                    pattern=[[1, 128]], channel_multiplier=-1).then_inc(iotas, 1)
            nc.gpsimd.affine_select(out=upto[:], in_=upto[:], compare_op=ALU.is_ge, fill=0.0, base=0,
                                    pattern=[[1, 128]], channel_multiplier=-1).then_inc(iotas, 1)

            def scan_input(s, q):
                n = s - GA
                wait(pool, u_pool, n - 1)
                k = GR - ACT_STEPS
                cols = P[:, bass.ds(n * GR + ACT_STEPS, k), :].rearrange("p a c -> p (a c)").unsqueeze(2).to_broadcast([128, 2 * k, 128])
                nc.gpsimd.tensor_tensor(ap_[:, q % 2, 2 * ACT_STEPS:, :], A[:, GR * q + ACT_STEPS:GR * (q + 1), :, :]
                                        .rearrange("p a c n -> p (a c) n"), cols, ALU.add).then_inc(ap_ok, 1)
                pool.wait_ge(R_in[q], 4 * (n - q) + 16)
                wait(pool, rec, 4 * (s - 3))
                wait(pool, ap_ok, n + 1)
                wait(pool, ap_act, 2 * ACT_STEPS * (n + 1))
                nc.gpsimd.tensor_tensor(ub[:, q, :, :, :], ap_[:, q % 2, :, :].rearrange("p (a c) n -> p a c n", c=2),
                                        Rb[:, q, :, :].unsqueeze(2).to_broadcast([128, GR, 2, 128]),
                                        ALU.mult).then_inc(u_pool, 1)
                pool.wait_ge(pos_in[q], 4 * (n - q) + 16)
                wait(pool, h2_ok, s - 3)
                nc.gpsimd.tensor_tensor(h1[:, q, :, :], posb[:, q, :, :],
                                        base[:].unsqueeze(1).to_broadcast([128, GR, 128]), ALU.add).then_inc(h1_pool, 1)

            def slot(s, q, region):
                if isinstance(s, int) and s == GA:
                    scan_input(s, q)
                if live(s, L_X3):
                    g, q2 = s - L_X3, (q - L_X3) % 2
                    pool.wait_ge(ag, 4 * (g + 1))
                    nc.gpsimd.tensor_tensor(t3[:, q2, 0, :], mv3[:, q2, :, 1], keep["eps"][:], ALU.add).then_inc(r3a, 1)
                    nc.gpsimd.tensor_tensor(t3[:, q2, 1, :], mv3[:, q2, :, 0], keep["minus"][:], ALU.mult).then_inc(r3b, 1)
                    pool.wait_ge(r3a, g + 1)
                    wait(pool, x3_ok, 4 * (g - 1))
                    nc.gpsimd.tensor_tensor(r3[:, q2, 0, :], t3[:, q2, 0, :], halfneg[:], ALU.pow).then_inc(r3c, 1)
                    pool.wait_ge(r3b, g + 1)
                    pool.wait_ge(r3c, g + 1)
                    nc.gpsimd.tensor_tensor(r3[:, q2, 1, :], t3[:, q2, 1, :], r3[:, q2, 0, :], ALU.mult).then_inc(r3d, 1)
                if region == 1 and live(s + 1, 0):
                    scan_input(s + 1, (q + 1) % 4)
            slots(pool, slot, L_X3)

        @block.scalar
        def _(act):
            act.wait_ge(gt_ps, 1)
            nc.scalar.activation(gT[:], p_l[:, 0, 0:E], ACT.Copy).then_inc(gt_sb, 1)
            act.wait_ge(prep, 1)

            def add_positions(s, q):
                n = s - GA
                wait(act, u_pool, n - 1)
                for i in range(ACT_STEPS):
                    for c in range(2):
                        nc.scalar.activation(ap_[:, q % 2, 2 * i + c, :], A[:, GR * q + i, c, :], ACT.Identity,
                                             bias=P[:, bass.ds(n * GR + i, 1), c]).then_inc(ap_act, 1)

            def slot(s, q, region):
                if isinstance(s, int) and s == GA:
                    add_positions(s, q)
                    add_positions(s + 1, q + 1)
                if live(s, L_OUT):
                    g, r = s - L_OUT, (q - L_OUT) % 4
                    act.wait_ge(ix_ok, 4 * (g + 1))
                    nc.scalar.activation(x3[:, r, :, D:D + 2], mx[:, r, :, 0:2], ACT.Copy).then_inc(aug, 1)
                    nc.scalar.activation(x3[:, r, :, D + 2:D + 3], ix[:, r, :, 0:1], ACT.Copy).then_inc(aug, 1)
                    nc.scalar.activation(top[:, :, bass.ds(g * GR, GR)], ix[:, r, :, 0:2].rearrange("p a k -> p k a"),
                                         ACT.Copy).then_inc(aug, 1)
                if live(s, L_X3):
                    g, q2, r = s - L_X3, (q - L_X3) % 2, (q - L_X3) % 4
                    act.wait_ge(r3d, g + 1)
                    if not isinstance(s, int) or g >= 4:
                        act.wait_ge(x3_out[r], 4 * (g - r))
                    for i in range(GR):
                        nc.scalar.activation(x3[:, r, i, 0:D], h2[:, r, i, :], ACT.Identity,
                                             bias=r3[:, q2, 1, i:i + 1], scale=r3[:, q2, 0, i:i + 1]).then_inc(x3_ok, 1)
                if region == 1 and live(s + 2, 0):
                    add_positions(s + 2, (q + 2) % 4)
                if live(s, L_FF):
                    g, q2 = s - L_FF, (q - L_FF) % 2
                    act.wait_ge(a_ps, g + 1)
                    wait(act, hs_ok, g - 1)
                    nc.scalar.activation(sa[:, q2, :], p_a[:], ACT.Silu).then_inc(silu_ok, 1)
                if live(s, L_X3):
                    g, q2 = s - L_X3, (q - L_X3) % 2
                    act.wait_ge(xT_ps, g + 1)
                    wait(act, z_ps, g - 1)
                    nc.scalar.activation(xTs[:, q2, :], p_xT[:], ACT.Copy).then_inc(xT_sb, 1)
            slots(act, slot, L_OUT)
            act.wait_ge(aug, 3 * NG)
            nc.scalar.activation(top[:, :, STEPS:NP], none[:], ACT.Copy)

        @block.vector
        def _(dve):

            def slot(s, q, region):
                if live(s, L_OUT):
                    g, r, o = s - L_OUT, (q - L_OUT) % 4, (q - L_OUT) % 2
                    dve.wait_ge(sh_ps, g + 1)
                    if not isinstance(s, int) or g >= 2:
                        dve.wait_ge(o_out[o], 8 * (g - o))
                    nc.vector.tensor_tensor(ob[:, o, :], h2[:, r, :, :].rearrange("p a n -> p (a n)"), p_s[:], ALU.add).then_inc(out_ok, 1)
                if live(s, L_HS):
                    g, q2 = s - L_HS, (q - L_HS) % 2
                    dve.wait_ge(silu_ok, g + 1)
                    dve.wait_ge(z_ps, g + 1)
                    dve.wait_ge(lg_ps, g + 1)
                    wait(dve, aug, 3 * (g - 3))
                    wait(dve, sh_ps, g - 1)
                    nc.vector.tensor_tensor(hs[:, q2, :], sa[:, q2, :], p_z[:], ALU.mult).then_inc(hs_ok, 1)
                if live(s, L_H2):
                    g, q2, r = s - L_H2, (q - L_H2) % 2, (q - L_H2) % 4
                    dve.wait_ge(y_ps, g + 1)
                    wait(dve, out_ok, g - 3)
                    if region == 0 or isinstance(s, int) and g < GA:
                        dve.wait_ge(h1_in[r], 4 * (g - r) + 16)
                    else:
                        dve.wait_ge(h1_pool, g + 1 - GA)
                    nc.vector.tensor_tensor(h2[:, r, :, :], p_y[:, q2, :].rearrange("p (a n) -> p a n", a=GR),
                                            h1[:, r, :, :], ALU.add).then_inc(h2_ok, 1)
                if live(s, 0) and q == 0 and not (isinstance(s, int) and s == 0):
                    dve.wait_ge(rec, 4 * s)
                    k = s - 4
                    last = g2[:, 2 * GR - 1, :, :]
                    nc.vector.tensor_scalar(tre[:, 0, :], last[:, 1, :], colS[:, CH:CH + 1], None, ALU.mult).then_inc(turned, 1)
                    nc.vector.tensor_scalar(tre[:, 1, :], last[:, 0, :], colS[:, CH:CH + 1], None, ALU.mult).then_inc(turned, 1)
                    dve.wait_ge(turned, k + 1)
                    nc.vector.scalar_tensor_tensor(out=carry[:, 0, :], in0=last[:, 0, :], scalar=colC[:, CH:CH + 1],
                                                   in1=tre[:, 0, :], op0=ALU.mult, op1=ALU.subtract).then_inc(turned, 1)
                    dve.wait_ge(turned, k + 2)
                    nc.vector.scalar_tensor_tensor(out=carry[:, 1, :], in0=last[:, 1, :], scalar=colC[:, CH:CH + 1],
                                                   in1=tre[:, 1, :], op0=ALU.mult, op1=ALU.add).then_inc(turned, 1)
                g5, half, r5 = s - L_HS, (q - L_HS) % 2, (q - L_HS) % 4
                g2_, q2, r2 = s - L_H2, (q - L_H2) % 2, (q - L_H2) % 4
                if live(s, L_HS):
                    nc.vector.max(mx[:, r5, 0, :], p_l[:, half, 0:E]).then_inc(mx_ok, 1)
                for i in range(GR):
                    lg = p_l[:, half, i * E:(i + 1) * E]
                    if live(s, L_HS) and i + 1 < GR:
                        nc.vector.max(mx[:, r5, i + 1, :], p_l[:, half, (i + 1) * E:(i + 2) * E]).then_inc(mx_ok, 1)
                    if live(s, L_H2):
                        if i == 0:
                            dve.wait_ge(h2_ok, g2_ + 1)
                            wait(dve, r3d, g2_ - 1)
                        else:
                            wait(dve, bn, 4 * g2_ + i)
                    if live(s, L_HS):
                        dve.wait_ge(mx_ok, 4 * g5 + i + 1)
                    if live(s, L_H2):
                        nc.vector.bn_stats(st3[:, i, :], h2[:, r2, i, :]).then_inc(bn, 1)
                        if i:
                            nc.vector.bn_aggr(mv3[:, q2, i - 1, :], st3[:, i - 1, :]).then_inc(ag, 1)
                    if live(s, L_HS):
                        nc.vector.max_index(ix[:, r5, i, :], mx[:, r5, i, :], lg).then_inc(ix_ok, 1)
                    if i == GR - 1 and live(s, L_H2):
                        dve.wait_ge(bn, 4 * g2_ + GR)
                    if live(s, 0):
                        if i == 0:
                            if region == 0:
                                dve.wait_ge(u_in[q], 4 * (s - q) + 16)
                            else:
                                dve.wait_ge(u_pool, s + 1 - GA)
                            wait(dve, y_ps, s - 1)
                        wait(dve, rec, 4 * s + i)
                        if q == 0 and i == 0 and not (isinstance(s, int) and s == 0):
                            dve.wait_ge(turned, s)
                        k = (q % 2) * GR + i
                        prev = carry[:] if q == 0 and i == 0 else g2[:, (k - 1) % (2 * GR), :, :]
                        nc.vector.scalar_tensor_tensor(out=g2[:, k, :, :], in0=prev, scalar=decay[:, 0:1],
                                                       in1=ub[:, q, i, :, :], op0=ALU.mult, op1=ALU.add).then_inc(rec, 1)
                if live(s, L_H2):
                    nc.vector.bn_aggr(mv3[:, q2, GR - 1, :], st3[:, GR - 1, :]).then_inc(ag, 1)
            slots(dve, slot, L_OUT)

        @block.tensor
        def _(pe):
            pe.wait_ge(consts, 64)
            nc.tensor.transpose(p_l[:, 0, 0:E], gnat[:], ident[0:E, 0:E]).then_inc(gt_ps, 1)
            pe.wait_ge(gt_sb, 1)

            def slot(s, q, region):
                if live(s, L_Y):
                    g, q2 = s - L_Y, (q - L_Y) % 2
                    pe.wait_ge(rec, 4 * (g + 1))
                    wait(pe, h2_ok, g - 1)
                    for i in range(GR):
                        j, o = GR * ((q - L_Y) % 4) + i, p_y[:, q2, i * 128:(i + 1) * 128]
                        nc.tensor.matmul(o, g2[:, q2 * GR + i, 0, :], turn[:, j, 0, :], start=True, stop=False)
                        ins = nc.tensor.matmul(o, g2[:, q2 * GR + i, 1, :], turn[:, j, 1, :], start=False, stop=True)
                    ins.then_inc(y_ps, 1)
                if live(s, L_FF):
                    g, q2 = s - L_FF, (q - L_FF) % 2
                    pe.wait_ge(xT_sb, g + 1)
                    wait(pe, silu_ok, g)
                    nc.tensor.matmul(p_a[:], w13[:, 0, :], xTs[:, q2, :], start=True, stop=True).then_inc(a_ps, 1)
                    wait(pe, ix_ok, 4 * (g - 1))
                    for i in range(GR):
                        ins = nc.tensor.matmul(p_l[:, q2, i * E:(i + 1) * E], xTs[:, q2, i * 128:(i + 1) * 128],
                                               gT[:], start=True, stop=True)
                    ins.then_inc(lg_ps, 1)
                    wait(pe, hs_ok, g)
                    nc.tensor.matmul(p_z[:], w13[:, 1, :], xTs[:, q2, :], start=True, stop=True).then_inc(z_ps, 1)
                if live(s, L_HS):
                    g, q2 = s - L_HS, (q - L_HS) % 2
                    pe.wait_ge(hs_ok, g + 1)
                    wait(pe, out_ok, g)
                    for i in range(GR):
                        ins = nc.tensor.matmul(p_s[:, i * 128:(i + 1) * 128], hs[:, q2, i * 128:(i + 1) * 128], w2s[:],
                                               start=True, stop=True)
                    ins.then_inc(sh_ps, 1)
                if live(s, L_X3):
                    g, r = s - L_X3, (q - L_X3) % 4
                    pe.wait_ge(x3_ok, 4 * (g + 1))
                    wait(pe, xT_sb, g)
                    for i in range(GR):
                        ins = nc.tensor.transpose(p_xT[:, i * 128:(i + 1) * 128], x3[:, r, i, 0:D], ident[:])
                    ins.then_inc(xT_ps, 1)
            slots(pe, slot, L_ST)


def routed(nc, keep, scratch, w13, w2, out):
    ident, top = keep["ident"], keep["top"]
    ecol, necol, slot_row, slot_col, slot_half, empty_row, before, upto, one_b, rowp1 = (keep[k] for k in
        ("ecol necol slot_row slot_col slot_half empty_row before upto one_b rowp1").split())
    T = CAP // 128
    L_CNT, L_EXC, L_SEL, L_IDX = 0, 1, 2, 3
    L_W, L_T, L_A, L_H, L_WT, L_Y, L_YS, L_SC = 3, 5, 5, 6, 6, 7, 7, 8
    U = 8
    with ExitStack() as ctx:
        def sb(name, shape, dt=F32):
            return ctx.enter_context(nc.sbuf_tensor("r_" + name, shape, dt))

        def ps(name, shape):
            return ctx.enter_context(nc.psum_tensor("r_" + name, shape, F32))

        def sem(name):
            return keep["sems"].enter_context(nc.semaphore("r_" + name))

        cnt = sb("cnt", [128, 4, NP], F16)
        is0 = sb("is0", [128, 2, NP], BF16)
        is1 = sb("is1", [128, 2, NP], BF16)
        off = sb("off", [128, NP])
        ei = sb("ei", [128, 4, 2])
        exc16 = sb("exc16", [128, 4], F16)
        past = sb("past", [128, CAP], F16)
        S = sb("S", [128, 2, CAP], F16)
        le = sb("le", [128, NP])
        sg_junk = sb("sg_junk", [128, NP])
        nstar = sb("nstar", [128, 2, T])
        signs = sb("signs", [128, 2])
        flat = sb("flat", [128, T])
        vac = sb("vac", [128, T])
        ridx = sb("ridx", [128, U, T], U32)
        xg = sb("xg", [128, U, T, ROW])
        sv = sb("sv", [128, 2, T, 2])
        wt = sb("wt", [128, 5, T])
        wgt = sb("wgt", [128, 4, T])
        xT = sb("xT", [128, 2, CAP])
        wr = sb("wr", [128, 4, 2 * HID])
        w2r = sb("w2r", [HID, 4, D])
        sg = sb("sg", [HID, 2, CAP])
        asg = sb("asg", [HID, CAP])
        hh = sb("hh", [HID, 2, CAP])
        ys = sb("ys", [128, 2, T, D])
        p_n = [ps(f"p_n{t}", [128, 512]) for t in range(T)]
        p_b, p_e, p_x, p_y = (ps(n, [128, 512]) for n in ("p_b", "p_e", "p_x", "p_y"))
        p_az = ps("p_az", [128, 2, 2, CAP])

        w_in = [sem(f"w_in{i}") for i in range(4)]
        gathered = [sem(f"gathered{i}") for i in range(U)]
        names = ("m0_ok off_ok m1_ok c_ok exc_ps exc_ok past_ok S_ok sel_ps cnt0 cnt1 n1 fl vc ridx_ok T_ps T_sb az_ps "
                 "sv_ok w_ok sg_ok asg_ok h_ok y_ps ys_ok added wk passed").split()
        (m0_ok, off_ok, m1_ok, c_ok, exc_ps, exc_ok, past_ok, S_ok, sel_ps, cnt0, cnt1, n1, fl, vc, ridx_ok, T_ps, T_sb,
         az_ps, sv_ok, w_ok, sg_ok, asg_ok, h_ok, y_ps, ys_ok, added, wk, passed) = (sem(n) for n in names)
        block = ctx.enter_context(nc.Block())

        def slots(eng, slot):
            for s in range(2 * U):
                slot(s, s % U)
            with eng.Fori(2, E // U) as c:
                for q in range(U):
                    slot(U * c + q, q)
            for s in range(E, E + L_SC):
                slot(s, s % U)

        def live(s, lag):
            return not isinstance(s, int) or 0 <= s - lag < E

        @block.sync
        def _(sp):
            def slot(s, q):
                if live(s, L_W):
                    g, r = s - L_W, (q - L_W) % 4
                    wait(sp, az_ps, g - 3)
                    sp.dma_start(wr[:, r, :], w13[bass.ds(g, 1), :, :].rearrange("a p n -> (a p) n")).then_inc(w_in[r], 16)
                    wait(sp, y_ps, g - 3)
                    sp.dma_start(w2r[:, r, :], w2[bass.ds(g, 1), :, :].rearrange("a p n -> (a p) n")).then_inc(w_in[r], 16)
            slots(sp, slot)

        @block.gpsimd
        def _(pool):
            last_row = pool.to_reg(ROWS - 1)

            def slot(s, q):
                if live(s, L_SC):
                    g, r = s - L_SC, (q - L_SC) % U
                    pool.wait_ge(ys_ok, T * (g + 1))
                    wait(pool, added, 16 * T * g)
                    pool.sem_inc(passed, 1)
                    for t in range(T):
                        nc.gpsimd.indirect_dma_start(out, bass.IndirectOffsetOnAxis(ap=ridx[:, r, t:t + 1], axis=0),
                                                     ys[:, r % 2, t, :], None, bounds_check=last_row, oob_is_err=True,
                                                     compute_op=ALU.add).then_inc(added, 16)
                if live(s, L_IDX):
                    g, r = s - L_IDX, (q - L_IDX) % U
                    wait(pool, w_ok, g - U + 1)
                    pool.wait_ge(ridx_ok, g + 1)
                    pool.sem_inc(passed, 1)
                    for t in range(T):
                        nc.gpsimd.indirect_dma_start(xg[:, r, t, :], None, scratch["x3"],
                                                     bass.IndirectOffsetOnAxis(ap=ridx[:, r, t:t + 1], axis=0),
                                                     bounds_check=last_row, oob_is_err=True).then_inc(gathered[r], 16)
            slots(pool, slot)
            pool.wait_ge(added, 16 * T * E)

        @block.scalar
        def _(act):

            def slot(s, q):
                if live(s, L_IDX):
                    g = s - L_IDX
                    act.wait_ge(sel_ps, g + 1)
                    wait(act, n1, g - 1)
                    nc.scalar.activation(sg_junk[:], p_n[1][:], ACT.Sign, bias=slot_half[:, 1:2], scale=-1.0,
                                         accum_out=signs[:, (q - L_IDX) % 2:(q - L_IDX) % 2 + 1]).then_inc(cnt1, 1)
                if live(s, L_H):
                    g, q2 = s - L_H, (q - L_H) % 2
                    act.wait_ge(az_ps, g + 1)
                    wait(act, asg_ok, g - 1)
                    nc.scalar.activation(sg[:, q2, :], p_az[0:HID, q2, 0, :], ACT.Sigmoid).then_inc(sg_ok, 1)
                if live(s, L_T):
                    g, q2, r = s - L_T, (q - L_T) % 2, (q - L_T) % U
                    act.wait_ge(T_ps, g + 1)
                    wait(act, az_ps, g - 1)
                    nc.scalar.activation(xT[:, q2, :], p_x[:, 0:CAP], ACT.Copy).then_inc(T_sb, 1)
                    act.wait_ge(gathered[r], 4 * (g - r) + 16 * T)
                    wait(act, w_ok, g - 1)
                    nc.scalar.activation(sv[:, q2, :, :], xg[:, r, :, D:D + 2], ACT.Sigmoid).then_inc(sv_ok, 1)
                if live(s, L_YS):
                    g, q2 = s - L_YS, (q - L_YS) % 2
                    act.wait_ge(y_ps, g + 1)
                    act.wait_ge(w_ok, g + 1)
                    wait(act, added, 16 * T * (g - 1))
                    for t in range(T):
                        nc.scalar.activation(ys[:, q2, t, :], p_y[:, t * D:(t + 1) * D], ACT.Identity,
                                             scale=wgt[:, (q - L_YS) % 4, t:t + 1]).then_inc(ys_ok, 1)
                if live(s, L_CNT):
                    wait(act, m1_ok, s)
                    nc.scalar.activation(off[:], top[:, 1, :], ACT.Square, bias=necol[:, bass.ds(s, 1)], scale=1.0).then_inc(off_ok, 1)
                    wait(act, off_ok, s + 1)
                    wait(act, c_ok, s - 1)
                    nc.scalar.activation(is1[:, q % 2, :], off[:], ACT.Relu, bias=one_b[:], scale=-1.0).then_inc(m1_ok, 1)
            slots(act, slot)

        @block.vector
        def _(dve):
            def slot(s, q):
                gi, i2, ir = s - L_IDX, (q - L_IDX) % 2, (q - L_IDX) % U
                gs, s2, sr = s - L_SEL, (q - L_SEL) % 2, (q - L_SEL) % 4
                gh, h2 = s - L_H, (q - L_H) % 2
                ga, a2, ar = s - L_WT, (q - L_WT) % 2, (q - L_WT) % U
                if live(s, L_IDX):
                    dve.wait_ge(sel_ps, gi + 1)
                    wait(dve, fl, gi - 1)
                    wait(dve, cnt0, gi)
                    nc.vector.tensor_scalar(le[:], p_n[0][:], slot_col[:, 0:1], 0.0, ALU.is_le, ALU.add,
                                            accum_out=nstar[:, i2, 0:1]).then_inc(cnt0, 1)
                    wait(dve, ridx_ok, gi)
                    nc.vector.scalar_tensor_tensor(out=vac[:], in0=p_b[:, 0:T], scalar=0.0, in1=empty_row[:],
                                                   op0=ALU.is_equal, op1=ALU.mult).then_inc(vc, 1)
                if live(s, L_CNT):
                    wait(dve, c_ok, s - 1)
                    nc.vector.tensor_scalar(is0[:, q % 2, :], top[:, 0, :], ecol[:, bass.ds(s, 1)], None, ALU.is_equal).then_inc(m0_ok, 1)
                if live(s, L_IDX):
                    dve.wait_ge(cnt1, gi + 1)
                    nc.vector.tensor_scalar(nstar[:, i2, 1:2], signs[:, i2:i2 + 1], 0.5, NP / 2, ALU.mult, ALU.add).then_inc(n1, 1)
                if live(s, L_H):
                    wait(dve, sg_ok, gh + 1)
                    wait(dve, h_ok, gh)
                    nc.vector.tensor_tensor(asg[:], sg[:, h2, :], p_az[0:HID, h2, 0, :], ALU.mult).then_inc(asg_ok, 1)
                if live(s, L_IDX):
                    dve.wait_ge(cnt0, gi + 1)
                    dve.wait_ge(n1, gi + 1)
                    nc.vector.scalar_tensor_tensor(out=flat[:], in0=p_b[:, 0:T], scalar=float(NP), in1=nstar[:, i2, :],
                                                   op0=ALU.mult, op1=ALU.add).then_inc(fl, 1)
                if live(s, L_SEL):
                    wait(dve, exc_ok, 2 * (gs + 1))
                    wait(dve, S_ok, gs)
                    nc.vector.tensor_scalar(past[:], slot_row[:], ei[:, sr, 1:2], None, ALU.is_ge).then_inc(past_ok, 1)
                if live(s, L_IDX):
                    dve.wait_ge(fl, gi + 1)
                    dve.wait_ge(vc, gi + 1)
                    wait(dve, added, 16 * T * (gi - U + 1))
                    nc.vector.scalar_tensor_tensor(out=ridx[:, ir, :], in0=flat[:], scalar=float(-NP), in1=vac[:],
                                                   op0=ALU.add, op1=ALU.add).then_inc(ridx_ok, 1)
                if live(s, L_H):
                    wait(dve, asg_ok, gh + 1)
                    wait(dve, y_ps, gh - 1)
                    nc.vector.tensor_tensor(hh[:, h2, :], asg[:], p_az[0:HID, h2, 1, :], ALU.mult).then_inc(h_ok, 1)
                if live(s, L_SEL):
                    wait(dve, sel_ps, gs - 1)
                    wait(dve, past_ok, gs + 1)
                    nc.vector.scalar_tensor_tensor(out=S[:, s2, :], in0=slot_row[:], scalar=ei[:, sr, 0:1],
                                                   in1=past[:], op0=ALU.is_ge, op1=ALU.subtract).then_inc(S_ok, 1)
                s1, s2_, e1 = sv[:, a2, :, 0], sv[:, a2, :, 1], xg[:, ar, :, D + 2]
                if live(s, L_WT):
                    me = ecol[:, bass.ds(ga, 1)]
                    dve.wait_ge(sv_ok, ga + 1)
                    wait(dve, w_ok, ga)
                    nc.vector.scalar_tensor_tensor(out=wt[:, 2, :], in0=s1, scalar=1e-20, in1=s2_, op0=ALU.add,
                                                   op1=ALU.add).then_inc(wk, 1)
                    nc.vector.scalar_tensor_tensor(out=wt[:, 0, :], in0=e1, scalar=me, in1=s1, op0=ALU.is_equal,
                                                   op1=ALU.mult).then_inc(wk, 1)
                    nc.vector.scalar_tensor_tensor(out=wt[:, 1, :], in0=e1, scalar=me, in1=s2_, op0=ALU.not_equal,
                                                   op1=ALU.mult).then_inc(wk, 1)
                    dve.wait_ge(wk, 5 * ga + 1)
                    nc.vector.reciprocal(wt[:, 4, :], wt[:, 2, :]).then_inc(wk, 1)
                if live(s, L_EXC):
                    g, r = s - L_EXC, (q - L_EXC) % 4
                    wait(dve, exc_ps, g + 1)
                    wait(dve, sel_ps, g - 3)
                    wait(dve, S_ok, g - 3)
                    nc.vector.tensor_copy(ei[:, r, :], p_e[:, 0:2]).then_inc(exc_ok, 1)
                    nc.vector.tensor_scalar(exc16[:, r:r + 1], p_e[:, 0:1], 4.0 * CAP, None, ALU.min).then_inc(exc_ok, 1)
                if live(s, L_WT):
                    dve.wait_ge(wk, 5 * ga + 4)
                    nc.vector.tensor_tensor(wt[:, 3, :], wt[:, 0, :], wt[:, 1, :], ALU.add).then_inc(wk, 1)
                if live(s, L_CNT):
                    wait(dve, m0_ok, s + 1)
                    wait(dve, m1_ok, s + 1)
                    wait(dve, sel_ps, s - 3)
                    nc.vector.tensor_tensor_scan(cnt[:, q % 4, :], is0[:, q % 2, :], is1[:, q % 2, :],
                                                 0.0, ALU.add, ALU.add).then_inc(c_ok, 1)
                if live(s, L_WT):
                    dve.wait_ge(wk, 5 * ga + 5)
                    wait(dve, ys_ok, T * (ga - 3))
                    nc.vector.scalar_tensor_tensor(out=wgt[:, (q - L_WT) % 4, :], in0=wt[:, 3, :], scalar=ROUTE_SCALE, in1=wt[:, 4, :],
                                                   op0=ALU.mult, op1=ALU.mult).then_inc(w_ok, 1)
            slots(dve, slot)

        @block.tensor
        def _(pe):

            def slot(s, q):
                if live(s, L_EXC):
                    g, r = s - L_EXC, (q - L_EXC) % 4
                    wait(pe, c_ok, g + 1)
                    wait(pe, exc_ok, 2 * g)
                    nc.tensor.matmul(p_e[:, 0:1], before[:], cnt[:, r, NP - 1:NP], start=True, stop=True)
                    nc.tensor.matmul(p_e[:, 1:2], upto[:], cnt[:, r, NP - 1:NP], start=True, stop=True).then_inc(exc_ps, 1)
                if live(s, L_T):
                    g, q2, r = s - L_T, (q - L_T) % 2, (q - L_T) % U
                    pe.wait_ge(gathered[r], 4 * (g - r) + 16 * T)
                    wait(pe, T_sb, g)
                    for t in range(T):
                        ins = nc.tensor.transpose(p_x[:, t * 128:(t + 1) * 128], xg[:, r, t, 0:D], ident[:])
                    ins.then_inc(T_ps, 1)
                if live(s, L_Y):
                    g, q2 = s - L_Y, (q - L_Y) % 2
                    pe.wait_ge(h_ok, g + 1)
                    wait(pe, ys_ok, T * g)
                    for t in range(T):
                        ins = nc.tensor.matmul(p_y[:, t * D:(t + 1) * D], hh[:, q2, t * 128:(t + 1) * 128], w2r[:, (q - L_Y) % 4, :],
                                               start=True, stop=True)
                    ins.then_inc(y_ps, 1)
                if live(s, L_A):
                    g, q2, r = s - L_A, (q - L_A) % 2, (q - L_A) % 4
                    pe.wait_ge(T_sb, g + 1)
                    pe.wait_ge(w_in[r], 8 * (g - r) + 32)
                    wait(pe, h_ok, g - 1)
                    nc.tensor.matmul(p_az[0:HID, q2, 0, :], wr[:, r, 0:HID], xT[:, q2, :], start=True, stop=True)
                    nc.tensor.matmul(p_az[0:HID, q2, 1, :], wr[:, r, HID:2 * HID], xT[:, q2, :], start=True, stop=True).then_inc(az_ps, 1)
                if live(s, L_SEL):
                    g, q2, r = s - L_SEL, (q - L_SEL) % 2, (q - L_SEL) % 4
                    pe.wait_ge(S_ok, g + 1)
                    wait(pe, cnt0, g)
                    wait(pe, cnt1, g)
                    wait(pe, fl, g)
                    for t in range(T):
                        St = S[:, q2, t * 128:(t + 1) * 128]
                        nc.tensor.matmul(p_n[t][:], St, cnt[:, r, :], start=True, stop=False)
                        nc.tensor.matmul(p_n[t][:], St, exc16[:, r:r + 1].to_broadcast([128, NP]), start=False, stop=True)
                        ins = nc.tensor.matmul(p_b[:, t:t + 1], St, rowp1[:], start=True, stop=True)
                    ins.then_inc(sel_ps, 1)
            slots(pe, slot)


def kernel(**inputs):
    import numpy as np
    import concourse.bacc as bacc
    from concourse.bass_utils import run_bass_kernel_spmd

    a = {k.replace("L0_", "").replace("tok_", "").replace("attn_", "").replace("ffn_", ""): np.asarray(v)
         for k, v in inputs.items()}
    x = a["x"]
    steps = (FG * GR + 1) * STRIDE
    arrays = {
        "x": np.pad(x, ((0, 0), (0, steps - x.shape[1]), (0, 0)), mode="edge").reshape(B, steps * C),
        "W": a["W"].reshape(C, PATCH, D).transpose(1, 0, 2).reshape(C * PATCH, D),
        "b": a["b"], "ln_g": a["ln_g"], "ln_b": a["ln_b"],
        "posA": np.pad(a["pos_emb"][0, :FIRST], ((0, GR), (0, 0))).reshape(1, -1),
        "pos": np.pad(a["pos_emb"][0], ((0, NP - STEPS), (0, 0))),
        "type_emb": a["type_emb"], "Br": a["B_real"], "Bi": a["B_img"],
        "nu": a["nu"], "theta": a["theta"], "delta": a["delta"], "h0r": a["h0_real"], "h0i": a["h0_img"],
        "gate_w": a["gate_w"], "w13": np.concatenate([a["w1"], a["w3"]], axis=2), "w2": a["w2"],
        "sw1": a["sw1"], "sw3": a["sw3"], "sw2": a["sw2"],
    }
    nc = bacc.Bacc("TRN2", target_bir_lowering=False, num_devices=1)
    fed, args = {}, []
    for name, v in arrays.items():
        v = np.ascontiguousarray(v)
        fed[f"in_{name}"] = v
        args.append(nc.dram_tensor(f"in_{name}", v.shape, mybir.dt.from_np(v.dtype), kind="ExternalInput").ap())
    out = nc.dram_tensor("out_rows", (ROWS, D), F32, kind="ExternalOutput").ap()
    tower(nc, *args, out)
    r = run_bass_kernel_spmd(nc, [fed], core_ids=[0])
    return r.results[0]["out_rows"][:B * NP].reshape(B, NP, D)[:, :STEPS]
```
